# Optimizing a Trainium2 kernel written in Bass

```python
import numpy as np
import jax
import jax.numpy as jnp

def _softmax(x, axis=-1):
    return jax.nn.softmax(x, axis=axis)

def _gelu(x):
    return jax.nn.gelu(x, approximate=True)

def _silu(x):
    return jax.nn.silu(x)

def _sigmoid(x):
    return jax.nn.sigmoid(x)

def _layernorm(x, axis=-1, eps=1e-05):
    m = jnp.mean(x, axis=axis, keepdims=True)
    v = jnp.var(x, axis=axis, keepdims=True)
    return (x - m) / jnp.sqrt(v + eps)

def _scatter_add(tgt, idx, src, axis=0):
    return tgt.at[idx].add(src)

def _segment_sum(src, seg, n):
    return jax.ops.segment_sum(src, seg, n)
kernel_name = 'mk_early_fusion_d1_tok_img256_r4_17954a'

def setup_inputs(seed: int=0):
    np.random.seed(seed)
    _w = jnp.asarray

    def _rec_inputs():
        import jax
        import jax.numpy as jnp
        _rk = jax.random.key(seed)
        x = -0.00016672 + 0.999947 * jax.random.normal(jax.random.fold_in(_rk, 1), (16, 3, 224, 224), jnp.float32)
        txt = 0.000202745 + 0.998873 * jax.random.normal(jax.random.fold_in(_rk, 2), (16, 512, 64), jnp.float32)
        return (x, txt)
    x, txt = _rec_inputs()

    def _L0_tok_setup():
        import jax, jax.numpy as jnp
        import numpy as np
        PATCH = 16
        key = jax.random.key(seed)
        k1, k2, k3 = jax.random.split(key, 3)
        B, C, H, Wd = (64, 3, 96, 96)
        E = 64
        pdim = PATCH * PATCH * C
        x = jax.random.normal(k1, (B, C, H, Wd), dtype=jnp.float32)
        W = jax.random.normal(k2, (E, pdim), dtype=jnp.float32) * pdim ** (-0.5)
        b = jax.random.normal(k3, (E,), dtype=jnp.float32) * 0.01
        return {'x': x, 'W': W, 'b': b}
    _L0_tok_all = _L0_tok_setup()
    _L0_tok_in = {k: v for k, v in _L0_tok_all.items() if k in ('W', 'b')}
    del _L0_tok_all

    def _L0_attn_setup():
        import math
        import jax, jax.numpy as jnp
        import numpy as np
        EPS_DIV = 1e-07
        EPS_NORM = 1e-12

        def _l2_normalize(x, axis):
            n = jnp.sqrt(jnp.sum(x * x, axis=axis, keepdims=True))
            return x / jnp.maximum(n, EPS_NORM)
        key = jax.random.key(seed)
        ks = jax.random.split(key, 5)
        b, N, C = (8, 1024, 64)
        x = jax.random.normal(ks[0], (b, N, C), dtype=jnp.float32)
        W_qkv = jax.random.normal(ks[1], (C, 3 * C), dtype=jnp.float32) * (1.0 / math.sqrt(C))
        b_qkv = jax.random.normal(ks[2], (3 * C,), dtype=jnp.float32) * 0.02
        W_out = jax.random.normal(ks[3], (C, C), dtype=jnp.float32) * (1.0 / math.sqrt(C))
        b_out = jax.random.normal(ks[4], (C,), dtype=jnp.float32) * 0.02
        return {'x': x, 'W_qkv': W_qkv, 'b_qkv': b_qkv, 'W_out': W_out, 'b_out': b_out}
    _L0_attn_all = _L0_attn_setup()
    _L0_attn_in = {k: v for k, v in _L0_attn_all.items() if k in ('W_qkv', 'b_qkv', 'W_out', 'b_out')}
    del _L0_attn_all

    def _L0_ffn_setup():
        import jax, jax.numpy as jnp
        import numpy as np
        B, S, H, NH, NE = (4, 256, 64, 4, 4)
        D = H // NH
        EPS = 1e-08

        def layernorm(x, g, b):
            m = jnp.mean(x, axis=-1, keepdims=True)
            v = jnp.mean((x - m) ** 2, axis=-1, keepdims=True)
            return (x - m) / jnp.sqrt(v + EPS) * g + b
        key = jax.random.key(seed)
        ks = jax.random.split(key, 18)
        sc = 0.05
        return {'x': jax.random.normal(ks[0], (B, S, H), jnp.float32), 'hl_w': jax.random.normal(ks[1], (NH, D, H), jnp.float32) * sc, 'hl_b': jax.random.normal(ks[2], (NH, D), jnp.float32) * sc, 'wq': jax.random.normal(ks[3], (NH, NE, D, D), jnp.float32) * sc, 'wk': jax.random.normal(ks[4], (NH, D, D), jnp.float32) * sc, 'wv': jax.random.normal(ks[5], (NH, D, D), jnp.float32) * sc, 'gate_w': jax.random.normal(ks[6], (NH, NE, NE * D), jnp.float32) * sc, 'gate_b': jax.random.normal(ks[7], (NH, NE), jnp.float32) * sc, 'ln_g': jnp.ones((D,), jnp.float32), 'ln_b': jnp.zeros((D,), jnp.float32), 'fc1_w': jax.random.normal(ks[8], (D, D), jnp.float32) * sc, 'fc1_b': jax.random.normal(ks[9], (D,), jnp.float32) * sc, 'fc2_w': jax.random.normal(ks[10], (D, D), jnp.float32) * sc, 'fc2_b': jax.random.normal(ks[11], (D,), jnp.float32) * sc, 'fnorm_g': jnp.ones((D,), jnp.float32), 'fnorm_b': jnp.zeros((D,), jnp.float32), 'fgate_w': jax.random.normal(ks[12], (NH, H), jnp.float32) * sc}
    _L0_ffn_all = _L0_ffn_setup()
    _L0_ffn_in = {k: v for k, v in _L0_ffn_all.items() if k in ('hl_w', 'hl_b', 'wq', 'wk', 'wv', 'gate_w', 'gate_b', 'ln_g', 'ln_b', 'fc1_w', 'fc1_b', 'fc2_w', 'fc2_b', 'fnorm_g', 'fnorm_b', 'fgate_w')}
    del _L0_ffn_all
    return {'x': x, 'txt': txt, 'L0_tok_W': _L0_tok_in['W'], 'L0_tok_b': _L0_tok_in['b'], 'L0_attn_W_qkv': _L0_attn_in['W_qkv'], 'L0_attn_b_qkv': _L0_attn_in['b_qkv'], 'L0_attn_W_out': _L0_attn_in['W_out'], 'L0_attn_b_out': _L0_attn_in['b_out'], 'L0_ffn_hl_w': _L0_ffn_in['hl_w'], 'L0_ffn_hl_b': _L0_ffn_in['hl_b'], 'L0_ffn_wq': _L0_ffn_in['wq'], 'L0_ffn_wk': _L0_ffn_in['wk'], 'L0_ffn_wv': _L0_ffn_in['wv'], 'L0_ffn_gate_w': _L0_ffn_in['gate_w'], 'L0_ffn_gate_b': _L0_ffn_in['gate_b'], 'L0_ffn_ln_g': _L0_ffn_in['ln_g'], 'L0_ffn_ln_b': _L0_ffn_in['ln_b'], 'L0_ffn_fc1_w': _L0_ffn_in['fc1_w'], 'L0_ffn_fc1_b': _L0_ffn_in['fc1_b'], 'L0_ffn_fc2_w': _L0_ffn_in['fc2_w'], 'L0_ffn_fc2_b': _L0_ffn_in['fc2_b'], 'L0_ffn_fnorm_g': _L0_ffn_in['fnorm_g'], 'L0_ffn_fnorm_b': _L0_ffn_in['fnorm_b'], 'L0_ffn_fgate_w': _L0_ffn_in['fgate_w']}

def reference(x, txt, L0_tok_W, L0_tok_b, L0_attn_W_qkv, L0_attn_b_qkv, L0_attn_W_out, L0_attn_b_out, L0_ffn_hl_w, L0_ffn_hl_b, L0_ffn_wq, L0_ffn_wk, L0_ffn_wv, L0_ffn_gate_w, L0_ffn_gate_b, L0_ffn_ln_g, L0_ffn_ln_b, L0_ffn_fc1_w, L0_ffn_fc1_b, L0_ffn_fc2_w, L0_ffn_fc2_b, L0_ffn_fnorm_g, L0_ffn_fnorm_b, L0_ffn_fgate_w):
    import jax
    import jax.numpy as jnp

    def _L0_tok_ref(x, W, b):
        import jax, jax.numpy as jnp
        import numpy as np
        PATCH = 16
        B, C, H, Wd = x.shape
        p = PATCH
        nH, nW = (H // p, Wd // p)
        patches = x.reshape(B, C, nH, p, nW, p)
        patches = patches.transpose(0, 2, 4, 1, 3, 5)
        patches = patches.reshape(B, nH * nW, C * p * p)
        return jnp.einsum('bnk,ek->bne', patches, W) + b

    def _L0_attn_ref(x, W_qkv, b_qkv, W_out, b_out):
        import math
        import jax, jax.numpy as jnp
        import numpy as np
        EPS_DIV = 1e-07
        EPS_NORM = 1e-12

        def _l2_normalize(x, axis):
            n = jnp.sqrt(jnp.sum(x * x, axis=axis, keepdims=True))
            return x / jnp.maximum(n, EPS_NORM)
        b, N, C = x.shape
        qkv = x @ W_qkv + b_qkv
        q, k, v = jnp.split(qkv, 3, axis=2)
        q = q - jnp.mean(q, axis=2, keepdims=True)
        k = k - jnp.mean(k, axis=2, keepdims=True)
        q2 = q * q
        k2 = k * k
        q2s = jnp.sum(q2, axis=2, keepdims=True)
        k2s = jnp.sum(k2, axis=2, keepdims=True)
        k2 = _l2_normalize(k2 / (k2s + EPS_DIV), axis=-2)
        q2 = _l2_normalize(q2 / (q2s + EPS_DIV), axis=-1)
        kv = jnp.einsum('bnc,bnd->bcd', k2, v)
        t2 = jnp.einsum('bnc,bcd->bnd', q2, kv) / math.sqrt(N)
        attn = v + t2
        return attn @ W_out + b_out

    def _L0_ffn_ref(x, hl_w, hl_b, wq, wk, wv, gate_w, gate_b, ln_g, ln_b, fc1_w, fc1_b, fc2_w, fc2_b, fnorm_g, fnorm_b, fgate_w):
        import jax, jax.numpy as jnp
        import numpy as np
        B, S, H, NH, NE = (4, 256, 64, 4, 4)
        D = H // NH
        EPS = 1e-08

        def layernorm(x, g, b):
            m = jnp.mean(x, axis=-1, keepdims=True)
            v = jnp.mean((x - m) ** 2, axis=-1, keepdims=True)
            return (x - m) / jnp.sqrt(v + EPS) * g + b
        b, s, h = x.shape
        nh, d, _ = wk.shape
        ne = wq.shape[1]
        sx = jnp.einsum('bsh,ndh->bnsd', x, hl_w) + hl_b[None, :, None, :]
        pad = sx == 0
        q = jnp.einsum('bnsd,neod->bneso', sx, wq)
        k = jnp.einsum('bnsd,nod->bnso', sx, wk)
        v = jnp.einsum('bnsd,nod->bnso', sx, wv)
        causal = jnp.where(jnp.tril(jnp.ones((s, s), bool)), 0.0, -jnp.inf).astype(x.dtype)
        scores = jnp.einsum('bnesd,bntd->bnest', q, k) * d ** 0.5 + causal
        att = jax.nn.softmax(scores, axis=-1)
        qkv = jnp.einsum('bnest,bntd->bnesd', att, v)
        qkv = jnp.where(pad[:, :, None], 0.0, qkv)
        out = jnp.transpose(qkv, (0, 1, 3, 2, 4)).reshape(b, nh, s, ne * d)
        gs = jax.nn.softmax(jnp.einsum('bnsf,nef->bnse', out, gate_w) + gate_b[None, :, None, :], axis=-1)
        mixed = jnp.einsum('bnsed,bnse->bnsd', out.reshape(b, nh, s, ne, d), gs)
        resid = sx[jnp.arange(nh), jnp.arange(nh)]
        hn = layernorm(mixed + resid, ln_g, ln_b)
        f_n = jnp.transpose(hn, (0, 2, 1, 3)).reshape(b, s, h)
        fx = f_n.reshape(b, s, nh, d)
        pm = fx == 0
        hx = jnp.where(pm, 0.0, fx @ fc1_w.T + fc1_b)
        hx = jax.nn.relu(hx)
        hx = jnp.where(pm, 0.0, hx @ fc2_w.T + fc2_b)
        hx = layernorm(hx + fx, fnorm_g, fnorm_b)
        fout = hx.reshape(b, s, h)
        fg = jax.nn.softmax(fout @ fgate_w.T, axis=-1)
        return (fout.reshape(b, s, nh, d) * fg[..., None]).reshape(b, s, h)
    h = _L0_tok_ref(x, L0_tok_W, L0_tok_b)
    h = jnp.concatenate([h, txt], axis=1)
    h = h + _L0_attn_ref(_layernorm(h, axis=-1), L0_attn_W_qkv, L0_attn_b_qkv, L0_attn_W_out, L0_attn_b_out)
    h = h + _L0_ffn_ref(_layernorm(h, axis=-1), L0_ffn_hl_w, L0_ffn_hl_b, L0_ffn_wq, L0_ffn_wk, L0_ffn_wv, L0_ffn_gate_w, L0_ffn_gate_b, L0_ffn_ln_g, L0_ffn_ln_b, L0_ffn_fc1_w, L0_ffn_fc1_b, L0_ffn_fc2_w, L0_ffn_fc2_b, L0_ffn_fnorm_g, L0_ffn_fnorm_b, L0_ffn_fgate_w)
    return h

_drawn_inputs = setup_inputs


def setup_inputs(seed=0):
    import zlib

    import numpy as np

    out = dict(_drawn_inputs(seed))
    spreads = {'L0_ffn_ln_g': (1.0, 0.545),
     'L0_ffn_ln_b': (0.0, 0.459),
     'L0_ffn_fnorm_g': (1.0, 0.2),
     'L0_ffn_fnorm_b': (0.0, 0.446)}
    factors = {'L0_tok_b': 6.339,
     'L0_attn_b_out': 4.135,
     'L0_ffn_wq': 8.0,
     'L0_ffn_wk': 8.0,
     'L0_ffn_wv': 6.418,
     'L0_ffn_gate_w': 8.0,
     'L0_ffn_gate_b': 8.0,
     'L0_ffn_fc1_w': 8.0,
     'L0_ffn_fc1_b': 8.0,
     'L0_ffn_fc2_w': 8.0,
     'L0_ffn_fc2_b': 4.291}
    for name, (base, spread) in spreads.items():
        noise = np.random.default_rng([zlib.crc32(name.encode()), seed]).standard_normal(out[name].shape)
        drawn = base * np.exp(spread * noise) if base else spread * noise
        out[name] = jnp.asarray(drawn.astype(out[name].dtype))
    for name, factor in factors.items():
        out[name] = (out[name] * factor).astype(out[name].dtype)
    return out
```

```python
import numpy as np
from contextlib import ExitStack

import concourse.bass as bass
from concourse import mybir
from concourse.alu_op_type import AluOpType as ALU

ACT = mybir.ActivationFunctionType
AX = mybir.AxisListType
F32 = mybir.dt.float32
BF16 = mybir.dt.bfloat16
U8 = mybir.dt.uint8

P = 128
BATCH, CHANNELS, IMAGE, PATCH = 16, 3, 224, 16
GRID = IMAGE // PATCH
PATCHES = GRID * GRID
TEXT = 512
E = 64
SEQ = PATCHES + TEXT
TILES = -(-SEQ // P)
TAIL = SEQ - (TILES - 1) * P
PADDED = TILES * P
HEADS, EXPERTS, D = 4, 4, 16
GROUP = BATCH // 2
QUAD = 4
ROWS = GROUP * GRID
KCHUNKS = CHANNELS * PATCH * PATCH // P
IMG_TAIL = PATCHES - P
TXT_HEAD = P - IMG_TAIL
BANK = 512
A_COLS = 452
LN_EPS = 1e-5
DIV_EPS = 1e-7
NORM_EPS = 1e-12
INNER_EPS = 1e-8
MASKED = -1e30

C_IDENT, C_MASK, C_BD, C_BDE, C_SEL = 0, P, 2 * P, 2 * P + 4, 2 * P + 8
RAWC = EXPERTS * (D + 1)
SELC = RAWC + EXPERTS * EXPERTS
C_ALL = C_SEL + RAWC


def shape_constants():
    c = np.zeros((P, C_ALL), np.float32)
    c[:, C_IDENT:C_IDENT + P] = np.eye(P)
    s, t = np.arange(P)[:, None], np.arange(P)[None, :]
    c[:, C_MASK:C_MASK + P] = np.where(t <= s, 0.0, MASKED)
    for r in range(HEADS * D):
        c[r, C_BD + r // D] = 1.0
    for e in range(EXPERTS):
        c[32 * e:32 * e + D, C_BDE + e] = 1.0
        for d in range(D + 1):
            c[32 * e + d, C_SEL + e * (D + 1) + d] = 1.0
    return c


UNITS_S = []
for _j in range(TILES):
    for _lo, _hi in ((_j * P, BANK), (max(BANK, _j * P), SEQ)):
        if _lo < _hi:
            _n = min(EXPERTS, BANK // (_hi - _lo))
            UNITS_S += [(_j, _lo, _hi - _lo, _e, _n) for _e in range(0, EXPERTS, _n)]
UNITS_M = []
for _i in range(TILES):
    _w = TAIL + _i * P
    _cut = _w if _w <= BANK else (_w - P if _w - P <= BANK else BANK)
    for _lo, _hi in ((0, _cut), (_cut, _w)):
        if _lo < _hi:
            _n = min(EXPERTS, BANK // (_hi - _lo))
            UNITS_M += [(_i, _lo, _hi - _lo, _e, _n) for _e in range(0, EXPERTS, _n)]
UNITS = len(UNITS_S)
assert UNITS == len(UNITS_M) == 22
SLOTS = HEADS * UNITS
LAST_UNIT = [max(u for u, x in enumerate(UNITS_S) if x[0] == j) for j in range(TILES)]
Q_PARTS, K_PARTS = (1, 1, 2, 2, 1, 3), (1, 2, 1, 2, 3, 1)
PARTS = len(Q_PARTS)
KDIM = PARTS * D
MROWS = 3
PV_LAG, MASK_LAG, OT_AT, SEL_AT = 6, 2, 28, 31


MAX_STEPS = (
    "max_whole", "max1", "max_rest", "max2", "max3"
)
NORM_STEPS = (
    "a_sum", "a_mean", "a_centred", "a_var", "a_norm"
)
FF_STEPS = (
    "den_rec", "gate_logits", "gate_biased", "gate_max", "gate_sub", "gate_sum", "gate_rec", "gate_den",
    "mix_w", "mixture", "y_in", "y_sum", "y_mean", "y_centred", "y_var", "y_norm", "y_gain", "y_out",
    "fx_mask", "fc2", "z_in", "z_sum", "z_mean", "z_centred", "z_var", "z_norm", "z_gain", "z_out",
    "fg_logits", "fg_max", "fg_sub", "fg_sum", "fg_rec", "fgate"
)
STEPS = {step: (group, steps) for group, steps in (("max_steps", MAX_STEPS), ("norm_steps", NORM_STEPS), ("ff_steps", FF_STEPS))
         for step in steps}


def query_tile(i):
    return (0, TAIL) if i == 0 else (TAIL + (i - 1) * P, P)


def rows(tile):
    return P if tile < TILES - 1 else TAIL


def build(nc, a, out):
    ctx = ExitStack()
    with ctx:
        signals = {}

        def S(name):
            if name not in signals:
                signals[name] = ctx.enter_context(nc.semaphore(name))
            return signals[name]

        def sb(name, shape, dt=F32, stack=ctx):
            return stack.enter_context(nc.sbuf_tensor(name, shape, dt))

        H = sb("H", [P, BATCH, TILES, E])
        CONST = sb("CONST", [P, C_ALL])
        IDENT = CONST[:, C_IDENT:C_IDENT + P]
        BD = CONST[0:HEADS * D, C_BD:C_BD + HEADS]
        BDE = CONST[:, C_BDE:C_BDE + EXPERTS]
        IDB = sb("IDB", [P, P], BF16)
        MASKB = sb("MASKB", [P, P], BF16)
        HLT = sb("HLT", [E + 1, E])
        HLD = sb("HLD", [E + 1, E])
        WQ = sb("WQ", [E + 1, 2, P])
        WK = sb("WK", [E + 1, E])
        WV = sb("WV", [E + 1, HEADS, 32])
        F1 = sb("F1", [E + 1, HEADS, D])
        F2 = sb("F2", [E + 1, HEADS, D])
        FGW = sb("FGW", [E, HEADS])
        SEL = sb("SEL", [P, HEADS, SELC])
        R = sb("R", [P, HEADS, TILES, D])
        GB = sb("GB", [P, HEADS, EXPERTS])
        LNG = sb("LNG", [P, HEADS, D])
        LNB = sb("LNB", [P, HEADS, D])
        FNG = sb("FNG", [P, HEADS, D])
        FNB = sb("FNB", [P, HEADS, D])
        ONES = sb("ONES", [P, 1])
        HALF = sb("HALF", [P, 2 * QUAD * TILES])
        NEG_HALF, POS_HALF = HALF[:, 0:QUAD * TILES], HALF[:, QUAD * TILES:]
        PS = ctx.enter_context(nc.psum_tensor("PS", [P, 8, BANK], F32))

        first = ExitStack()
        WT = sb("WT", [P, KCHUNKS, E], stack=first)
        TOKB = sb("TOKB", [E, 1], stack=first)
        WQKV = sb("WQKV", [E + 1, 3 * E], stack=first)
        WQC = sb("WQC", [E + 1, E], stack=first)
        WKV = sb("WKV", [E + 1, 3 * E], stack=first)
        WOUT = sb("WOUT", [E, E], stack=first)
        BOUT = sb("BOUT", [E + 1, E], stack=first)
        X = sb("X", [ROWS, CHANNELS, PATCH * IMAGE], stack=first)
        XR = sb("XR", [ROWS, 2, GRID, P], stack=first)
        XT = sb("XT", [P, 4, 4 * ROWS], stack=first)
        HT = sb("HT", [E, GROUP, PATCHES], stack=first)
        XC = sb("XC", [P, QUAD * TILES, E], stack=first)
        SQ = sb("SQ", [P, QUAD * TILES, E], stack=first)
        XN = sb("XN", [P, QUAD * TILES, E], stack=first)
        K2 = sb("K2", [P, QUAD * TILES, E], stack=first)
        V = sb("V", [P, QUAD * TILES, E], stack=first)
        KN = sb("KN", [P, QUAD * TILES, E], stack=first)
        KNS = sb("KNS", [P, QUAD * TILES, E], stack=first)
        TMP = sb("TMP", [P, QUAD * TILES, E], stack=first)
        XNT = sb("XNT", [E + 1, QUAD, PADDED], stack=first)
        Q2T = sb("Q2T", [E, QUAD, PADDED], stack=first)
        Q4T = sb("Q4T", [E, QUAD, PADDED], stack=first)
        KVT = sb("KVT", [E, QUAD, E], stack=first)
        KVW = sb("KVW", [E, QUAD, E + 1], stack=first)
        ST = sb("ST", [P, 16, QUAD * TILES], stack=first)
        (MEAN, VAR, VARE, RSTD, K2S, RK, Q2S, Q4S, RQ, NQ, NQ2, FQ) = (ST[:, n, :] for n in range(12))
        SN = sb("SN", [E, 4, QUAD], stack=first)
        TOKW = sb("TOKW", [E, KCHUNKS * P], stack=first)
        HL = sb("HL", [HEADS * D, E + 1], stack=first)
        WQN = sb("WQN", [EXPERTS * D, HEADS, D], stack=first)
        WKN = sb("WKN", [D, HEADS, D], stack=first)
        WVN = sb("WVN", [D, HEADS, D], stack=first)
        GN = sb("GN", [HEADS * EXPERTS, EXPERTS, 32], stack=first)
        F1N = sb("F1N", [D, HEADS, D], stack=first)
        F2N = sb("F2N", [D, HEADS, D], stack=first)
        FGN = sb("FGN", [HEADS, E], stack=first)
        BQ = sb("BQ", [HEADS * D, HEADS, EXPERTS * D], stack=first)
        BKV = sb("BKV", [HEADS * D, 2, HEADS, D], stack=first)
        WVT = sb("WVT", [E, E + 1], stack=first)
        CM = sb("CM", [E + 1, 2, 1], stack=first)
        first.close()

        QA = [sb(f"QA{p}", [P, HEADS * EXPERTS, SEQ], BF16) for p in range(2)]
        KA = [sb(f"KA{p}", [P, HEADS, SEQ], BF16) for p in range(2)]
        PT = [sb(f"PT{j}", [P, EXPERTS, SEQ - j * P]) for j in range(TILES)]
        MT = [sb(f"MT{p}", [P, HEADS, SEQ], U8) for p in range(2)]
        VA = [sb(f"VA{p}", [P, TILES, HEADS, 32]) for p in range(2)]
        XFT = [sb(f"XFT{p}", [E + 1, PADDED]) for p in range(2)]
        Q1 = sb("Q1", [P, 2, SEQ], BF16)
        Q2 = sb("Q2", [P, 2, SEQ], BF16)
        Q3 = sb("Q3", [P, 2, SEQ], BF16)
        QR = sb("QR", [P, SEQ])
        K1 = sb("K1", [E, SEQ], BF16)
        K2B = sb("K2B", [E, SEQ], BF16)
        K3 = sb("K3", [E, SEQ], BF16)
        MK = sb("MK", [E, SEQ], U8)
        OT = sb("OT", [P, PADDED])
        RAW = sb("RAW", [P, HEADS, TILES, SELC])
        NM = sb("NM", [P, TILES, HEADS * EXPERTS])
        NP = sb("NP", [P, 2, HEADS * EXPERTS])
        NR = sb("NR", [P, TILES, 8])
        NB = sb("NB", [P, 2, TILES, 3, 8], BF16)
        NT = [sb(f"NT{h}", [24, SEQ], BF16) for h in range(2)]
        AC = sb("AC", [P, TILES, E])
        AS = sb("AS", [P, TILES, E])
        AN = sb("AN", [P, TILES, E])
        GL = sb("GL", [P, HEADS * TILES, EXPERTS, EXPERTS])
        MIXP = sb("MIXP", [P, HEADS * TILES, EXPERTS, D])
        Y = sb("Y", [P, HEADS * TILES, D])
        YC = sb("YC", [P, HEADS * TILES, D])
        FX = sb("FX", [P, TILES, HEADS, D])
        FM = sb("FM", [P, TILES, HEADS, D], BF16)
        FO = sb("FO", [P, TILES, HEADS, D])
        OUT = sb("OUT", [P, TILES, E])
        FXT = sb("FXT", [E + 1, PADDED])
        FMT = sb("FMT", [E, PADDED], BF16)
        HXT = sb("HXT", [E + 1, PADDED])
        FOT = FXT[0:E, :]
        S4 = sb("S4", [P, 6, HEADS * TILES, EXPERTS])
        RD, LG, EG, W4 = (S4[:, n, :, :] for n in range(4))
        FL, FE = (S4[:, n, 0:TILES, :] for n in (4, 5))
        S1 = sb("S1", [P, 20, HEADS * TILES])

        def it_static(it):
            return it if isinstance(it, int) else None

        def schedule(eng, iteration):
            def run(it, p):
                t = it_static(it)
                known = t is not None
                iteration(it, p,
                          C=not known or 0 <= t < BATCH,
                          M=not known or 0 <= t + 1 < BATCH,
                          A=not known or 0 <= t + 2 < BATCH,
                          D1=not known or 0 <= t - 1 < BATCH,
                          prev_a=not known or 0 <= t + 1 < BATCH,
                          first=known and t < 1)
            for it in (-2, -1, 0, 1):
                run(it, it % 2)
            with eng.Fori(1, BATCH // 2 - 1) as k:
                run(k * 2, 0)
                run(k * 2 + 1, 1)
            for it in (BATCH - 2, BATCH - 1, BATCH):
                run(it, it % 2)

        WEIGHT_DMAS = 26

        def apart(eng):
            eng.sem_inc(S("apart"), 1)

        def done(eng, step, times):
            group, steps = STEPS[step]
            eng.wait_ge(S(group), (times - 1) * len(steps) + steps.index(step) + 1)

        def at_least(eng, name, value):
            if isinstance(value, int) and value <= 0:
                return
            if name in STEPS:
                done(eng, name, value)
            else:
                eng.wait_ge(S(name), value)

        def halves(width):
            return ((0, BANK), (BANK, width))

        S_BANKS, M_BANKS, PV_BANK, MISC = (0, 1, 2), (3, 4), 5, 7

        def score_bank(p, slot):
            return S_BANKS[(slot + p) % len(S_BANKS)]

        def bank_left(it, p, slot):
            ring = len(S_BANKS)
            if slot >= ring:
                return it * SLOTS + slot - ring + 1
            last = max(x for x in range(SLOTS) if score_bank(1 - p, x) == score_bank(p, slot))
            return (it - 1) * SLOTS + last + 1

        def first_out(it):
            return isinstance(it, int) and it == 1

        PROJ_AT = (16, 18, 20, 22, 24, 26)
        PADS_AT, V_AT, TURN_AT = (28, 33), (35, 37), (12, 14)
        FX_AT, FC1_AT, FC2_AT, FO_AT, FG_AT = (43, 45), (48, 50), 54, (69, 71), 74
        MAX0_AT, MAX1_AT = 57, 2
        CLEARS = 10

        def txt_parts(g):
            yield 1, IMG_TAIL, 0, TXT_HEAD
            for t in range(2, TILES):
                yield t, 0, TXT_HEAD + (t - 2) * P, rows(t)

        block = ctx.enter_context(nc.Block())

        @block.sync
        def _(sp):
            n = 0

            def weight(dst, src):
                sp.dma_start(dst, src).then_inc(S("weights_in"), 16)
                return 1

            sp.wait_ge(S("weights_cleared"), 6)
            n += weight(CONST[:, :], a["const"])
            n += weight(TOKW[:, :], a["L0_tok_W"])
            n += weight(TOKB[:, :], a["L0_tok_b"].rearrange("(e o) -> e o", o=1))
            n += weight(WQKV[0:E, :], a["L0_attn_W_qkv"])
            n += weight(WQKV[E:E + 1, :], a["L0_attn_b_qkv"].rearrange("(o n) -> o n", o=1))
            n += weight(WOUT[:, :], a["L0_attn_W_out"])
            n += weight(BOUT[E:E + 1, :], a["L0_attn_b_out"].rearrange("(o n) -> o n", o=1))
            n += weight(HL[:, 0:E], a["L0_ffn_hl_w"].rearrange("n d h -> (n d) h"))
            n += weight(HL[:, E:E + 1], a["L0_ffn_hl_b"].rearrange("n (d o) -> (n d) o", o=1))
            n += weight(WQN[:, :, :], a["L0_ffn_wq"].rearrange("n e o d -> (e o) n d"))
            n += weight(WKN[:, :, :], a["L0_ffn_wk"].rearrange("n o d -> o n d"))
            n += weight(WVN[:, :, :], a["L0_ffn_wv"].rearrange("n o d -> o n d"))
            for e in range(EXPERTS):
                n += weight(GN[:, e, 0:D], a["L0_ffn_gate_w"].rearrange("n g (e d) -> (n g) e d", d=D)[:, e, :])
            for dst, name in ((F1, "fc1"), (F2, "fc2")):
                n += weight((F1N if dst is F1 else F2N)[:, :, :],
                            a[f"L0_ffn_{name}_w"].rearrange("o (n d) -> o n d", n=1).broadcast_to((D, HEADS, D)))
                n += weight(dst[E:E + 1, :, :],
                            a[f"L0_ffn_{name}_b"].rearrange("(a n d) -> a n d", a=1, n=1).broadcast_to((1, HEADS, D)))
            n += weight(FGN[:, :], a["L0_ffn_fgate_w"])
            n += weight(GB[:, :, :], a["L0_ffn_gate_b"].rearrange("(a n) e -> a n e", a=1).broadcast_to((P, HEADS, EXPERTS)))
            for dst, name in ((LNG, "ln_g"), (LNB, "ln_b"), (FNG, "fnorm_g"), (FNB, "fnorm_b")):
                n += weight(dst[:, :, :],
                            a[f"L0_ffn_{name}"].rearrange("(a n d) -> a n d", a=1, n=1).broadcast_to((P, HEADS, D)))
            assert n == WEIGHT_DMAS, n
            for g in range(BATCH // GROUP):
                for c in range(CHANNELS):
                    if g > 0:
                        sp.wait_ge(S("chunk"), (g - 1) * KCHUNKS + 2 * c + 2)
                    for b in range(GROUP):
                        sp.dma_start(X[b * GRID:(b + 1) * GRID, c, :],
                                     a["x"][g * GROUP + b, c, :, :].rearrange("(h p) w -> h (p w)", p=PATCH)
                                     ).then_inc(S(f"x_in{c}"), 16)
            def parts_in(b, p, half, first):
                h8, n2 = half * 8, half * 2
                sp.wait_ge(S("q3"), 6 * b + 2 * half + 2)
                if not first:
                    sp.wait_ge(S("scores"), (b - 2) * SLOTS + (half + 1) * SLOTS // 2)
                for r, (x, y) in enumerate(zip(Q_PARTS, K_PARTS)):
                    sp.dma_start(QA[p][r * D:(r + 1) * D, h8:h8 + 8, :], (Q1, Q2, Q3)[x - 1][:, half, :]
                                 ).then_inc(S(f"q_in{half}"), 16)
                sp.wait_ge(S("q3"), 6 * b + 6)
                for r, (x, y) in enumerate(zip(Q_PARTS, K_PARTS)):
                    sp.dma_start(KA[p][r * D:(r + 1) * D, n2:n2 + 2, :], (K1, K2B, K3)[y - 1][half * 32:half * 32 + 32, :]
                                 ).then_inc(S(f"k_in{half}"), 16)

            def max_in(b, p, half):
                sp.wait_ge(S("max_sbuf"), 2 * b + half + 1)
                sp.dma_start(QA[p][KDIM:KDIM + MROWS, half * 8:half * 8 + 8, :], NT[half][:, :]).then_inc(S(f"max_in{half}"), 16)

            def iteration(it, p, C, M, A, D1, prev_a, first):
                if prev_a:
                    parts_in(it + 1, 1 - p, 1, first)
                if C:
                    max_in(it, p, 1)
                if prev_a:
                    sp.wait_ge(S("pads"), 2 * (it + 1) + 2)
                    if not first:
                        sp.wait_ge(S("ot"), HEADS * it)
                    for e in range(EXPERTS):
                        sp.dma_start(MT[1 - p][32 * e:32 * e + D, :, :], MK[:, :]).then_inc(S("pads_in"), 16)
                if A:
                    parts_in(it + 2, p, 0, it_static(it) in (-2, -1))
                if M:
                    max_in(it + 1, 1 - p, 0)
                if D1:
                    sp.wait_ge(S("out_made"), it)
                    b = it - 1
                    o = out[bass.ds(b, 1), :, :] if not isinstance(b, int) else out[b:b + 1, :, :]
                    sp.dma_start(o[:, 0:SEQ - TAIL, :].rearrange("o (t p) e -> p (o t) e", p=P), OUT[:, 0:TILES - 1, :]
                                 ).then_inc(S("out_dma"), 16)
                    sp.dma_start(o[:, SEQ - TAIL:SEQ, :].rearrange("o p e -> (o p) e"), OUT[0:TAIL, TILES - 1, :]
                                 ).then_inc(S("out_dma"), 16)

            schedule(sp, iteration)
            sp.wait_ge(S("out_dma"), 32 * BATCH)

        @block.gpsimd
        def _(pool):
            for n, (dst, value, name) in enumerate((
                    (GN[:, :, :], 0.0, "weights_cleared"), (BOUT[:, :], 0.0, "weights_cleared"), (WV[:, :, :], 0.0, "weights_cleared"),
                    (NEG_HALF, -0.5, "weights_cleared"), (POS_HALF, 0.5, "weights_cleared"), (ONES[:, :], 1.0, "weights_cleared"))):
                pool.memset(dst, value).then_inc(S(name), 1)
                pool.wait_ge(S(name), n + 1)
            pool.memset(H[:, :, TILES - 1, :], 0.0).then_inc(S("tail_cleared"), 1)
            pool.wait_ge(S("tail_cleared"), 1)
            for n, (dst, value) in enumerate(((XNT[E:E + 1, :, :], 1.0), (KVW[:, :, E:E + 1], 1.0), (ST[:, :, :], 0.0))):
                pool.memset(dst, value).then_inc(S("ones_row"), 1)
                pool.wait_ge(S("ones_row"), n + 1)

            for g in range(BATCH // GROUP):
                for q in range(GROUP // QUAD):
                    i = g * (GROUP // QUAD) + q
                    pool.wait_ge(S("var"), i + 1)
                    pool.tensor_scalar(VARE, VAR, 1.0 / E, LN_EPS, ALU.mult, ALU.add).then_inc(S("var_eps"), 1)
                    pool.wait_ge(S("var_eps"), i + 1)
                    pool.tensor_tensor(RSTD, VARE, NEG_HALF, ALU.pow).then_inc(S("rstd"), 1)
                    for b in range(QUAD):
                        pool.wait_ge(S("q2t"), i * QUAD + b + 1)
                        pool.tensor_tensor(Q4T[:, b, :], Q2T[:, b, :], Q2T[:, b, :], ALU.mult).then_inc(S("q4t"), 1)
                    pool.wait_ge(S("k_len2"), i + 1)
                    pool.tensor_tensor(SN[:, 1, :], SN[:, 0, :], POS_HALF[0:E, 0:QUAD], ALU.pow).then_inc(S("k_len"), 1)
                    pool.wait_ge(S("q4s"), QUAD * (i + 1))
                    pool.tensor_tensor(NQ, Q4S, POS_HALF, ALU.pow).then_inc(S("q_len"), 1)

            i = BATCH // QUAD
            pool.wait_ge(S("var"), i + 1)
            pool.tensor_scalar(VARE, VAR, 1.0 / E, LN_EPS, ALU.mult, ALU.add).then_inc(S("var_eps"), 1)
            pool.wait_ge(S("var_eps"), i + 1)
            pool.tensor_tensor(RSTD, VARE, NEG_HALF, ALU.pow).then_inc(S("rstd"), 1)

            pool.wait_ge(S("resid"), HEADS)
            clears = [(MT[0][:, :, :], 1), (MT[1][:, :, :], 1), (OT[:, :], 1.0), (NM[:, :, :], 0.0),
                      (KA[0][KDIM:KDIM + MROWS, :, :], 1.0), (KA[1][KDIM:KDIM + MROWS, :, :], 1.0),
                      (XFT[0][E:E + 1, :], 1.0), (XFT[1][E:E + 1, :], 1.0), (FXT[E:E + 1, :], 1.0), (HXT[E:E + 1, :], 1.0)]
            for n, (dst, value) in enumerate(clears):
                pool.memset(dst, value).then_inc(S("cleared"), 1)
                pool.wait_ge(S("cleared"), n + 1)
            assert len(clears) == CLEARS

            def iteration(it, p, C, M, A, D1, prev_a, first):
                def mask(b, n, j):
                    r = rows(j)
                    units = [u for u, x in enumerate(UNITS_S) if x[0] == j and x[1] == j * P]
                    pool.wait_ge(S("exped"), b * SLOTS + n * UNITS + max(units) + 1)
                    apart(pool)
                    pool.affine_select(out=PT[j][0:r, :, 0:r], in_=PT[j][0:r, :, 0:r], pattern=[[0, EXPERTS], [1, r]],
                                       compare_op=ALU.is_ge, fill=0.0, base=0, channel_multiplier=-1
                                       ).then_inc(S("masked"), 1)

                for slot in range(SLOTS):
                    for n in range(-1, HEADS):
                        for j in range(TILES):
                            if slot == n * UNITS + LAST_UNIT[j] + MASK_LAG:
                                if n >= 0 and C:
                                    mask(it, n, j)
                                if n < 0 and D1:
                                    mask(it - 1, HEADS - 1, j)
                    if A:
                        b = it + 2
                        if slot == 8:
                            done(pool, "a_var", b + 1)
                            apart(pool)
                            pool.tensor_scalar(S1[:, 2, 0:TILES], S1[:, 1, 0:TILES], 1.0 / E, LN_EPS, ALU.mult, ALU.add
                                               ).then_inc(S("a_eps"), 1)
                            pool.wait_ge(S("a_eps"), b + 1)
                            pool.tensor_tensor(S1[:, 3, 0:TILES], S1[:, 2, 0:TILES], NEG_HALF[:, 0:TILES], ALU.pow
                                               ).then_inc(S("a_rstd"), 1)
                        for idx, at in enumerate(PROJ_AT):
                            if slot == at + 1:
                                half, c = divmod(idx, 2)
                                lo, hi = halves(SEQ)[c]
                                if half < 2:
                                    src, mid, low = QR[:, lo:hi], Q2[:, half, lo:hi], Q3[:, half, lo:hi]
                                else:
                                    src, mid, low = QR[0:E, lo:hi], K2B[:, lo:hi], K3[:, lo:hi]
                                pool.wait_ge(S("q_rest"), 6 * b + idx + 1)
                                apart(pool)
                                pool.tensor_scalar(mid, src, 1.0, 0.0, ALU.mult, ALU.add).then_inc(S("q2"), 1)
                                pool.wait_ge(S("q2"), 6 * b + idx + 1)
                                pool.tensor_tensor(low, src, mid, ALU.subtract).then_inc(S("q3"), 1)
                                if half == 2:
                                    pool.wait_ge(S("q3"), 6 * b + idx + 1)
                    if D1:
                        b = it - 1
                        if slot == 12:
                            pool.wait_ge(S("raw"), HEADS * (b + 1))
                            done(pool, "den_rec", b + 1)
                            pool.tensor_tensor(GL[:, :, :, :], RAW[:, :, :, RAWC:SELC].rearrange("p n t (e g) -> p (n t) e g", e=EXPERTS),
                                               RD.rearrange("p k (e o) -> p k e o", o=1).broadcast_to((P, HEADS * TILES, EXPERTS, EXPERTS)),
                                               ALU.mult).then_inc(S("gate_parts"), 1)
                        for n in range(HEADS):
                            if slot == 24 + n:
                                done(pool, "mix_w", b + 1)
                                k6 = slice(n * TILES, (n + 1) * TILES)
                                pool.tensor_tensor(MIXP[:, k6, :, :],
                                                   RAW[:, n, :, 0:RAWC].rearrange("p t (e c) -> p t e c", e=EXPERTS)[:, :, :, 0:D],
                                                   W4[:, k6, :].rearrange("p k (e o) -> p k e o", o=1).broadcast_to((P, TILES, EXPERTS, D)),
                                                   ALU.mult).then_inc(S("mixed"), 1)
                        for name, at, v in (("y", 37, 6), ("z", 64, 12)):
                            if slot == at:
                                done(pool, f"{name}_var", b + 1)
                                apart(pool)
                                pool.tensor_scalar(S1[:, v, :], S1[:, v - 1, :], 1.0 / D, INNER_EPS, ALU.mult, ALU.add
                                                   ).then_inc(S(f"{name}_eps"), 1)
                                pool.wait_ge(S(f"{name}_eps"), b + 1)
                                pool.tensor_tensor(S1[:, v + 1, :], S1[:, v, :], NEG_HALF, ALU.pow).then_inc(S(f"{name}_rstd"), 1)
                        if slot == 83:
                            done(pool, "fgate", b + 1)
                            if not first_out(it):
                                pool.wait_ge(S("out_dma"), 32 * b)
                            pool.tensor_tensor(OUT[:, :, :].rearrange("p t (n d) -> p (t n) d", n=HEADS),
                                               FO[:, :, :, :].rearrange("p t n d -> p (t n) d"),
                                               FE.rearrange("p t (n o) -> p (t n) o", o=1).broadcast_to((P, HEADS * TILES, D)),
                                               ALU.mult).then_inc(S("out_gated"), 1)
                            pool.wait_ge(S("out_gated"), b + 1)
                            pool.tensor_tensor(OUT[:, :, :], OUT[:, :, :], H[:, bass.ds(b, 1), :, :].rearrange("p o t e -> p (o t) e"),
                                               ALU.add).then_inc(S("out_made"), 1)

            schedule(pool, iteration)

        @block.scalar
        def _(act):
            act.wait_ge(S("tail_cleared"), 1)
            for g in range(BATCH // GROUP):
                for t, p0, tok, n in txt_parts(g):
                    act.dma_start(H[p0:p0 + n, g * GROUP:(g + 1) * GROUP, t, :],
                                  a["txt"][g * GROUP:(g + 1) * GROUP, tok:tok + n, :].rearrange("b p e -> p b e")
                                  ).then_inc(S(f"txt_in{g}"), 16)

            for g in range(BATCH // GROUP):
                for u in range(0, 4 * KCHUNKS, 2):
                    act.wait_ge(S("xt_psum"), g * 4 * KCHUNKS + u + 1)
                    if u >= 4:
                        act.wait_ge(S("xt_read"), g * 4 * KCHUNKS + u - 4 + 1)
                    act.copy(XT[:, u % 4, :], PS[:, 4 + u % 4, 0:4 * ROWS]).then_inc(S("xt_sbuf_act"), 1)
                act.wait_ge(S("xt_read"), (g + 1) * 4 * KCHUNKS)
                for w in range(2):
                    act.activation(HT[:, :, :].rearrange("e b (h w) -> e w (b h)", w=GRID)[:, 4 * w:4 * w + 4, :],
                                   PS[0:E, w, 0:4 * ROWS].rearrange("e (w r) -> e w r", w=4),
                                   ACT.Identity, bias=TOKB[:, 0:1]).then_inc(S("ht"), 1)
                for q in range(GROUP // QUAD):
                    i = g * (GROUP // QUAD) + q
                    b0 = g * GROUP + q * QUAD
                    act.wait_ge(S("img_tokens"), i + 1)
                    act.copy(H[:, b0:b0 + QUAD, 0, :], PS[:, 4, 0:QUAD * E].rearrange("p (b e) -> p b e", b=QUAD)
                             ).then_inc(S("img_in_h"), 1)
                    act.copy(H[0:IMG_TAIL, b0:b0 + QUAD, 1, :],
                             PS[0:IMG_TAIL, 4, QUAD * E:2 * QUAD * E].rearrange("p (b e) -> p b e", b=QUAD)
                             ).then_inc(S("img_in_h"), 1)
                    act.wait_ge(S("centred"), i + 1)
                    act.activation(SQ[:, :, :], XC[:, :, :], ACT.Square).then_inc(S("squared"), 1)
                    for b in range(QUAD):
                        n = i * QUAD + b
                        act.wait_ge(S("xnt_psum"), n + 1)
                        act.copy(XNT[0:E, b, :], PS[0:E, 0:2, :].rearrange("e a n -> e (a n)")[:, 0:PADDED]).then_inc(S("xnt"), 1)
                        act.wait_ge(S("q_psum"), n + 1)
                        act.activation(Q2T[:, b, :], PS[0:E, 2:4, :].rearrange("e a n -> e (a n)")[:, 0:PADDED],
                                       ACT.Square).then_inc(S("q2t"), 1)
                        act.wait_ge(S("kv_psum"), n + 1)
                        act.activation(K2[:, b * TILES:(b + 1) * TILES, :].rearrange("p (a t) e -> p a t e", a=3),
                                       PS[:, 5:8, 0:6 * E].rearrange("p a (t n) -> p a t n", t=2)[:, :, :, 0:E],
                                       ACT.Square).then_inc(S("k2"), 1)
                        act.copy(V[:, b * TILES:(b + 1) * TILES, :].rearrange("p (a t) e -> p a t e", a=3),
                                 PS[:, 5:8, 0:6 * E].rearrange("p a (t n) -> p a t n", t=2)[:, :, :, E:2 * E]
                                 ).then_inc(S("v"), 1)
                    act.wait_ge(S("kn"), i + 1)
                    act.activation(KNS[:, :, :], KN[:, :, :], ACT.Square).then_inc(S("kns"), 1)
                    act.wait_ge(S("kvt_psum"), i + 1)
                    act.copy(KVT[:, :, :], PS[0:E, 4, 0:QUAD * E].rearrange("p (b e) -> p b e", b=QUAD)).then_inc(S("kvt"), 1)

            i = BATCH // QUAD
            act.wait_ge(S("centred"), i + 1)
            act.activation(SQ[:, :, :], XC[:, :, :], ACT.Square).then_inc(S("squared"), 1)
            for b in range(HEADS):
                act.wait_ge(S("xnt_psum"), BATCH + b + 1)
                act.copy(XNT[0:E, b, :], PS[0:E, 0:2, :].rearrange("e a n -> e (a n)")[:, 0:PADDED]).then_inc(S("xnt"), 1)
                act.wait_ge(S("resid_psum"), b + 1)
                act.copy(R[:, b, :, :], PS[:, 2, 0:TILES * D].rearrange("p (t d) -> p t d", t=TILES)).then_inc(S("resid"), 1)

            act.wait_ge(S("cleared"), CLEARS)

            def iteration(it, p, C, M, A, D1, prev_a, first):
                def exponentials(slot):
                    n, u = divmod(slot, UNITS)
                    j, lo, w, e0, ne = UNITS_S[u]
                    count = it * SLOTS + slot
                    r = rows(j)
                    act.wait_ge(S("scores"), count + 1)
                    if UNITS_S[u - 1][0] != j or u == 0:
                        at_least(act, "summed", (it * HEADS + n - 1) * TILES + j + 1)
                    act.activation(PT[j][0:r, e0:e0 + ne, lo - j * P:lo - j * P + w],
                                   PS[0:r, score_bank(p, slot), 0:ne * w].rearrange("p (e w) -> p e w", e=ne),
                                   ACT.Exp).then_inc(S("exped"), 1)

                def raw(b, n):
                    act.wait_ge(S("raw_psum"), b * HEADS + n + 1)
                    if n == 0:
                        at_least(act, "mixed", HEADS * b)
                    act.copy(RAW[:, n, :, :], PS[:, 7, 0:TILES * SELC].rearrange("p (t c) -> p t c", t=TILES)).then_inc(S("raw"), 1)

                def maxima(b, half):
                    act.wait_ge(S("max_psum"), 2 * b + half + 1)
                    at_least(act, f"max_in{half}", 16 * b)
                    act.copy(NT[half][:, :], PS[0:24, 7, 0:SEQ // 2].bitcast(BF16)).then_inc(S("max_sbuf"), 1)

                for slot in range(SLOTS):
                    if C:
                        exponentials(slot)
                    if slot == MAX1_AT and C:
                        maxima(it, 1)
                    if slot == MAX0_AT and M:
                        maxima(it + 1, 0)
                    if D1 and slot == SEL_AT + 3 * UNITS - SLOTS:
                        raw(it - 1, HEADS - 1)
                    for n in range(HEADS - 1):
                        if C and slot == SEL_AT + n * UNITS:
                            raw(it, n)
                    if A:
                        b = it + 2
                        if slot == 4:
                            done(act, "a_centred", b + 1)
                            act.activation(AS[:, :, :], AC[:, :, :], ACT.Square).then_inc(S("a_squared"), 1)
                        for c, at in enumerate(TURN_AT):
                            if slot == at:
                                lo, hi = halves(PADDED)[c]
                                act.wait_ge(S("xft_psum"), 2 * b + c + 1)
                                act.copy(XFT[p][0:E, lo:hi], PS[0:E, 7, 0:hi - lo]).then_inc(S("xft"), 1)
                        for idx, at in enumerate(PROJ_AT):
                            if slot == at:
                                half, c = divmod(idx, 2)
                                lo, hi = halves(SEQ)[c]
                                if c == 0 and half < 2:
                                    at_least(act, f"q_in{half}", 16 * PARTS * b)
                                if c == 0 and half == 2:
                                    at_least(act, "k_in0", 16 * PARTS * b)
                                    at_least(act, "k_in1", 16 * PARTS * b)
                                dst = Q1[:, half, lo:hi] if half < 2 else K1[:, lo:hi]
                                act.wait_ge(S("proj"), 6 * b + idx + 1)
                                act.copy(dst, PS[0:(P if half < 2 else E), 7, 0:hi - lo]).then_inc(S("q1"), 1)
                    if M:
                        for c, at in enumerate(V_AT):
                            if slot == at:
                                b = it + 1
                                t0, t1 = ((0, 4), (4, TILES))[c]
                                act.wait_ge(S("v_psum"), 2 * b + c + 1)
                                act.copy(VA[1 - p][:, t0:t1, :, :],
                                         PS[:, 7, 0:(t1 - t0) * P].rearrange("p (t n c) -> p t n c", t=t1 - t0, n=HEADS)
                                         ).then_inc(S("va"), 1)
                    if D1:
                        b = it - 1
                        if slot == 18:
                            done(act, "gate_sub", b + 1)
                            act.activation(EG, LG, ACT.Exp).then_inc(S("gate_exp"), 1)
                        for name, at in (("y", 35), ("z", 62)):
                            if slot == at:
                                done(act, f"{name}_centred", b + 1)
                                act.activation(GL[:, :, :, :].rearrange("p k e g -> p k (e g)"), YC[:, :, :], ACT.Square
                                               ).then_inc(S(f"{name}_squared"), 1)
                        for c, at in enumerate(FX_AT):
                            if slot == at:
                                lo, hi = halves(PADDED)[c]
                                act.wait_ge(S("fxt_psum"), 2 * b + c + 1)
                                act.copy(FXT[0:E, lo:hi], PS[0:E, 7, 0:hi - lo]).then_inc(S("fxt"), 1)
                        for c, at in enumerate(FO_AT):
                            if slot == at:
                                lo, hi = halves(PADDED)[c]
                                act.wait_ge(S("fot_psum"), 2 * b + c + 1)
                                act.copy(FOT[:, lo:hi], PS[0:E, 7, 0:hi - lo]).then_inc(S("fot"), 1)
                        if slot == 79:
                            done(act, "fg_sub", b + 1)
                            act.activation(FE, FL, ACT.Exp).then_inc(S("fg_exp"), 1)

            schedule(act, iteration)

        @block.vector
        def _(dve):
            def stage(ins, name):
                ins.then_inc(S(STEPS[name][0] if name in STEPS else name), 1)

            dve.wait_ge(S("weights_in"), 16 * WEIGHT_DMAS)
            dve.tensor_copy(IDB[:, :], IDENT).then_inc(S("w_forms"), 1)
            dve.tensor_copy(MASKB[:, :], CONST[:, C_MASK:C_MASK + P]).then_inc(S("w_forms"), 1)
            dve.reduce_sum(CM[:, :, 0], WQKV[:, 0:2 * E].rearrange("p (a e) -> p a e", a=2), AX.X).then_inc(S("w_mean"), 1)
            dve.wait_ge(S("w_mean"), 1)
            dve.tensor_scalar(CM[:, :, 0], CM[:, :, 0], 1.0 / E, None, ALU.mult).then_inc(S("w_mean"), 1)
            dve.wait_ge(S("w_mean"), 2)
            dve.tensor_tensor(WQC[:, :], WQKV[:, 0:E], CM[:, 0, :].broadcast_to((E + 1, E)), ALU.subtract).then_inc(S("w_forms"), 1)
            dve.tensor_tensor(WKV[:, 0:E], WQKV[:, E:2 * E], CM[:, 1, :].broadcast_to((E + 1, E)), ALU.subtract).then_inc(S("w_forms"), 1)
            dve.tensor_copy(WKV[:, E:2 * E], WQKV[:, 2 * E:3 * E]).then_inc(S("w_forms"), 1)
            dve.wait_ge(S("w_turned"), 1)
            dve.tensor_copy(WT[:, :, :], PS[:, 0, 0:KCHUNKS * E].rearrange("p (k e) -> p k e", k=KCHUNKS)).then_inc(S("w_forms"), 1)
            dve.tensor_copy(HLT[:, :], PS[0:E + 1, 1, 0:E]).then_inc(S("w_forms"), 1)
            dve.tensor_copy(HLD[:, :].rearrange("p (d n) -> p n d", n=HEADS),
                            PS[0:E + 1, 1, 0:E].rearrange("p (n d) -> p n d", n=HEADS)).then_inc(S("w_forms"), 1)
            bd = BD.rearrange("p (n o) -> p n o", o=1)
            dve.tensor_tensor(BQ[:, :, :], PS[0:E, 1, 64:128].rearrange("p (n c) -> p n c", n=1).broadcast_to((E, HEADS, E)),
                              bd.broadcast_to((E, HEADS, E)), ALU.mult).then_inc(S("w_forms"), 1)
            for dst, at in ((BKV[:, 0, :, :], 128), (BKV[:, 1, :, :], 144), (F1[0:E, :, :], 176), (F2[0:E, :, :], 192)):
                dve.tensor_tensor(dst, PS[0:E, 1, at:at + D].rearrange("p (n c) -> p n c", n=1).broadcast_to((E, HEADS, D)),
                                  bd.broadcast_to((E, HEADS, D)), ALU.mult).then_inc(S("w_forms"), 1)
            dve.tensor_copy(FGW[:, :], PS[0:E, 1, 208:212]).then_inc(S("w_forms"), 1)
            dve.tensor_copy(WVT[:, :], PS[0:E, 1, 256:256 + E + 1]).then_inc(S("w_forms"), 1)
            for n in range(HEADS):
                dve.tensor_copy(SEL[:, n, 0:RAWC], CONST[:, C_SEL:C_SEL + RAWC]).then_inc(S("w_forms"), 1)
                dve.tensor_tensor(SEL[:, n, RAWC:SELC].rearrange("p (e g) -> p e g", e=EXPERTS),
                                  PS[:, 1, 160 + n * EXPERTS:160 + (n + 1) * EXPERTS].rearrange("p (e g) -> p e g", e=1)
                                  .broadcast_to((P, EXPERTS, EXPERTS)),
                                  BDE.rearrange("p (e g) -> p e g", g=1).broadcast_to((P, EXPERTS, EXPERTS)),
                                  ALU.mult).then_inc(S("w_forms"), 1)
            dve.wait_ge(S("w_made"), 1)
            for half in range(2):
                dve.tensor_scalar(WQ[:, half, :].rearrange("p (o h) -> p h o", o=D),
                                  PS[0:E + 1, 2, half * P:(half + 1) * P].rearrange("p (h o) -> p h o", o=D),
                                  float(D) ** 0.5, None, ALU.mult).then_inc(S("w_forms"), 1)
                dve.tensor_copy(WK[:, half * 32:half * 32 + 32].rearrange("p (o n) -> p n o", n=2),
                                PS[0:E + 1, 2, 256 + half * 32:256 + half * 32 + 32].rearrange("p (n o) -> p n o", n=2)
                                ).then_inc(S("w_forms"), 1)
            dve.tensor_copy(WV[:, :, 0:D], PS[0:E + 1, 2, 320:384].rearrange("p (n d) -> p n d", n=HEADS)).then_inc(S("w_forms"), 1)
            dve.memset(WV[E:E + 1, :, D:D + 1], 1.0).then_inc(S("w_forms"), 1)
            dve.tensor_tensor(WKV[:, 2 * E:3 * E], PS[0:E + 1, 3, 0:E], BOUT[:, :], ALU.add).then_inc(S("w_ready"), 1)

            def bc(x):
                return x.rearrange("p (n o) -> p n o", o=1).broadcast_to((P, QUAD * TILES, E))

            for g in range(BATCH // GROUP):
                def cut(chunk):
                    c, half = divmod(chunk, 2)
                    if half == 0:
                        dve.wait_ge(S(f"x_in{c}"), 16 * GROUP * (g + 1))
                    if chunk >= 2:
                        dve.wait_ge(S("xt_psum"), g * 4 * KCHUNKS + 4 * (chunk - 1))
                    x = X[:, c, :].rearrange("r (p w x) -> r w p x", p=PATCH, w=GRID)
                    dve.tensor_copy(XR[:, chunk % 2, :, :].rearrange("r w (p x) -> r w p x", p=8),
                                         x[:, :, half * 8:half * 8 + 8, :]).then_inc(S("chunk"), 1)

                cut(0)
                for u in range(1, 4 * KCHUNKS, 2):
                    if u % 4 == 1 and u // 4 + 1 < KCHUNKS:
                        cut(u // 4 + 1)
                    dve.wait_ge(S("xt_psum"), g * 4 * KCHUNKS + u + 1)
                    if u >= 4:
                        dve.wait_ge(S("xt_read"), g * 4 * KCHUNKS + u - 4 + 1)
                    n = (4 if u % 4 < 3 else 2) * ROWS
                    dve.tensor_copy(XT[:, u % 4, 0:n], PS[:, 4 + u % 4, 0:n]).then_inc(S("xt_sbuf_dve"), 1)
                dve.wait_ge(S("xt_read"), (g + 1) * 4 * KCHUNKS)
                for w, n in ((2, 4), (3, 2)):
                    dve.tensor_scalar(HT[:, :, :].rearrange("e b (h w) -> e w (b h)", w=GRID)[:, 4 * w:4 * w + n, :],
                                      PS[0:E, w, 0:n * ROWS].rearrange("e (w r) -> e w r", w=n),
                                      TOKB[:, 0:1], None, ALU.add).then_inc(S("ht"), 1)
                for q in range(GROUP // QUAD):
                    i = g * (GROUP // QUAD) + q
                    b0 = g * GROUP + q * QUAD
                    h = H[:, b0:b0 + QUAD, :, :].rearrange("p b t e -> p (b t) e")
                    dve.wait_ge(S("img_in_h"), 2 * (i + 1))
                    for gg in range(BATCH // GROUP):
                        dve.wait_ge(S(f"txt_in{gg}"), 16 * (TILES - 1))
                    stage(dve.reduce_sum(MEAN, h, AX.X), "sum")
                    dve.wait_ge(S("sum"), i + 1)
                    stage(dve.tensor_scalar(MEAN, MEAN, 1.0 / E, None, ALU.mult), "mean")
                    dve.wait_ge(S("mean"), i + 1)
                    stage(dve.tensor_tensor(XC[:, :, :], h, bc(MEAN), ALU.subtract), "centred")
                    dve.wait_ge(S("squared"), i + 1)
                    stage(dve.reduce_sum(VAR, SQ[:, :, :], AX.X), "var")
                    dve.wait_ge(S("rstd"), i + 1)
                    stage(dve.tensor_tensor(XN[:, :, :], XC[:, :, :], bc(RSTD), ALU.mult), "xn")
                    for b in range(QUAD):
                        n = i * QUAD + b
                        dve.wait_ge(S("kv_psum"), n + 1)
                        dve.wait_ge(S("v"), n + 1)
                        hb = H[:, b0 + b:b0 + b + 1, :, :].rearrange("p b (a t) e -> p (b a) t e", a=3)
                        stage(dve.tensor_tensor(hb, PS[:, 5:8, 0:6 * E].rearrange("p a (t n) -> p a t n", t=2)[:, :, :, 2 * E:3 * E],
                                                hb, ALU.add), "h_vo")
                    dve.wait_ge(S("k2"), QUAD * (i + 1))
                    stage(dve.reduce_sum(K2S, K2[:, :, :], AX.X), "k2s")
                    dve.wait_ge(S("k2s"), i + 1)
                    stage(dve.tensor_scalar(K2S, K2S, DIV_EPS, None, ALU.add), "k2s_eps")
                    dve.wait_ge(S("k2s_eps"), i + 1)
                    stage(dve.reciprocal(RK, K2S), "rk")
                    dve.wait_ge(S("rk"), i + 1)
                    stage(dve.tensor_tensor(KN[:, :, :], K2[:, :, :], bc(RK), ALU.mult), "kn")
                    dve.wait_ge(S("kvt_psum"), i + 1)
                    dve.wait_ge(S("kvt"), i + 1)
                    stage(dve.tensor_copy(SN[:, 0, :], PS[0:E, 4, QUAD * E:QUAD * E + QUAD]), "k_len2")
                    dve.wait_ge(S("k_len"), i + 1)
                    stage(dve.tensor_scalar(SN[:, 2, :], SN[:, 1, :], NORM_EPS, float(SEQ) ** 0.5, ALU.max, ALU.mult), "k_len_max")
                    dve.wait_ge(S("k_len_max"), i + 1)
                    stage(dve.reciprocal(SN[:, 3, :], SN[:, 2, :]), "k_scale")
                    dve.wait_ge(S("k_scale"), i + 1)
                    dve.wait_ge(S("kvw_psum"), i + 1)
                    stage(dve.tensor_tensor(KVW[:, :, 0:E], PS[0:E, 5, 0:QUAD * E].rearrange("p (b e) -> p b e", b=QUAD),
                                            SN[:, 3, :].rearrange("p (b o) -> p b o", o=1).broadcast_to((E, QUAD, E)),
                                            ALU.mult), "kvw")
                    for b in range(QUAD):
                        n = i * QUAD + b
                        t6 = slice(b * TILES, (b + 1) * TILES)
                        dve.wait_ge(S("t2_psum"), n + 1)
                        ps = PS[:, 6 + b % 2, 0:TILES * (E + 2)].rearrange("p (t n) -> p t n", t=TILES)
                        stage(dve.tensor_copy(TMP[:, t6, :], ps[:, :, 0:E]), "t2")
                        stage(dve.tensor_copy(Q2S[:, t6], ps[:, :, E]), "q2s")
                        stage(dve.tensor_copy(Q4S[:, t6], ps[:, :, E + 1]), "q4s")
                    dve.wait_ge(S("q2s"), QUAD * (i + 1))
                    stage(dve.tensor_scalar(Q2S, Q2S, DIV_EPS, None, ALU.add), "q2s_eps")
                    dve.wait_ge(S("q2s_eps"), i + 1)
                    stage(dve.reciprocal(RQ, Q2S), "rq")
                    dve.wait_ge(S("q_len"), i + 1)
                    dve.wait_ge(S("rq"), i + 1)
                    stage(dve.tensor_tensor(NQ2, NQ, RQ, ALU.mult), "nq")
                    dve.wait_ge(S("nq"), i + 1)
                    stage(dve.tensor_scalar(NQ2, NQ2, NORM_EPS, None, ALU.max), "nq_max")
                    dve.wait_ge(S("nq_max"), i + 1)
                    stage(dve.reciprocal(FQ, NQ2), "nq_rec")
                    dve.wait_ge(S("nq_rec"), i + 1)
                    stage(dve.tensor_tensor(FQ, FQ, RQ, ALU.mult), "fq")
                    dve.wait_ge(S("fq"), i + 1)
                    stage(dve.tensor_tensor(TMP[:, :, :], TMP[:, :, :], bc(FQ), ALU.mult), "t2f")
                    dve.wait_ge(S("t2f"), i + 1)
                    stage(dve.tensor_tensor(h, h, TMP[:, :, :], ALU.add), "h2_done")

            i = BATCH // QUAD
            h = H[:, 0:QUAD, :, :].rearrange("p b t e -> p (b t) e")
            stage(dve.reduce_sum(MEAN, h, AX.X), "sum")
            dve.wait_ge(S("sum"), i + 1)
            stage(dve.tensor_scalar(MEAN, MEAN, 1.0 / E, None, ALU.mult), "mean")
            dve.wait_ge(S("mean"), i + 1)
            stage(dve.tensor_tensor(XC[:, :, :], h, bc(MEAN), ALU.subtract), "centred")
            dve.wait_ge(S("squared"), i + 1)
            stage(dve.reduce_sum(VAR, SQ[:, :, :], AX.X), "var")
            dve.wait_ge(S("rstd"), i + 1)
            stage(dve.tensor_tensor(XN[:, :, :], XC[:, :, :], bc(RSTD), ALU.mult), "xn")

            dve.wait_ge(S("cleared"), CLEARS)

            def iteration(it, p, C, M, A, D1, prev_a, first):
                def maximum(b, slot):
                    n, u = divmod(slot, UNITS)
                    i, lo, w, e0, ne = UNITS_M[u]
                    r = query_tile(i)[1]
                    heads = slice(n * EXPERTS + e0, n * EXPERTS + e0 + ne)
                    dst = NM[0:r, i, heads] if lo == 0 else NP[0:r, i - (TILES - 2), heads]
                    dve.wait_ge(S("max_scores"), b * SLOTS + slot + 1)
                    dve.tensor_reduce(dst, PS[0:r, M_BANKS[slot % 2], 0:ne * w].rearrange("p (e w) -> p e w", e=ne), AX.X, ALU.max,
                                      negate=True).then_inc(S("maxed"), 1)

                def split_maxima(b, half, step):
                    h8 = slice(half * 8, half * 8 + 8)
                    count = 2 * b + half + 1
                    if step == 0:
                        dve.wait_ge(S("maxed"), b * SLOTS + (half + 1) * SLOTS // 2)
                        stage(dve.tensor_tensor(NM[:, TILES - 2:TILES, h8], NM[:, TILES - 2:TILES, h8], NP[:, :, h8], ALU.min), "max_whole")
                    if step == 1:
                        done(dve, "max_whole", count)
                        at_least(dve, "max_psum", count - 2)
                        stage(dve.tensor_copy(NB[:, half, :, 0, :], NM[:, :, h8]), "max1")
                    if step == 2:
                        done(dve, "max1", count)
                        stage(dve.tensor_tensor(NR[:, :, :], NM[:, :, h8], NB[:, half, :, 0, :], ALU.subtract), "max_rest")
                    if step == 3:
                        done(dve, "max_rest", count)
                        stage(dve.tensor_copy(NB[:, half, :, 1, :], NR[:, :, :]), "max2")
                    if step == 4:
                        done(dve, "max2", count)
                        stage(dve.tensor_tensor(NB[:, half, :, 2, :], NR[:, :, :], NB[:, half, :, 1, :], ALU.subtract), "max3")

                def sums(b, n, q):
                    dve.wait_ge(S("summed"), (b * HEADS + n + 1) * TILES)
                    dve.wait_ge(S("pads_in"), 16 * EXPERTS * (b + 1))
                    at_least(dve, "raw_psum", b * HEADS + n)
                    stage(dve.tensor_tensor(OT[:, 0:SEQ], PS[:, PV_BANK:PV_BANK + 2, :].rearrange("p a w -> p (a w)")[:, 0:SEQ],
                                            MT[q][:, n, :], ALU.mult), "ot")

                def inner_norm(name, b, slot, at, src, v, gain, bias, dst):
                    k24 = HEADS * TILES
                    s1 = lambda x: S1[:, x, :].rearrange("p (k o) -> p k o", o=1).broadcast_to((P, k24, D))
                    if slot == at:
                        done(dve, f"{name}_in", b + 1)
                        stage(dve.reduce_sum(S1[:, v - 3, :], src, AX.X), f"{name}_sum")
                    if slot == at + 1:
                        done(dve, f"{name}_sum", b + 1)
                        stage(dve.tensor_scalar(S1[:, v - 2, :], S1[:, v - 3, :], 1.0 / D, None, ALU.mult), f"{name}_mean")
                    if slot == at + 2:
                        done(dve, f"{name}_mean", b + 1)
                        stage(dve.tensor_tensor(YC[:, :, :], src, s1(v - 2), ALU.subtract), f"{name}_centred")
                    if slot == at + 4:
                        dve.wait_ge(S(f"{name}_squared"), b + 1)
                        stage(dve.reduce_sum(S1[:, v - 1, :], GL[:, :, :, :].rearrange("p k e g -> p k (e g)"), AX.X), f"{name}_var")
                    if slot == at + 6:
                        dve.wait_ge(S(f"{name}_rstd"), b + 1)
                        stage(dve.tensor_tensor(YC[:, :, :], YC[:, :, :], s1(v + 1), ALU.mult), f"{name}_norm")
                    if slot == at + 7:
                        done(dve, f"{name}_norm", b + 1)
                        stage(dve.tensor_tensor(YC[:, :, :], YC[:, :, :], gain[:, 0:1, :].broadcast_to((P, k24, D)), ALU.mult), f"{name}_gain")
                    if slot == at + 8:
                        done(dve, f"{name}_gain", b + 1)
                        stage(dve.tensor_tensor(dst, YC[:, :, :] if name == "z" else YC[:, :, :].rearrange("p (n t) d -> p n t d", n=HEADS),
                                                bias[:, 0:1, :].broadcast_to((P, k24, D)) if name == "z" else
                                                bias[:, 0:1, :].rearrange("p o (t d) -> p o t d", t=1).broadcast_to((P, HEADS, TILES, D)),
                                                ALU.add), f"{name}_out")

                for slot in range(SLOTS):
                    if M:
                        maximum(it + 1, slot)
                        if SLOTS // 2 <= slot < SLOTS // 2 + 5:
                            split_maxima(it + 1, 0, slot - SLOTS // 2)
                    if C and slot == 0:
                        for step in range(5):
                            split_maxima(it, 1, step)
                    if D1 and slot == OT_AT + 3 * UNITS - SLOTS:
                        sums(it - 1, HEADS - 1, 1 - p)
                    for n in range(HEADS - 1):
                        if C and slot == OT_AT + n * UNITS:
                            sums(it, n, p)
                    if A:
                        b = it + 2
                        h = H[:, bass.ds(b, 1), :, :].rearrange("p o t e -> p (o t) e")
                        s1 = lambda x: S1[:, x, 0:TILES].rearrange("p (t o) -> p t o", o=1).broadcast_to((P, TILES, E))
                        if slot == 1:
                            stage(dve.reduce_sum(S1[:, 0, 0:TILES], h, AX.X), "a_sum")
                        if slot == 2:
                            done(dve, "a_sum", b + 1)
                            stage(dve.tensor_scalar(S1[:, 16, 0:TILES], S1[:, 0, 0:TILES], 1.0 / E, None, ALU.mult), "a_mean")
                        if slot == 3:
                            done(dve, "a_mean", b + 1)
                            stage(dve.tensor_tensor(AC[:, :, :], h, s1(16), ALU.subtract), "a_centred")
                        if slot == 6:
                            dve.wait_ge(S("a_squared"), b + 1)
                            stage(dve.reduce_sum(S1[:, 1, 0:TILES], AS[:, :, :], AX.X), "a_var")
                        if slot == 9:
                            dve.wait_ge(S("a_rstd"), b + 1)
                            stage(dve.tensor_tensor(AN[:, :, :], AC[:, :, :], s1(3), ALU.mult), "a_norm")
                        for idx, at in enumerate(PROJ_AT):
                            if slot == at:
                                half, c = divmod(idx, 2)
                                lo, hi = halves(SEQ)[c]
                                r = P if half < 2 else E
                                top = Q1[:, half, lo:hi] if half < 2 else K1[:, lo:hi]
                                dve.wait_ge(S("q1"), 6 * b + idx + 1)
                                at_least(dve, "q3", 6 * b + idx - 1)
                                stage(dve.tensor_tensor(QR[0:r, lo:hi], PS[0:r, MISC, 0:hi - lo], top, ALU.subtract), "q_rest")
                        for c, at in enumerate(PADS_AT):
                            if slot == at:
                                lo, hi = halves(SEQ)[c]
                                dve.wait_ge(S("pads_psum"), 2 * b + c + 1)
                                at_least(dve, "pads_in", 16 * EXPERTS * b)
                                stage(dve.tensor_scalar(MK[:, lo:hi], PS[0:E, MISC, 0:hi - lo], 0.0, None, ALU.not_equal), "pads")
                    if D1:
                        b = it - 1
                        k24 = HEADS * TILES
                        bc4 = lambda x: S1[:, x, :].rearrange("p (k o) -> p k o", o=1).broadcast_to((P, k24, EXPERTS))
                        if slot == 10:
                            dve.wait_ge(S("raw"), HEADS * (b + 1))
                            stage(dve.reciprocal(RD, RAW[:, :, :, 0:RAWC].rearrange("p n t (e c) -> p (n t) e c", e=EXPERTS)[:, :, :, D]), "den_rec")
                        if slot == 13:
                            dve.wait_ge(S("gate_parts"), b + 1)
                            stage(dve.reduce_sum(LG, GL[:, :, :, :].rearrange("p k e g -> p k g e"), AX.X), "gate_logits")
                        if slot == 14:
                            done(dve, "gate_logits", b + 1)
                            stage(dve.tensor_tensor(LG.rearrange("p (n t) g -> p n t g", n=HEADS), LG.rearrange("p (n t) g -> p n t g", n=HEADS),
                                                    GB[:, :, :].rearrange("p n (t g) -> p n t g", t=1).broadcast_to((P, HEADS, TILES, EXPERTS)),
                                                    ALU.add), "gate_biased")
                        if slot == 15:
                            done(dve, "gate_biased", b + 1)
                            stage(dve.reduce_max(S1[:, 17, :], LG, AX.X), "gate_max")
                        if slot == 17:
                            done(dve, "gate_max", b + 1)
                            stage(dve.tensor_tensor(LG, LG, bc4(17), ALU.subtract), "gate_sub")
                        if slot == 19:
                            dve.wait_ge(S("gate_exp"), b + 1)
                            stage(dve.reduce_sum(S1[:, 18, :], EG, AX.X), "gate_sum")
                        if slot == 20:
                            done(dve, "gate_sum", b + 1)
                            stage(dve.reciprocal(S1[:, 19, :], S1[:, 18, :]), "gate_rec")
                        if slot == 21:
                            stage(dve.tensor_tensor(W4, EG, RD, ALU.mult), "gate_den")
                        if slot == 23:
                            done(dve, "gate_rec", b + 1)
                            done(dve, "gate_den", b + 1)
                            stage(dve.tensor_tensor(W4, W4, bc4(19), ALU.mult), "mix_w")
                        if slot == 30:
                            dve.wait_ge(S("mixed"), HEADS * (b + 1))
                            stage(dve.reduce_sum(Y[:, :, :], MIXP[:, :, :, :].rearrange("p k e d -> p k d e"), AX.X), "mixture")
                        if slot == 31:
                            done(dve, "mixture", b + 1)
                            stage(dve.tensor_tensor(Y[:, :, :], Y[:, :, :], R[:, :, :, :].rearrange("p n t d -> p (n t) d"), ALU.add), "y_in")
                        inner_norm("y", b, slot, 32, Y[:, :, :], 6, LNG, LNB, FX[:, :, :, :].rearrange("p t n d -> p n t d"))
                        if slot == 46:
                            done(dve, "y_out", b + 1)
                            stage(dve.tensor_scalar(FM[:, :, :, :], FX[:, :, :, :], 0.0, None, ALU.not_equal), "fx_mask")
                        for c, at in enumerate(FX_AT):
                            if slot == at:
                                lo, hi = halves(PADDED)[c]
                                dve.wait_ge(S("fxt"), 2 * b + c + 1)
                                stage(dve.tensor_scalar(FMT[:, lo:hi], PS[0:E, MISC, 0:hi - lo], 0.0, None, ALU.not_equal), "fxt_mask")
                        for c, at in enumerate(FC1_AT):
                            if slot == at:
                                lo, hi = halves(PADDED)[c]
                                dve.wait_ge(S("fc1_psum"), 2 * b + c + 1)
                                dve.wait_ge(S("fxt_mask"), 2 * b + c + 1)
                                stage(dve.scalar_tensor_tensor(HXT[0:E, lo:hi], PS[0:E, MISC, 0:hi - lo], 0.0, FMT[:, lo:hi],
                                                               ALU.max, ALU.mult), "hxt")
                        if slot == FC2_AT:
                            dve.wait_ge(S("fc2_psum"), b + 1)
                            done(dve, "fx_mask", b + 1)
                            flat = lambda x: x[:, :, :, :].rearrange("p t n d -> p (t n d)")
                            stage(dve.tensor_tensor(Y[:, :, :].rearrange("p k d -> p (k d)"), PS[:, MISC, 0:TILES * E], flat(FM), ALU.mult), "fc2")
                        if slot == FC2_AT + 2:
                            done(dve, "fc2", b + 1)
                            stage(dve.tensor_tensor(Y[:, :, :], Y[:, :, :], FX[:, :, :, :].rearrange("p t n d -> p (t n) d"), ALU.add), "z_in")
                        inner_norm("z", b, slot, 59, Y[:, :, :], 12, FNG, FNB, FO[:, :, :, :].rearrange("p t n d -> p (t n) d"))
                        bf = lambda x: S1[:, x, 0:TILES].rearrange("p (t o) -> p t o", o=1).broadcast_to((P, TILES, HEADS))
                        if slot == FG_AT:
                            dve.wait_ge(S("fg_psum"), b + 1)
                            stage(dve.tensor_copy(FL, PS[:, MISC, 0:TILES * HEADS].rearrange("p (t n) -> p t n", n=HEADS)), "fg_logits")
                        if slot == FG_AT + 1:
                            done(dve, "fg_logits", b + 1)
                            stage(dve.reduce_max(S1[:, 14, 0:TILES], FL, AX.X), "fg_max")
                        if slot == FG_AT + 3:
                            done(dve, "fg_max", b + 1)
                            stage(dve.tensor_tensor(FL, FL, bf(14), ALU.subtract), "fg_sub")
                        if slot == 80:
                            dve.wait_ge(S("fg_exp"), b + 1)
                            stage(dve.reduce_sum(S1[:, 14, 0:TILES], FE, AX.X), "fg_sum")
                        if slot == 81:
                            done(dve, "fg_sum", b + 1)
                            stage(dve.reciprocal(S1[:, 15, 0:TILES], S1[:, 14, 0:TILES]), "fg_rec")
                        if slot == 82:
                            done(dve, "fg_rec", b + 1)
                            stage(dve.tensor_tensor(FE, FE, bf(15), ALU.mult), "fgate")

            schedule(dve, iteration)

        @block.tensor
        def _(pe):
            pe.wait_ge(S("weights_in"), 16 * WEIGHT_DMAS)
            for k in range(KCHUNKS):
                pe.transpose(PS[:, 0, k * E:(k + 1) * E], TOKW[:, k * P:(k + 1) * P], IDENT[0:E, 0:E])
            turned = ((HL[:, :], 0), (WQN[:, :, :], 64), (WKN[:, :, :], 128), (WVN[:, :, :], 144), (GN[:, :, :], 160),
                      (F1N[:, :, :], 176), (F2N[:, :, :], 192), (FGN[:, :], 208), (WQKV[:, 2 * E:3 * E], 256))
            for w, at in turned:
                k = w.shape[0]
                m = int(np.prod(w.shape[1:]))
                last = pe.transpose(PS[0:m, 1, at:at + k], w, IDENT[0:k, 0:k])
            last.then_inc(S("w_turned"), 1)
            pe.wait_ge(S("w_forms"), 23)
            pe.matmul(PS[0:E + 1, 2, 0:256], HL[:, :], BQ[:, :, :], start=True, stop=True)
            pe.matmul(PS[0:E + 1, 2, 256:384], HL[:, :], BKV[:, :, :, :], start=True, stop=True)
            pe.matmul(PS[0:E + 1, 3, 0:E], WVT[:, :], WOUT[:, :], start=True, stop=True).then_inc(S("w_made"), 1)
            pe.wait_ge(S("w_ready"), 1)
            pe.wait_ge(S("ones_row"), 3)

            PATCH_UNITS = 4 * KCHUNKS

            def turn_patches(g, u):
                chunk, w4 = divmod(u, 4)
                c, half = divmod(chunk, 2)
                if w4 == 0:
                    pe.wait_ge(S("chunk"), g * KCHUNKS + chunk + 1)
                if u >= 4:
                    pe.wait_ge(S("xt_sbuf_act" if u % 2 == 0 else "xt_sbuf_dve"), g * PATCH_UNITS // 2 + (u - 4) // 2 + 1)
                for j in range(4 if w4 < 3 else 2):
                    last = pe.transpose(PS[:, 4 + u % 4, j * ROWS:(j + 1) * ROWS],
                                        XR[:, chunk % 2, 4 * w4 + j, :], IDENT[0:ROWS, 0:ROWS])
                last.then_inc(S("xt_psum"), 1)

            for g in range(BATCH // GROUP):
                at_least(pe, "q4s", g * GROUP)
                AHEAD = 3
                for u in range(AHEAD):
                    turn_patches(g, u)
                for u in range(PATCH_UNITS):
                    if u + AHEAD < PATCH_UNITS:
                        turn_patches(g, u + AHEAD)
                    chunk, w4 = divmod(u, 4)
                    n = (4 if w4 < 3 else 2) * ROWS
                    pe.wait_ge(S("xt_sbuf_act" if u % 2 == 0 else "xt_sbuf_dve"), g * PATCH_UNITS // 2 + u // 2 + 1)
                    mm = pe.matmul(PS[0:E, w4, 0:n], WT[:, chunk, :], XT[:, u % 4, 0:n],
                                   start=(chunk == 0), stop=(chunk == KCHUNKS - 1))
                    mm.then_inc(S("xt_read"), 1)

                for q in range(GROUP // QUAD):
                    i = g * (GROUP // QUAD) + q
                    pe.wait_ge(S("ht"), 4 * (g + 1))
                    at_least(pe, "kvt", i)
                    at_least(pe, "k_len2", i)
                    for b in range(QUAD):
                        pe.transpose(PS[:, 4, b * E:(b + 1) * E], HT[:, q * QUAD + b, 0:P], IDENT[0:E, 0:E])
                        mm = pe.transpose(PS[0:IMG_TAIL, 4, (QUAD + b) * E:(QUAD + b + 1) * E], HT[:, q * QUAD + b, P:PATCHES],
                                          IDENT[0:E, 0:E])
                    mm.then_inc(S("img_tokens"), 1)
                    pe.wait_ge(S("xn"), i + 1)
                    for b in range(QUAD):
                        n = i * QUAD + b
                        at_least(pe, "xnt", n)
                        for t in range(TILES):
                            mm = pe.transpose(PS[0:E, t // 4, (t % 4) * P:(t % 4 + 1) * P], XN[:, b * TILES + t, :], IDENT)
                        mm.then_inc(S("xnt_psum"), 1)
                        pe.wait_ge(S("xnt"), n + 1)
                        at_least(pe, "q2t", n)
                        pe.matmul(PS[0:E, 2, :], WQC[:, :], XNT[:, b, 0:BANK], start=True, stop=True)
                        pe.matmul(PS[0:E, 3, 0:PADDED - BANK], WQC[:, :], XNT[:, b, BANK:PADDED],
                                  start=True, stop=True).then_inc(S("q_psum"), 1)
                        at_least(pe, "h_vo", n)
                        at_least(pe, "q4s", QUAD * i)
                        for t in range(TILES):
                            mm = pe.matmul(PS[:, 5 + t // 2, (t % 2) * 3 * E:(t % 2 + 1) * 3 * E],
                                           XNT[:, b, t * P:(t + 1) * P], WKV[:, :], start=True, stop=True)
                        mm.then_inc(S("kv_psum"), 1)
                    pe.wait_ge(S("img_in_h"), 2 * (i + 1))
                    pe.wait_ge(S("v"), QUAD * (i + 1))
                    pe.wait_ge(S("kn"), i + 1)
                    for b in range(QUAD):
                        for t in range(TILES):
                            r = rows(t)
                            pe.matmul(PS[0:E, 4, b * E:(b + 1) * E], V[0:r, b * TILES + t, :], KN[0:r, b * TILES + t, :],
                                      start=(t == 0), stop=(t == TILES - 1))
                    pe.wait_ge(S("kns"), i + 1)
                    for b in range(QUAD):
                        for t in range(TILES):
                            r = rows(t)
                            mm = pe.matmul(PS[0:E, 4, QUAD * E + b:QUAD * E + b + 1], KNS[0:r, b * TILES + t, :], ONES[0:r, :],
                                           start=(t == 0), stop=(t == TILES - 1))
                    mm.then_inc(S("kvt_psum"), 1)
                    pe.wait_ge(S("kvt"), i + 1)
                    pe.wait_ge(S("h_vo"), QUAD * (i + 1))
                    for b in range(QUAD):
                        mm = pe.matmul(PS[0:E, 5, b * E:(b + 1) * E], KVT[:, b, :], WOUT[:, :], start=True, stop=True)
                    mm.then_inc(S("kvw_psum"), 1)
                    pe.wait_ge(S("kvw"), i + 1)
                    for b in range(QUAD):
                        n = i * QUAD + b
                        pe.wait_ge(S("q4t"), n + 1)
                        if b >= 2:
                            pe.wait_ge(S("q4s"), n - 1)
                        for t in range(TILES):
                            at = t * (E + 2)
                            pe.matmul(PS[:, 6 + b % 2, at:at + E + 1], Q2T[:, b, t * P:(t + 1) * P], KVW[:, b, :],
                                      start=True, stop=True)
                            mm = pe.matmul(PS[:, 6 + b % 2, at + E + 1:at + E + 2], Q4T[:, b, t * P:(t + 1) * P],
                                           ONES[0:E, :], start=True, stop=True)
                        mm.then_inc(S("t2_psum"), 1)
            i = BATCH // QUAD
            pe.wait_ge(S("xn"), i + 1)
            pe.wait_ge(S("h2_done"), i)
            for b in range(HEADS):
                n = BATCH + b
                at_least(pe, "xnt", n)
                for t in range(TILES):
                    mm = pe.transpose(PS[0:E, t // 4, (t % 4) * P:(t % 4 + 1) * P], XN[:, b * TILES + t, :], IDENT)
                mm.then_inc(S("xnt_psum"), 1)
                pe.wait_ge(S("xnt"), n + 1)
                if b > 0:
                    pe.wait_ge(S("resid"), b)
                for t in range(TILES):
                    mm = pe.matmul(PS[:, 2, t * D:(t + 1) * D], XNT[:, b, t * P:(t + 1) * P], HLT[:, b * D:(b + 1) * D],
                                   start=True, stop=True)
                mm.then_inc(S("resid_psum"), 1)

            pe.wait_ge(S("cleared"), CLEARS)

            def iteration(it, p, C, M, A, D1, prev_a, first):
                last_taken = ["raw", HEADS * (it - 1) + HEADS - 1]

                def side_bank(name, count):
                    at_least(pe, last_taken[0], last_taken[1])
                    last_taken[:] = [name, count]

                def side(width):
                    return PS[:, MISC, 0:width]

                def scores(slot):
                    n, u = divmod(slot, UNITS)
                    j, lo, w, e0, ne = UNITS_S[u]
                    r = rows(j)
                    if slot % (SLOTS // 2) == 0:
                        pe.wait_ge(S(f"max_in{n // 2}"), 16 * (it + 1))
                    at_least(pe, "exped", bank_left(it, p, slot))
                    h0 = n * EXPERTS + e0
                    pe.matmul(PS[0:r, score_bank(p, slot), 0:ne * w], KA[p][0:KDIM + MROWS, n, j * P:j * P + r],
                              QA[p][0:KDIM + MROWS, h0:h0 + ne, lo:lo + w], start=True, stop=True).then_inc(S("scores"), 1)

                def max_scores(b, q, slot):
                    n, u = divmod(slot, UNITS)
                    i, lo, w, e0, ne = UNITS_M[u]
                    s0, r = query_tile(i)
                    if slot % (SLOTS // 2) == 0:
                        pe.wait_ge(S(f"q_in{n // 2}"), 16 * PARTS * (b + 1))
                        pe.wait_ge(S(f"k_in{n // 2}"), 16 * PARTS * (b + 1))
                    at_least(pe, "maxed", b * SLOTS + slot - 1)
                    diagonal = lo + w == TAIL + i * P
                    bank = PS[0:r, M_BANKS[slot % 2], 0:ne * w]
                    for e in range(ne):
                        mm = pe.matmul(bank[:, e * w:(e + 1) * w], QA[q][0:KDIM, n * EXPERTS + e0 + e, s0:s0 + r],
                                       KA[q][0:KDIM, n, lo:lo + w], start=(e == 0), stop=(not diagonal and e == ne - 1))
                    if diagonal:
                        mm = pe.matmul(bank.rearrange("p (e w) -> p e w", e=ne)[:, :, w - r:w], IDB[:, 0:r],
                                       MASKB[:, 0:r].rearrange("p (e w) -> p e w", e=1).broadcast_to((P, ne, r)),
                                       start=False, stop=True)
                    mm.then_inc(S("max_scores"), 1)

                def weighted_sums(b, n, j, q):
                    r = rows(j)
                    pe.wait_ge(S("masked"), (b * HEADS + n) * TILES + j + 1)
                    if j == 0:
                        at_least(pe, "ot", b * HEADS + n)
                        if n == 0:
                            pe.wait_ge(S("va"), 2 * b + 2)
                    for bank, lo, hi in ((PV_BANK, j * P, BANK), (PV_BANK + 1, max(BANK, j * P), SEQ)):
                        if lo < hi:
                            lo_b = lo % BANK
                            for e in range(EXPERTS):
                                mm = pe.matmul(PS[32 * e:32 * e + 32, bank, lo_b:lo_b + hi - lo], VA[q][0:r, j, n, :],
                                               PT[j][0:r, e, lo - j * P:hi - j * P], start=(j == 0),
                                               stop=(j == (BANK // P - 1 if bank == PV_BANK else TILES - 1)))
                    mm.then_inc(S("summed"), 1)

                def to_tokens(b, n):
                    side_bank("raw", b * HEADS + n + 1)
                    pe.wait_ge(S("ot"), b * HEADS + n + 1)
                    for t in range(TILES):
                        mm = pe.matmul(side(TILES * SELC)[:, t * SELC:(t + 1) * SELC], OT[:, t * P:(t + 1) * P], SEL[:, n, :],
                                       start=True, stop=True)
                    mm.then_inc(S("raw_psum"), 1)

                def turn_maxima(b, half):
                    side_bank("max_sbuf", 2 * b + half + 1)
                    done(pe, "max3", 2 * b + half + 1)
                    bank = PS[0:24, MISC, 0:SEQ // 2].bitcast(BF16)
                    apart(pe)
                    for i in range(TILES):
                        s0, r = query_tile(i)
                        mm = pe.transpose(bank[:, s0:s0 + r], NB[0:r, half, i, :, :], IDB[0:r, 0:r])
                    mm.then_inc(S("max_psum"), 1)

                def turn(src, t0, t1):
                    for t in range(t0, t1):
                        mm = pe.transpose(side(BANK)[0:E, (t - t0) * P:(t - t0 + 1) * P], src(t), IDENT)
                    return mm

                for slot in range(SLOTS):
                    if C:
                        scores(slot)
                    if M:
                        max_scores(it + 1, 1 - p, slot)
                    for n in range(-1, HEADS):
                        for j in range(TILES):
                            if slot == n * UNITS + LAST_UNIT[j] + PV_LAG:
                                if n >= 0 and C:
                                    weighted_sums(it, n, j, p)
                                if n < 0 and D1:
                                    weighted_sums(it - 1, HEADS - 1, j, 1 - p)
                    if C and slot == MAX1_AT:
                        turn_maxima(it, 1)
                    if M and slot == MAX0_AT:
                        turn_maxima(it + 1, 0)
                    if D1 and slot == SEL_AT + 3 * UNITS - SLOTS:
                        to_tokens(it - 1, HEADS - 1)
                    for n in range(HEADS - 1):
                        if C and slot == SEL_AT + n * UNITS:
                            to_tokens(it, n)
                    if A:
                        b = it + 2
                        for c, at in enumerate(TURN_AT):
                            if slot == at:
                                side_bank("xft", 2 * b + c + 1)
                                done(pe, "a_norm", b + 1)
                                apart(pe)
                                turn(lambda t: AN[:, t, :], *((0, 4), (4, TILES))[c]).then_inc(S("xft_psum"), 1)
                        for idx, at in enumerate(PROJ_AT):
                            if slot == at:
                                half, c = divmod(idx, 2)
                                lo, hi = halves(SEQ)[c]
                                side_bank("q_rest", 6 * b + idx + 1)
                                if idx == 0:
                                    pe.wait_ge(S("xft"), 2 * b + 2)
                                w = WQ[:, half, :] if half < 2 else WK[:, :]
                                pe.matmul(side(hi - lo)[0:w.shape[1]], w, XFT[p][:, lo:hi], start=True, stop=True).then_inc(S("proj"), 1)
                        for c, at in enumerate(PADS_AT):
                            if slot == at:
                                lo, hi = halves(SEQ)[c]
                                side_bank("pads", 2 * b + c + 1)
                                pe.matmul(side(hi - lo)[0:E], HLD[:, :], XFT[p][:, lo:hi], start=True, stop=True).then_inc(S("pads_psum"), 1)
                    if M:
                        for c, at in enumerate(V_AT):
                            if slot == at:
                                b = it + 1
                                t0, t1 = ((0, 4), (4, TILES))[c]
                                side_bank("va", 2 * b + c + 1)
                                for t in range(t0, t1):
                                    mm = pe.matmul(side(BANK)[:, (t - t0) * P:(t - t0 + 1) * P], XFT[1 - p][:, t * P:(t + 1) * P],
                                                   WV[:, :, :], start=True, stop=True)
                                mm.then_inc(S("v_psum"), 1)
                    if D1:
                        b = it - 1
                        for c, at in enumerate(FX_AT):
                            if slot == at:
                                side_bank("fxt_mask", 2 * b + c + 1)
                                done(pe, "y_out", b + 1)
                                apart(pe)
                                turn(lambda t: FX[:, t, :, :], *((0, 4), (4, TILES))[c]).then_inc(S("fxt_psum"), 1)
                        for c, at in enumerate(FC1_AT):
                            if slot == at:
                                lo, hi = halves(PADDED)[c]
                                side_bank("hxt", 2 * b + c + 1)
                                pe.wait_ge(S("fxt"), 2 * b + c + 1)
                                pe.matmul(side(hi - lo)[0:E], F1[:, :, :], FXT[:, lo:hi], start=True, stop=True).then_inc(S("fc1_psum"), 1)
                        if slot == FC2_AT:
                            side_bank("fc2", b + 1)
                            pe.wait_ge(S("hxt"), 2 * b + 2)
                            for t in range(TILES):
                                mm = pe.matmul(side(TILES * E)[:, t * E:(t + 1) * E], HXT[:, t * P:(t + 1) * P], F2[:, :, :],
                                               start=True, stop=True)
                            mm.then_inc(S("fc2_psum"), 1)
                        for c, at in enumerate(FO_AT):
                            if slot == at:
                                side_bank("fot", 2 * b + c + 1)
                                done(pe, "z_out", b + 1)
                                apart(pe)
                                turn(lambda t: FO[:, t, :, :], *((0, 4), (4, TILES))[c]).then_inc(S("fot_psum"), 1)
                        if slot == FG_AT:
                            side_bank("fg_logits", b + 1)
                            pe.wait_ge(S("fot"), 2 * b + 2)
                            for t in range(TILES):
                                mm = pe.matmul(side(TILES * HEADS)[:, t * HEADS:(t + 1) * HEADS], FOT[:, t * P:(t + 1) * P], FGW[:, :],
                                               start=True, stop=True)
                            mm.then_inc(S("fg_psum"), 1)

            schedule(pe, iteration)



def kernel(**inputs):
    import concourse.bacc as _bacc
    from concourse import mybir as _mybir
    from concourse.bass_utils import run_bass_kernel_spmd as _run

    nc = _bacc.Bacc("TRN2", target_bir_lowering=False, num_devices=1)
    nc.disable_value_cache = True
    arrays, aps = {}, {}
    for name, v in list(inputs.items()) + [("const", shape_constants())]:
        v = np.ascontiguousarray(v)
        arrays["in_" + name] = v
        aps[name] = nc.dram_tensor("in_" + name, v.shape, _mybir.dt.from_np(v.dtype), kind="ExternalInput").ap()
    out = nc.dram_tensor("out_0", (BATCH, SEQ, E), _mybir.dt.float32, kind="ExternalOutput").ap()
    build(nc, aps, out)
    result = _run(nc, [arrays], core_ids=[0])
    return result.results[0]["out_0"]
```

```python
import numpy as np
from contextlib import ExitStack

import concourse.bass as bass
from concourse import mybir
from concourse.alu_op_type import AluOpType as ALU

ACT = mybir.ActivationFunctionType
AX = mybir.AxisListType
F32 = mybir.dt.float32
BF16 = mybir.dt.bfloat16
U8 = mybir.dt.uint8

P = 128
BATCH, CHANNELS, IMAGE, PATCH = 16, 3, 224, 16
GRID = IMAGE // PATCH
PATCHES = GRID * GRID
TEXT = 512
E = 64
SEQ = PATCHES + TEXT
TILES = -(-SEQ // P)
TAIL = SEQ - (TILES - 1) * P
PADDED = TILES * P
HEADS, EXPERTS, D = 4, 4, 16
GROUP = BATCH // 2
PAIR = 2
PAIRS = BATCH // PAIR
QUAD = 4
ROWS = GROUP * GRID
KCHUNKS = CHANNELS * PATCH * PATCH // P
IMG_TAIL = PATCHES - P
TXT_HEAD = P - IMG_TAIL
BANK = 512
A_COLS = 452
LN_EPS = 1e-5
DIV_EPS = 1e-7
NORM_EPS = 1e-12
INNER_EPS = 1e-8
MASKED = -1e30

C_IDENT, C_MASK, C_BD, C_BDE, C_SEL = 0, P, 2 * P, 2 * P + 4, 2 * P + 8
RAWC = EXPERTS * (D + 1)
SELC = RAWC + EXPERTS * EXPERTS
C_ALL = C_SEL + RAWC


def shape_constants():
    c = np.zeros((P, C_ALL), np.float32)
    c[:, C_IDENT:C_IDENT + P] = np.eye(P)
    s, t = np.arange(P)[:, None], np.arange(P)[None, :]
    c[:, C_MASK:C_MASK + P] = np.where(t <= s, 0.0, MASKED)
    for r in range(HEADS * D):
        c[r, C_BD + r // D] = 1.0
    for e in range(EXPERTS):
        c[32 * e:32 * e + D, C_BDE + e] = 1.0
        for d in range(D + 1):
            c[32 * e + d, C_SEL + e * (D + 1) + d] = 1.0
    return c


UNITS_S = []
for _j in range(TILES):
    for _lo, _hi in ((_j * P, BANK), (max(BANK, _j * P), SEQ)):
        if _lo < _hi:
            _n = min(EXPERTS, BANK // (_hi - _lo))
            UNITS_S += [(_j, _lo, _hi - _lo, _e, _n) for _e in range(0, EXPERTS, _n)]
UNITS_M = []
for _i in range(TILES):
    _w = TAIL + _i * P
    _cut = _w if _w <= BANK else (_w - P if _w - P <= BANK else BANK)
    for _lo, _hi in ((0, _cut), (_cut, _w)):
        if _lo < _hi:
            _n = min(EXPERTS, BANK // (_hi - _lo))
            UNITS_M += [(_i, _lo, _hi - _lo, _e, _n) for _e in range(0, EXPERTS, _n)]
UNITS = len(UNITS_S)
assert UNITS == len(UNITS_M) == 22
SLOTS = HEADS * UNITS
LAST_UNIT = [max(u for u, x in enumerate(UNITS_S) if x[0] == j) for j in range(TILES)]
Q_PARTS, K_PARTS = (1, 1, 2, 2, 1, 3), (1, 2, 1, 2, 3, 1)
PARTS = len(Q_PARTS)
KDIM = PARTS * D
MROWS = 3
PV_LAG, MASK_LAG, OT_AT, SEL_AT = 6, 2, 28, 34


MAX_STEPS = (
    "max_whole", "max1", "max_rest", "max2", "max3"
)
NORM_STEPS = (
    "a_sum", "a_mean", "a_centred", "a_var", "a_norm"
)
FF_STEPS = (
    "den_rec", "gate_logits", "gate_biased", "gate_max", "gate_sub", "gate_sum", "gate_den", "gate_rec",
    "mix_w", "mixture", "y_in", "y_sum", "y_mean", "y_centred", "y_var", "y_norm", "y_gain", "y_out",
    "fx_mask", "fc2", "z_in", "z_sum", "z_mean", "z_centred", "z_var", "z_norm", "z_gain", "z_out",
    "fg_logits", "fg_max", "fg_sub", "fg_sum", "fg_rec", "fgate"
)
STEPS = {step: (group, steps) for group, steps in (("max_steps", MAX_STEPS), ("norm_steps", NORM_STEPS), ("ff_steps", FF_STEPS))
         for step in steps}


def query_tile(i):
    return (0, TAIL) if i == 0 else (TAIL + (i - 1) * P, P)


def rows(tile):
    return P if tile < TILES - 1 else TAIL


def build(nc, a, out):
    ctx = ExitStack()
    with ctx:
        signals = {}

        def S(name):
            if name not in signals:
                signals[name] = ctx.enter_context(nc.semaphore(name))
            return signals[name]

        def sb(name, shape, dt=F32, stack=ctx):
            return stack.enter_context(nc.sbuf_tensor(name, shape, dt))

        H = sb("H", [P, BATCH, TILES, E])
        CONST = sb("CONST", [P, C_ALL])
        IDENT = CONST[:, C_IDENT:C_IDENT + P]
        BD = CONST[0:HEADS * D, C_BD:C_BD + HEADS]
        BDE = CONST[:, C_BDE:C_BDE + EXPERTS]
        IDB = sb("IDB", [P, P], BF16)
        MASKB = sb("MASKB", [P, P], BF16)
        HLT = sb("HLT", [E + 1, E])
        HLD = sb("HLD", [E + 1, E])
        WQ = sb("WQ", [E + 1, 2, P])
        WK = sb("WK", [E + 1, E])
        WV = sb("WV", [E + 1, HEADS, 32])
        F1 = sb("F1", [E + 1, HEADS, D])
        F2 = sb("F2", [E + 1, HEADS, D])
        FGW = sb("FGW", [E, HEADS])
        SEL = sb("SEL", [P, HEADS, SELC])
        R = sb("R", [P, HEADS, TILES, D])
        GB = sb("GB", [P, HEADS, EXPERTS])
        LNG = sb("LNG", [P, HEADS, D])
        LNB = sb("LNB", [P, HEADS, D])
        FNG = sb("FNG", [P, HEADS, D])
        FNB = sb("FNB", [P, HEADS, D])
        ONES = sb("ONES", [P, 1])
        HALF = sb("HALF", [P, 2 * HEADS * TILES])
        NEG_HALF, POS_HALF = HALF[:, 0:HEADS * TILES], HALF[:, HEADS * TILES:]
        PS = ctx.enter_context(nc.psum_tensor("PS", [P, 8, BANK], F32))

        first = ExitStack()
        WT = sb("WT", [P, KCHUNKS, E], stack=first)
        TOKB = sb("TOKB", [E, 1], stack=first)
        WQKV = sb("WQKV", [E + 1, 3 * E], stack=first)
        WQC = sb("WQC", [E + 1, E], stack=first)
        WKV = sb("WKV", [E + 1, 3 * E], stack=first)
        WOUT = sb("WOUT", [E, E], stack=first)
        BOUT = sb("BOUT", [E + 1, E], stack=first)
        X = sb("X", [ROWS, CHANNELS, PATCH * IMAGE], stack=first)
        XR = sb("XR", [ROWS, 2, GRID, P], stack=first)
        XT = sb("XT", [P, 4, 4 * ROWS], stack=first)
        HT = sb("HT", [E, GROUP, PATCHES], stack=first)
        XC = sb("XC", [P, PAIR * TILES, E], stack=first)
        SQ = sb("SQ", [P, PAIR * TILES, E], stack=first)
        XN = sb("XN", [P, 2, PAIR * TILES, E], stack=first)
        K2 = sb("K2", [P, PAIR * TILES, E], stack=first)
        V = sb("V", [P, 2, PAIR * TILES, E], stack=first)
        KN = sb("KN", [P, 2, PAIR * TILES, E], stack=first)
        KNS = sb("KNS", [P, 2, PAIR * TILES, E], stack=first)
        TMP = sb("TMP", [P, PAIR * TILES, E], stack=first)
        XNT = sb("XNT", [E + 1, PAIR, PADDED], stack=first)
        Q2T = sb("Q2T", [E, 2, PAIR, PADDED], stack=first)
        Q4T = sb("Q4T", [E, 2, PAIR, PADDED], stack=first)
        KVT = sb("KVT", [E, PAIR, E], stack=first)
        KVW = sb("KVW", [E, PAIR, E + 1], stack=first)
        ST = sb("ST", [P, 12, PAIR * TILES], stack=first)
        (MEAN, VAR, VARE, RSTD, K2S, RK, Q2S, Q4S, RQ, NQ, NQ2, FQ) = (ST[:, n, :] for n in range(12))
        SN = sb("SN", [E, 4, PAIR], stack=first)
        TOKW = sb("TOKW", [E, KCHUNKS * P], stack=first)
        HL = sb("HL", [HEADS * D, E + 1], stack=first)
        WQN = sb("WQN", [EXPERTS * D, HEADS, D], stack=first)
        WKN = sb("WKN", [D, HEADS, D], stack=first)
        WVN = sb("WVN", [D, HEADS, D], stack=first)
        GN = sb("GN", [HEADS * EXPERTS, EXPERTS, 32], stack=first)
        F1N = sb("F1N", [D, HEADS, D], stack=first)
        F2N = sb("F2N", [D, HEADS, D], stack=first)
        FGN = sb("FGN", [HEADS, E], stack=first)
        BQ = sb("BQ", [HEADS * D, HEADS, EXPERTS * D], stack=first)
        BKV = sb("BKV", [HEADS * D, 2, HEADS, D], stack=first)
        WVT = sb("WVT", [E, E + 1], stack=first)
        CM = sb("CM", [E + 1, 2, 1], stack=first)
        first.close()

        QA = [sb(f"QA{p}", [P, HEADS * EXPERTS, SEQ], BF16) for p in range(2)]
        KA = [sb(f"KA{p}", [P, HEADS, SEQ], BF16) for p in range(2)]
        PT = [sb(f"PT{j}", [P, EXPERTS, SEQ - j * P]) for j in range(TILES)]
        MT = [sb(f"MT{p}", [P, HEADS, SEQ], U8) for p in range(2)]
        VA = [sb(f"VA{p}", [P, TILES, HEADS, 32]) for p in range(2)]
        XFT = [sb(f"XFT{p}", [E + 1, PADDED]) for p in range(2)]
        Q1 = sb("Q1", [P, 2, SEQ], BF16)
        Q2 = sb("Q2", [P, 2, SEQ], BF16)
        Q3 = sb("Q3", [P, 2, SEQ], BF16)
        QR = sb("QR", [P, SEQ])
        K1 = sb("K1", [E, SEQ], BF16)
        K2B = sb("K2B", [E, SEQ], BF16)
        K3 = sb("K3", [E, SEQ], BF16)
        MK = sb("MK", [E, SEQ], U8)
        OT = sb("OT", [P, PADDED])
        RAW = sb("RAW", [P, HEADS, TILES, SELC])
        NM = sb("NM", [P, TILES, HEADS * EXPERTS])
        NP = sb("NP", [P, 2, HEADS * EXPERTS])
        NR = sb("NR", [P, TILES, 8])
        NB = sb("NB", [P, 2, TILES, 3, 8], BF16)
        NT = [sb(f"NT{h}", [24, SEQ], BF16) for h in range(2)]
        AC = sb("AC", [P, TILES, E])
        AS = sb("AS", [P, TILES, E])
        AN = sb("AN", [P, TILES, E])
        GL = sb("GL", [P, HEADS * TILES, EXPERTS, EXPERTS])
        MIXP = sb("MIXP", [P, HEADS * TILES, EXPERTS, D])
        Y = sb("Y", [P, HEADS * TILES, D])
        YC = sb("YC", [P, HEADS * TILES, D])
        FX = sb("FX", [P, TILES, HEADS, D])
        FM = sb("FM", [P, TILES, HEADS, D], BF16)
        FO = sb("FO", [P, TILES, HEADS, D])
        OUT = sb("OUT", [P, TILES, E])
        FXT = sb("FXT", [E + 1, PADDED])
        FMT = sb("FMT", [E, PADDED], BF16)
        HXT = sb("HXT", [E + 1, PADDED])
        FOT = FXT[0:E, :]
        S4 = sb("S4", [P, 6, HEADS * TILES, EXPERTS])
        RD, LG, EG, W4 = (S4[:, n, :, :] for n in range(4))
        FL, FE = (S4[:, n, 0:TILES, :] for n in (4, 5))
        S1 = sb("S1", [P, 20, HEADS * TILES])

        def it_static(it):
            return it if isinstance(it, int) else None

        def schedule(eng, iteration):
            def run(it, p):
                t = it_static(it)
                known = t is not None
                iteration(it, p,
                          C=not known or 0 <= t < BATCH,
                          M=not known or 0 <= t + 1 < BATCH,
                          A=not known or 0 <= t + 2 < BATCH,
                          D1=not known or 0 <= t - 1 < BATCH,
                          prev_a=not known or 0 <= t + 1 < BATCH,
                          first=known and t < 1)
            for it in (-2, -1, 0, 1):
                run(it, it % 2)
            with eng.Fori(1, BATCH // 2 - 1) as k:
                run(k * 2, 0)
                run(k * 2 + 1, 1)
            for it in (BATCH - 2, BATCH - 1, BATCH):
                run(it, it % 2)

        WEIGHT_DMAS = 26

        def apart(eng):
            eng.sem_inc(S("apart"), 1)

        def done(eng, step, times):
            group, steps = STEPS[step]
            eng.wait_ge(S(group), (times - 1) * len(steps) + steps.index(step) + 1)

        def at_least(eng, name, value):
            if isinstance(value, int) and value <= 0:
                return
            if name in STEPS:
                done(eng, name, value)
            else:
                eng.wait_ge(S(name), value)

        def halves(width):
            return ((0, BANK), (BANK, width))

        S_BANKS, M_BANKS, PV_BANK, MISC = (0, 1), (2, 3, 4), 5, 7

        def ring_bank(banks, p, slot):
            return banks[(slot + (p if SLOTS % len(banks) else 0)) % len(banks)]

        def bank_left(banks, it, p, slot):
            ring = len(banks)
            if slot >= ring:
                return it * SLOTS + slot - ring + 1
            last = max(x for x in range(SLOTS) if ring_bank(banks, 1 - p, x) == ring_bank(banks, p, slot))
            return (it - 1) * SLOTS + last + 1

        def first_out(it):
            return isinstance(it, int) and it == 1

        PROJ_AT = (19, 22, 25, 28, 31, 36)
        PADS_AT, V_AT, TURN_AT = (39, 42), (7, 9), (15, 17)
        DEN_AT, Y_AT = 14, 34
        FX_AT, FC1_AT, FC2_AT, Z_AT = (47, 49), (51, 54), 58, 61
        FO_AT, FG_AT = (74, 76), 81
        MAX0_AT, MAX1_AT = 62, 4
        CLEARS = 10
        RESID_AT = 18

        def known_first_heads(b):
            return isinstance(b, int) and b < HEADS

        def txt_parts(g):
            yield 1, IMG_TAIL, 0, TXT_HEAD
            for t in range(2, TILES):
                yield t, 0, TXT_HEAD + (t - 2) * P, rows(t)

        block = ctx.enter_context(nc.Block())

        @block.sync
        def _(sp):
            n = 0

            def weight(dst, src):
                sp.dma_start(dst, src).then_inc(S("weights_in"), 16)
                return 1

            sp.wait_ge(S("weights_cleared"), 6)
            n += weight(CONST[:, :], a["const"])
            n += weight(TOKW[:, :], a["L0_tok_W"])
            n += weight(TOKB[:, :], a["L0_tok_b"].rearrange("(e o) -> e o", o=1))
            n += weight(WQKV[0:E, :], a["L0_attn_W_qkv"])
            n += weight(WQKV[E:E + 1, :], a["L0_attn_b_qkv"].rearrange("(o n) -> o n", o=1))
            n += weight(WOUT[:, :], a["L0_attn_W_out"])
            n += weight(BOUT[E:E + 1, :], a["L0_attn_b_out"].rearrange("(o n) -> o n", o=1))
            n += weight(HL[:, 0:E], a["L0_ffn_hl_w"].rearrange("n d h -> (n d) h"))
            n += weight(HL[:, E:E + 1], a["L0_ffn_hl_b"].rearrange("n (d o) -> (n d) o", o=1))
            n += weight(WQN[:, :, :], a["L0_ffn_wq"].rearrange("n e o d -> (e o) n d"))
            n += weight(WKN[:, :, :], a["L0_ffn_wk"].rearrange("n o d -> o n d"))
            n += weight(WVN[:, :, :], a["L0_ffn_wv"].rearrange("n o d -> o n d"))
            for e in range(EXPERTS):
                n += weight(GN[:, e, 0:D], a["L0_ffn_gate_w"].rearrange("n g (e d) -> (n g) e d", d=D)[:, e, :])
            for dst, name in ((F1, "fc1"), (F2, "fc2")):
                n += weight((F1N if dst is F1 else F2N)[:, :, :],
                            a[f"L0_ffn_{name}_w"].rearrange("o (n d) -> o n d", n=1).broadcast_to((D, HEADS, D)))
                n += weight(dst[E:E + 1, :, :],
                            a[f"L0_ffn_{name}_b"].rearrange("(a n d) -> a n d", a=1, n=1).broadcast_to((1, HEADS, D)))
            n += weight(FGN[:, :], a["L0_ffn_fgate_w"])
            n += weight(GB[:, :, :], a["L0_ffn_gate_b"].rearrange("(a n) e -> a n e", a=1).broadcast_to((P, HEADS, EXPERTS)))
            for dst, name in ((LNG, "ln_g"), (LNB, "ln_b"), (FNG, "fnorm_g"), (FNB, "fnorm_b")):
                n += weight(dst[:, :, :],
                            a[f"L0_ffn_{name}"].rearrange("(a n d) -> a n d", a=1, n=1).broadcast_to((P, HEADS, D)))
            assert n == WEIGHT_DMAS, n
            for g in range(BATCH // GROUP):
                for c in range(CHANNELS):
                    if g > 0:
                        sp.wait_ge(S("chunk"), (g - 1) * KCHUNKS + 2 * c + 2)
                    for b in range(GROUP):
                        sp.dma_start(X[b * GRID:(b + 1) * GRID, c, :],
                                     a["x"][g * GROUP + b, c, :, :].rearrange("(h p) w -> h (p w)", p=PATCH)
                                     ).then_inc(S(f"x_in{c}"), 16)
            def parts_in(b, p, half, first):
                h8, n2 = half * 8, half * 2
                sp.wait_ge(S("q3"), 6 * b + 2 * half + 2)
                if not first:
                    sp.wait_ge(S("scores"), (b - 2) * SLOTS + (half + 1) * SLOTS // 2)
                for r, (x, y) in enumerate(zip(Q_PARTS, K_PARTS)):
                    sp.dma_start(QA[p][r * D:(r + 1) * D, h8:h8 + 8, :], (Q1, Q2, Q3)[x - 1][:, half, :]
                                 ).then_inc(S(f"q_in{half}"), 16)
                sp.wait_ge(S("q3"), 6 * b + 6)
                for r, (x, y) in enumerate(zip(Q_PARTS, K_PARTS)):
                    sp.dma_start(KA[p][r * D:(r + 1) * D, n2:n2 + 2, :], (K1, K2B, K3)[y - 1][half * 32:half * 32 + 32, :]
                                 ).then_inc(S(f"k_in{half}"), 16)

            def max_in(b, p, half):
                sp.wait_ge(S("max_sbuf"), 2 * b + half + 1)
                sp.dma_start(QA[p][KDIM:KDIM + MROWS, half * 8:half * 8 + 8, :], NT[half][:, :]).then_inc(S(f"max_in{half}"), 16)

            def iteration(it, p, C, M, A, D1, prev_a, first):
                if prev_a:
                    parts_in(it + 1, 1 - p, 1, first)
                if C:
                    max_in(it, p, 1)
                if prev_a:
                    sp.wait_ge(S("pads"), 2 * (it + 1) + 2)
                    if not first:
                        sp.wait_ge(S("ot"), HEADS * it)
                    for e in range(EXPERTS):
                        sp.dma_start(MT[1 - p][32 * e:32 * e + D, :, :], MK[:, :]).then_inc(S("pads_in"), 16)
                if A:
                    parts_in(it + 2, p, 0, it_static(it) in (-2, -1))
                if M:
                    max_in(it + 1, 1 - p, 0)
                if D1:
                    sp.wait_ge(S("out_made"), it)
                    b = it - 1
                    o = out[bass.ds(b, 1), :, :] if not isinstance(b, int) else out[b:b + 1, :, :]
                    sp.dma_start(o[:, 0:SEQ - TAIL, :].rearrange("o (t p) e -> p (o t) e", p=P), OUT[:, 0:TILES - 1, :]
                                 ).then_inc(S("out_dma"), 16)
                    sp.dma_start(o[:, SEQ - TAIL:SEQ, :].rearrange("o p e -> (o p) e"), OUT[0:TAIL, TILES - 1, :]
                                 ).then_inc(S("out_dma"), 16)

            schedule(sp, iteration)
            sp.wait_ge(S("out_dma"), 32 * BATCH)

        @block.gpsimd
        def _(pool):
            for n, (dst, value, name) in enumerate((
                    (GN[:, :, :], 0.0, "weights_cleared"), (BOUT[:, :], 0.0, "weights_cleared"), (WV[:, :, :], 0.0, "weights_cleared"),
                    (NEG_HALF, -0.5, "weights_cleared"), (POS_HALF, 0.5, "weights_cleared"), (ONES[:, :], 1.0, "weights_cleared"))):
                pool.memset(dst, value).then_inc(S(name), 1)
                pool.wait_ge(S(name), n + 1)
            pool.memset(H[:, :, TILES - 1, :], 0.0).then_inc(S("tail_cleared"), 1)
            pool.wait_ge(S("tail_cleared"), 1)
            for n, (dst, value) in enumerate(((XNT[E:E + 1, :, :], 1.0), (KVW[:, :, E:E + 1], 1.0), (ST[:, :, :], 0.0))):
                pool.memset(dst, value).then_inc(S("ones_row"), 1)
                pool.wait_ge(S("ones_row"), n + 1)

            for step in range(-1, PAIRS + 1):
                norm, back = step + 1, step - 1
                if 0 <= back < PAIRS:
                    pool.wait_ge(S("k_len2"), back + 1)
                    pool.tensor_tensor(SN[:, 1, :], SN[:, 0, :], POS_HALF[0:E, 0:PAIR], ALU.pow).then_inc(S("k_len"), 1)
                    pool.wait_ge(S("k_len"), back + 1)
                if norm < PAIRS:
                    pool.wait_ge(S("var"), norm + 1)
                    pool.tensor_scalar(VARE, VAR, 1.0 / E, LN_EPS, ALU.mult, ALU.add).then_inc(S("var_eps"), 1)
                    pool.wait_ge(S("var_eps"), norm + 1)
                    pool.tensor_tensor(RSTD, VARE, NEG_HALF[:, 0:PAIR * TILES], ALU.pow).then_inc(S("rstd"), 1)
                if 0 <= back < PAIRS:
                    pool.wait_ge(S("q4s"), PAIR * (back + 1))
                    pool.tensor_tensor(NQ, Q4S, POS_HALF[:, 0:PAIR * TILES], ALU.pow).then_inc(S("q_len"), 1)

            pool.wait_ge(S("h2_done"), PAIRS)
            clears = [(MT[0][:, :, :], 1), (MT[1][:, :, :], 1), (OT[:, :], 1.0), (NM[:, :, :], 0.0),
                      (KA[0][KDIM:KDIM + MROWS, :, :], 1.0), (KA[1][KDIM:KDIM + MROWS, :, :], 1.0),
                      (XFT[0][E:E + 1, :], 1.0), (XFT[1][E:E + 1, :], 1.0), (FXT[E:E + 1, :], 1.0), (HXT[E:E + 1, :], 1.0)]
            for n, (dst, value) in enumerate(clears):
                pool.memset(dst, value).then_inc(S("cleared"), 1)
                pool.wait_ge(S("cleared"), n + 1)
            assert len(clears) == CLEARS

            def iteration(it, p, C, M, A, D1, prev_a, first):
                def mask(b, n, j):
                    r = rows(j)
                    units = [u for u, x in enumerate(UNITS_S) if x[0] == j and x[1] == j * P]
                    pool.wait_ge(S("exped"), b * SLOTS + n * UNITS + max(units) + 1)
                    apart(pool)
                    pool.affine_select(out=PT[j][0:r, :, 0:r], in_=PT[j][0:r, :, 0:r], pattern=[[0, EXPERTS], [1, r]],
                                       compare_op=ALU.is_ge, fill=0.0, base=0, channel_multiplier=-1
                                       ).then_inc(S("masked"), 1)

                for slot in range(SLOTS):
                    for n in range(-1, HEADS):
                        for j in range(TILES):
                            if slot == n * UNITS + LAST_UNIT[j] + MASK_LAG:
                                if n >= 0 and C:
                                    mask(it, n, j)
                                if n < 0 and D1:
                                    mask(it - 1, HEADS - 1, j)
                    if A:
                        b = it + 2
                        if slot == 8:
                            done(pool, "a_var", b + 1)
                            apart(pool)
                            pool.tensor_scalar(S1[:, 2, 0:TILES], S1[:, 1, 0:TILES], 1.0 / E, LN_EPS, ALU.mult, ALU.add
                                               ).then_inc(S("a_eps"), 1)
                            pool.wait_ge(S("a_eps"), b + 1)
                            pool.tensor_tensor(S1[:, 3, 0:TILES], S1[:, 2, 0:TILES], NEG_HALF[:, 0:TILES], ALU.pow
                                               ).then_inc(S("a_rstd"), 1)
                        for idx, at in enumerate(PROJ_AT):
                            if slot == at + 3:
                                half, c = divmod(idx, 2)
                                lo, hi = halves(SEQ)[c]
                                if half < 2:
                                    src, mid, low = QR[:, lo:hi], Q2[:, half, lo:hi], Q3[:, half, lo:hi]
                                else:
                                    src, mid, low = QR[0:E, lo:hi], K2B[:, lo:hi], K3[:, lo:hi]
                                pool.wait_ge(S("q_rest"), 6 * b + idx + 1)
                                apart(pool)
                                pool.tensor_scalar(mid, src, 1.0, 0.0, ALU.mult, ALU.add).then_inc(S("q2"), 1)
                                pool.wait_ge(S("q2"), 6 * b + idx + 1)
                                pool.tensor_tensor(low, src, mid, ALU.subtract).then_inc(S("q3"), 1)
                                if half == 2:
                                    pool.wait_ge(S("q3"), 6 * b + idx + 1)
                    if D1:
                        b = it - 1
                        if slot == DEN_AT + 1:
                            pool.wait_ge(S("raw"), HEADS * (b + 1))
                            done(pool, "den_rec", b + 1)
                            pool.tensor_tensor(GL[:, :, :, :], RAW[:, :, :, RAWC:SELC].rearrange("p n t (e g) -> p (n t) e g", e=EXPERTS),
                                               RD.rearrange("p k (e o) -> p k e o", o=1).broadcast_to((P, HEADS * TILES, EXPERTS, EXPERTS)),
                                               ALU.mult).then_inc(S("gate_parts"), 1)
                        for n in range(HEADS):
                            if slot == 26 + n:
                                done(pool, "mix_w", b + 1)
                                k6 = slice(n * TILES, (n + 1) * TILES)
                                pool.tensor_tensor(MIXP[:, k6, :, :],
                                                   RAW[:, n, :, 0:RAWC].rearrange("p t (e c) -> p t e c", e=EXPERTS)[:, :, :, 0:D],
                                                   W4[:, k6, :].rearrange("p k (e o) -> p k e o", o=1).broadcast_to((P, TILES, EXPERTS, D)),
                                                   ALU.mult).then_inc(S("mixed"), 1)
                        for name, at, v in (("y", Y_AT + 5, 6), ("z", Z_AT + 5, 12)):
                            if slot == at:
                                done(pool, f"{name}_var", b + 1)
                                apart(pool)
                                pool.tensor_scalar(S1[:, v, :], S1[:, v - 1, :], 1.0 / D, INNER_EPS, ALU.mult, ALU.add
                                                   ).then_inc(S(f"{name}_eps"), 1)
                                pool.wait_ge(S(f"{name}_eps"), b + 1)
                                pool.tensor_tensor(S1[:, v + 1, :], S1[:, v, :], NEG_HALF, ALU.pow).then_inc(S(f"{name}_rstd"), 1)
                        if slot == SLOTS - 1:
                            done(pool, "fgate", b + 1)
                            if not first_out(it):
                                pool.wait_ge(S("out_dma"), 32 * b)
                            pool.tensor_tensor(OUT[:, :, :].rearrange("p t (n d) -> p (t n) d", n=HEADS),
                                               FO[:, :, :, :].rearrange("p t n d -> p (t n) d"),
                                               FE.rearrange("p t (n o) -> p (t n) o", o=1).broadcast_to((P, HEADS * TILES, D)),
                                               ALU.mult).then_inc(S("out_gated"), 1)
                            pool.wait_ge(S("out_gated"), b + 1)
                            pool.tensor_tensor(OUT[:, :, :], OUT[:, :, :], H[:, bass.ds(b, 1), :, :].rearrange("p o t e -> p (o t) e"),
                                               ALU.add).then_inc(S("out_made"), 1)

            schedule(pool, iteration)

        @block.scalar
        def _(act):
            act.wait_ge(S("tail_cleared"), 1)
            for g in range(BATCH // GROUP):
                for t, p0, tok, n in txt_parts(g):
                    act.dma_start(H[p0:p0 + n, g * GROUP:(g + 1) * GROUP, t, :],
                                  a["txt"][g * GROUP:(g + 1) * GROUP, tok:tok + n, :].rearrange("b p e -> p b e")
                                  ).then_inc(S(f"txt_in{g}"), 16)

            for g in range(BATCH // GROUP):
                for u in range(0, 4 * KCHUNKS, 2):
                    act.wait_ge(S("xt_psum"), g * 4 * KCHUNKS + u + 1)
                    if u >= 4:
                        act.wait_ge(S("xt_read"), g * 4 * KCHUNKS + u - 4 + 1)
                    act.copy(XT[:, u % 4, :], PS[:, 4 + u % 4, 0:4 * ROWS]).then_inc(S("xt_sbuf_act"), 1)
                act.wait_ge(S("xt_read"), (g + 1) * 4 * KCHUNKS)
                for w in range(2):
                    act.activation(HT[:, :, :].rearrange("e b (h w) -> e w (b h)", w=GRID)[:, 4 * w:4 * w + 4, :],
                                   PS[0:E, w, 0:4 * ROWS].rearrange("e (w r) -> e w r", w=4),
                                   ACT.Identity, bias=TOKB[:, 0:1]).then_inc(S("ht"), 1)
                for q in range(GROUP // QUAD):
                    b0 = g * GROUP + q * QUAD
                    act.wait_ge(S("img_tokens"), g * (GROUP // QUAD) + q + 1)
                    act.copy(H[:, b0:b0 + QUAD, 0, :], PS[:, 6 + q, 0:QUAD * E].rearrange("p (b e) -> p b e", b=QUAD)
                             ).then_inc(S("img_in_h"), 1)
                    act.copy(H[0:IMG_TAIL, b0:b0 + QUAD, 1, :],
                             PS[0:IMG_TAIL, 6 + q, QUAD * E:2 * QUAD * E].rearrange("p (b e) -> p b e", b=QUAD)
                             ).then_inc(S("img_in_h"), 1)

            def two_banks(bank):
                return PS[0:E, bank:bank + 2, :].rearrange("e a n -> e (a n)")[:, 0:PADDED]

            for step in range(-1, PAIRS + 1):
                norm, mid, back = step + 1, step, step - 1
                q = step % 2
                if 0 <= back < PAIRS:
                    act.wait_ge(S("kvt_psum"), back + 1)
                    act.copy(KVT[:, :, :], PS[0:E, 7, 0:PAIR * E].rearrange("p (b e) -> p b e", b=PAIR)).then_inc(S("kvt"), 1)
                for b in range(PAIR):
                    if 0 <= mid < PAIRS:
                        n = mid * PAIR + b
                        act.wait_ge(S("xnt_psum"), n + 1)
                        at_least(act, "kv_psum", n - PAIR + 1)
                        act.copy(XNT[0:E, b, :], two_banks(0)).then_inc(S("xnt"), 1)
                    if b == 0 and norm < PAIRS:
                        act.wait_ge(S("centred"), norm + 1)
                        act.activation(SQ[:, :, :], XC[:, :, :], ACT.Square).then_inc(S("squared"), 1)
                    if 0 <= mid < PAIRS:
                        at_least(act, "t2_psum", n - 2 * PAIR + 1)
                        act.wait_ge(S("q_psum"), n + 1)
                        act.activation(Q2T[:, q, b, :], two_banks(2), ACT.Square).then_inc(S("q2t"), 1)
                        at_least(act, "kn", mid)
                        at_least(act, "kvt_psum", mid - 1)
                        act.wait_ge(S("kv_psum"), n + 1)
                        act.activation(K2[:, b * TILES:(b + 1) * TILES, :].rearrange("p (a t) e -> p a t e", a=3),
                                       PS[:, 4:7, 0:6 * E].rearrange("p a (t n) -> p a t n", t=2)[:, :, :, 0:E],
                                       ACT.Square).then_inc(S("k2"), 1)
                        act.copy(V[:, q, b * TILES:(b + 1) * TILES, :].rearrange("p (a t) e -> p a t e", a=3),
                                 PS[:, 4:7, 0:6 * E].rearrange("p a (t n) -> p a t n", t=2)[:, :, :, E:2 * E]
                                 ).then_inc(S("v"), 1)
                        act.wait_ge(S("q2t"), n + 1)
                        act.activation(Q4T[:, q, b, :], Q2T[:, q, b, :], ACT.Square).then_inc(S("q4t"), 1)
                if 0 <= mid < PAIRS:
                    act.wait_ge(S("kn"), mid + 1)
                    act.activation(KNS[:, q, :, :], KN[:, q, :, :], ACT.Square).then_inc(S("kns"), 1)

            act.wait_ge(S("cleared"), CLEARS)

            def iteration(it, p, C, M, A, D1, prev_a, first):
                def exponentials(slot):
                    n, u = divmod(slot, UNITS)
                    j, lo, w, e0, ne = UNITS_S[u]
                    count = it * SLOTS + slot
                    r = rows(j)
                    act.wait_ge(S("scores"), count + 1)
                    if UNITS_S[u - 1][0] != j or u == 0:
                        at_least(act, "summed", (it * HEADS + n - 1) * TILES + j + 1)
                    act.activation(PT[j][0:r, e0:e0 + ne, lo - j * P:lo - j * P + w],
                                   PS[0:r, ring_bank(S_BANKS, p, slot), 0:ne * w].rearrange("p (e w) -> p e w", e=ne),
                                   ACT.Exp).then_inc(S("exped"), 1)

                def raw(b, n):
                    act.wait_ge(S("raw_psum"), b * HEADS + n + 1)
                    if n == 0:
                        at_least(act, "mixed", HEADS * b)
                    act.copy(RAW[:, n, :, :], PS[:, 7, 0:TILES * SELC].rearrange("p (t c) -> p t c", t=TILES)).then_inc(S("raw"), 1)

                def maxima(b, half):
                    act.wait_ge(S("max_psum"), 2 * b + half + 1)
                    at_least(act, f"max_in{half}", 16 * b)
                    act.copy(NT[half][:, :], PS[0:24, 7, 0:SEQ // 2].bitcast(BF16)).then_inc(S("max_sbuf"), 1)

                for slot in range(SLOTS):
                    if C:
                        exponentials(slot)
                    if slot == MAX1_AT and C:
                        maxima(it, 1)
                    if slot == MAX0_AT and M:
                        maxima(it + 1, 0)
                    if D1 and slot == SEL_AT + 3 * UNITS - SLOTS:
                        raw(it - 1, HEADS - 1)
                    for n in range(HEADS - 1):
                        if C and slot == SEL_AT + n * UNITS:
                            raw(it, n)
                    if A:
                        b = it + 2
                        if slot == 4:
                            done(act, "a_centred", b + 1)
                            act.activation(AS[:, :, :], AC[:, :, :], ACT.Square).then_inc(S("a_squared"), 1)
                        for c, at in enumerate(TURN_AT):
                            if slot == at:
                                lo, hi = halves(PADDED)[c]
                                act.wait_ge(S("xft_psum"), 2 * b + c + 1)
                                act.copy(XFT[p][0:E, lo:hi], PS[0:E, 7, 0:hi - lo]).then_inc(S("xft"), 1)
                        if slot == RESID_AT and known_first_heads(b):
                            act.wait_ge(S("resid_psum"), b + 1)
                            act.copy(R[:, b, :, :], PS[:, MISC, 0:TILES * D].rearrange("p (t d) -> p t d", t=TILES)).then_inc(S("resid"), 1)
                        for idx, at in enumerate(PROJ_AT):
                            if slot == at:
                                half, c = divmod(idx, 2)
                                lo, hi = halves(SEQ)[c]
                                r = P if half < 2 else E
                                act.wait_ge(S("proj"), 6 * b + idx + 1)
                                at_least(act, "q3", 6 * b + idx - 1)
                                act.copy(QR[0:r, lo:hi], PS[0:r, MISC, 0:hi - lo]).then_inc(S("q_out"), 1)
                            if slot == at + 1:
                                half, c = divmod(idx, 2)
                                lo, hi = halves(SEQ)[c]
                                if c == 0 and half < 2:
                                    at_least(act, f"q_in{half}", 16 * PARTS * b)
                                if c == 0 and half == 2:
                                    at_least(act, "k_in0", 16 * PARTS * b)
                                    at_least(act, "k_in1", 16 * PARTS * b)
                                dst, src = (Q1[:, half, lo:hi], QR[:, lo:hi]) if half < 2 else (K1[:, lo:hi], QR[0:E, lo:hi])
                                act.wait_ge(S("q_out"), 6 * b + idx + 1)
                                act.copy(dst, src).then_inc(S("q1"), 1)
                    if M:
                        for c, at in enumerate(V_AT):
                            if slot == at:
                                b = it + 1
                                t0, t1 = ((0, 4), (4, TILES))[c]
                                act.wait_ge(S("v_psum"), 2 * b + c + 1)
                                act.copy(VA[1 - p][:, t0:t1, :, :],
                                         PS[:, 7, 0:(t1 - t0) * P].rearrange("p (t n c) -> p t n c", t=t1 - t0, n=HEADS)
                                         ).then_inc(S("va"), 1)
                    if D1:
                        b = it - 1
                        if slot == 21:
                            done(act, "gate_sub", b + 1)
                            act.activation(EG, LG, ACT.Exp).then_inc(S("gate_exp"), 1)
                        for name, at in (("y", Y_AT + 3), ("z", Z_AT + 3)):
                            if slot == at:
                                done(act, f"{name}_centred", b + 1)
                                act.activation(GL[:, :, :, :].rearrange("p k e g -> p k (e g)"), YC[:, :, :], ACT.Square
                                               ).then_inc(S(f"{name}_squared"), 1)
                        for c, at in enumerate(FX_AT):
                            if slot == at:
                                lo, hi = halves(PADDED)[c]
                                act.wait_ge(S("fxt_psum"), 2 * b + c + 1)
                                act.copy(FXT[0:E, lo:hi], PS[0:E, 7, 0:hi - lo]).then_inc(S("fxt"), 1)
                        for c, at in enumerate(FO_AT):
                            if slot == at:
                                lo, hi = halves(PADDED)[c]
                                act.wait_ge(S("fot_psum"), 2 * b + c + 1)
                                act.copy(FOT[:, lo:hi], PS[0:E, 7, 0:hi - lo]).then_inc(S("fot"), 1)
                        if slot == 84:
                            done(act, "fg_sub", b + 1)
                            act.activation(FE, FL, ACT.Exp).then_inc(S("fg_exp"), 1)

            schedule(act, iteration)

        @block.vector
        def _(dve):
            def stage(ins, name):
                ins.then_inc(S(STEPS[name][0] if name in STEPS else name), 1)

            dve.wait_ge(S("weights_in"), 16 * WEIGHT_DMAS)
            dve.tensor_copy(IDB[:, :], IDENT).then_inc(S("w_forms"), 1)
            dve.tensor_copy(MASKB[:, :], CONST[:, C_MASK:C_MASK + P]).then_inc(S("w_forms"), 1)
            dve.reduce_sum(CM[:, :, 0], WQKV[:, 0:2 * E].rearrange("p (a e) -> p a e", a=2), AX.X).then_inc(S("w_mean"), 1)
            dve.wait_ge(S("w_mean"), 1)
            dve.tensor_scalar(CM[:, :, 0], CM[:, :, 0], 1.0 / E, None, ALU.mult).then_inc(S("w_mean"), 1)
            dve.wait_ge(S("w_mean"), 2)
            dve.tensor_tensor(WQC[:, :], WQKV[:, 0:E], CM[:, 0, :].broadcast_to((E + 1, E)), ALU.subtract).then_inc(S("w_forms"), 1)
            dve.tensor_tensor(WKV[:, 0:E], WQKV[:, E:2 * E], CM[:, 1, :].broadcast_to((E + 1, E)), ALU.subtract).then_inc(S("w_forms"), 1)
            dve.tensor_copy(WKV[:, E:2 * E], WQKV[:, 2 * E:3 * E]).then_inc(S("w_forms"), 1)
            dve.wait_ge(S("w_turned"), 1)
            dve.tensor_copy(WT[:, :, :], PS[:, 0, 0:KCHUNKS * E].rearrange("p (k e) -> p k e", k=KCHUNKS)).then_inc(S("w_forms"), 1)
            dve.tensor_copy(HLT[:, :], PS[0:E + 1, 1, 0:E]).then_inc(S("w_forms"), 1)
            dve.tensor_copy(HLD[:, :].rearrange("p (d n) -> p n d", n=HEADS),
                            PS[0:E + 1, 1, 0:E].rearrange("p (n d) -> p n d", n=HEADS)).then_inc(S("w_forms"), 1)
            bd = BD.rearrange("p (n o) -> p n o", o=1)
            dve.tensor_tensor(BQ[:, :, :], PS[0:E, 1, 64:128].rearrange("p (n c) -> p n c", n=1).broadcast_to((E, HEADS, E)),
                              bd.broadcast_to((E, HEADS, E)), ALU.mult).then_inc(S("w_forms"), 1)
            for dst, at in ((BKV[:, 0, :, :], 128), (BKV[:, 1, :, :], 144), (F1[0:E, :, :], 176), (F2[0:E, :, :], 192)):
                dve.tensor_tensor(dst, PS[0:E, 1, at:at + D].rearrange("p (n c) -> p n c", n=1).broadcast_to((E, HEADS, D)),
                                  bd.broadcast_to((E, HEADS, D)), ALU.mult).then_inc(S("w_forms"), 1)
            dve.tensor_copy(FGW[:, :], PS[0:E, 1, 208:212]).then_inc(S("w_forms"), 1)
            dve.tensor_copy(WVT[:, :], PS[0:E, 1, 256:256 + E + 1]).then_inc(S("w_forms"), 1)
            for n in range(HEADS):
                dve.tensor_copy(SEL[:, n, 0:RAWC], CONST[:, C_SEL:C_SEL + RAWC]).then_inc(S("w_forms"), 1)
                dve.tensor_tensor(SEL[:, n, RAWC:SELC].rearrange("p (e g) -> p e g", e=EXPERTS),
                                  PS[:, 1, 160 + n * EXPERTS:160 + (n + 1) * EXPERTS].rearrange("p (e g) -> p e g", e=1)
                                  .broadcast_to((P, EXPERTS, EXPERTS)),
                                  BDE.rearrange("p (e g) -> p e g", g=1).broadcast_to((P, EXPERTS, EXPERTS)),
                                  ALU.mult).then_inc(S("w_forms"), 1)
            dve.wait_ge(S("w_made"), 1)
            for half in range(2):
                dve.tensor_scalar(WQ[:, half, :].rearrange("p (o h) -> p h o", o=D),
                                  PS[0:E + 1, 2, half * P:(half + 1) * P].rearrange("p (h o) -> p h o", o=D),
                                  float(D) ** 0.5, None, ALU.mult).then_inc(S("w_forms"), 1)
                dve.tensor_copy(WK[:, half * 32:half * 32 + 32].rearrange("p (o n) -> p n o", n=2),
                                PS[0:E + 1, 2, 256 + half * 32:256 + half * 32 + 32].rearrange("p (n o) -> p n o", n=2)
                                ).then_inc(S("w_forms"), 1)
            dve.tensor_copy(WV[:, :, 0:D], PS[0:E + 1, 2, 320:384].rearrange("p (n d) -> p n d", n=HEADS)).then_inc(S("w_forms"), 1)
            dve.memset(WV[E:E + 1, :, D:D + 1], 1.0).then_inc(S("w_forms"), 1)
            dve.tensor_tensor(WKV[:, 2 * E:3 * E], PS[0:E + 1, 3, 0:E], BOUT[:, :], ALU.add).then_inc(S("w_ready"), 1)

            def bc(x):
                return x.rearrange("p (n o) -> p n o", o=1).broadcast_to((P, PAIR * TILES, E))

            for g in range(BATCH // GROUP):
                def cut(g, chunk):
                    c, half = divmod(chunk, 2)
                    if half == 0:
                        dve.wait_ge(S(f"x_in{c}"), 16 * GROUP * (g + 1))
                    at_least(dve, "xt_psum", g * 4 * KCHUNKS + 4 * (chunk - 1))
                    x = X[:, c, :].rearrange("r (p w x) -> r w p x", p=PATCH, w=GRID)
                    dve.tensor_copy(XR[:, chunk % 2, :, :].rearrange("r w (p x) -> r w p x", p=8),
                                         x[:, :, half * 8:half * 8 + 8, :]).then_inc(S("chunk"), 1)

                if g == 0:
                    cut(g, 0)
                for u in range(1, 4 * KCHUNKS, 2):
                    if u % 4 == 1 and u // 4 + 1 < KCHUNKS:
                        cut(g, u // 4 + 1)
                    dve.wait_ge(S("xt_psum"), g * 4 * KCHUNKS + u + 1)
                    if u >= 4:
                        dve.wait_ge(S("xt_read"), g * 4 * KCHUNKS + u - 4 + 1)
                    n = (4 if u % 4 < 3 else 2) * ROWS
                    dve.tensor_copy(XT[:, u % 4, 0:n], PS[:, 4 + u % 4, 0:n]).then_inc(S("xt_sbuf_dve"), 1)
                if g + 1 < BATCH // GROUP:
                    cut(g + 1, 0)
                dve.wait_ge(S("xt_read"), (g + 1) * 4 * KCHUNKS)
                for w, n in ((2, 4), (3, 2)):
                    dve.tensor_scalar(HT[:, :, :].rearrange("e b (h w) -> e w (b h)", w=GRID)[:, 4 * w:4 * w + n, :],
                                      PS[0:E, w, 0:n * ROWS].rearrange("e (w r) -> e w r", w=n),
                                      TOKB[:, 0:1], None, ALU.add).then_inc(S("ht"), 1)

            def pair(i):
                return H[:, i * PAIR:(i + 1) * PAIR, :, :].rearrange("p b t e -> p (b t) e")

            def tokens_and_v(n):
                dve.wait_ge(S("kv_psum"), n + 1)
                dve.wait_ge(S("v"), n + 1)
                h = H[:, n:n + 1, :, :].rearrange("p b (a t) e -> p (b a) t e", a=3)
                stage(dve.tensor_tensor(h, PS[:, 4:7, 0:6 * E].rearrange("p a (t n) -> p a t n", t=2)[:, :, :, 2 * E:3 * E],
                                        h, ALU.add), "h_vo")

            def attention_out(n):
                dve.wait_ge(S("t2_psum"), n + 1)
                b = n % PAIR
                t6 = slice(b * TILES, (b + 1) * TILES)
                ps = PS[:, 7, 0:TILES * (E + 2)].rearrange("p (t n) -> p t n", t=TILES)
                stage(dve.tensor_copy(TMP[:, t6, :], ps[:, :, 0:E]), "t2")
                stage(dve.tensor_copy(Q2S[:, t6], ps[:, :, E]), "q2s")
                stage(dve.tensor_copy(Q4S[:, t6], ps[:, :, E + 1]), "q4s")

            for g in range(BATCH // GROUP):
                dve.wait_ge(S(f"txt_in{g}"), 16 * (TILES - 1))
            for step in range(-1, PAIRS + 1):
                norm, mid, back = step + 1, step, step - 1
                NORM, MID, BACK = norm < PAIRS, 0 <= mid < PAIRS, 0 <= back < PAIRS
                q = step % 2
                if NORM:
                    dve.wait_ge(S("img_in_h"), 2 * (norm * PAIR // QUAD + 1))
                    stage(dve.reduce_sum(MEAN, pair(norm), AX.X), "sum")
                    dve.wait_ge(S("sum"), norm + 1)
                    stage(dve.tensor_scalar(MEAN, MEAN, 1.0 / E, None, ALU.mult), "mean")
                    dve.wait_ge(S("mean"), norm + 1)
                    stage(dve.tensor_tensor(XC[:, :, :], pair(norm), bc(MEAN), ALU.subtract), "centred")
                if BACK:
                    dve.wait_ge(S("kvt_psum"), back + 1)
                    dve.wait_ge(S("kvt"), back + 1)
                    stage(dve.tensor_copy(SN[:, 0, :], PS[0:E, 7, PAIR * E:PAIR * E + PAIR]), "k_len2")
                if NORM:
                    dve.wait_ge(S("squared"), norm + 1)
                    stage(dve.reduce_sum(VAR, SQ[:, :, :], AX.X), "var")
                if BACK:
                    dve.wait_ge(S("k_len"), back + 1)
                    stage(dve.tensor_scalar(SN[:, 2, :], SN[:, 1, :], NORM_EPS, float(SEQ) ** 0.5, ALU.max, ALU.mult), "k_len_max")
                    dve.wait_ge(S("k_len_max"), back + 1)
                    stage(dve.reciprocal(SN[:, 3, :], SN[:, 2, :]), "k_scale")
                    dve.wait_ge(S("k_scale"), back + 1)
                    dve.wait_ge(S("kvw_psum"), back + 1)
                    stage(dve.tensor_tensor(KVW[:, :, 0:E], PS[0:E, 7, 256:256 + PAIR * E].rearrange("p (b e) -> p b e", b=PAIR),
                                            SN[:, 3, :].rearrange("p (b o) -> p b o", o=1).broadcast_to((E, PAIR, E)),
                                            ALU.mult), "kvw")
                if MID:
                    tokens_and_v(mid * PAIR)
                if NORM:
                    dve.wait_ge(S("rstd"), norm + 1)
                    at_least(dve, "xnt_psum", PAIR * (norm - 1))
                    stage(dve.tensor_tensor(XN[:, 1 - q, :, :], XC[:, :, :], bc(RSTD), ALU.mult), "xn")
                if BACK:
                    attention_out(back * PAIR)
                if MID:
                    tokens_and_v(mid * PAIR + 1)
                    dve.wait_ge(S("k2"), PAIR * (mid + 1))
                    stage(dve.reduce_sum(K2S, K2[:, :, :], AX.X), "k2s")
                    dve.wait_ge(S("k2s"), mid + 1)
                    stage(dve.tensor_scalar(K2S, K2S, DIV_EPS, None, ALU.add), "k2s_eps")
                    dve.wait_ge(S("k2s_eps"), mid + 1)
                    stage(dve.reciprocal(RK, K2S), "rk")
                    dve.wait_ge(S("rk"), mid + 1)
                    at_least(dve, "kvt_psum", mid - 1)
                    stage(dve.tensor_tensor(KN[:, q, :, :], K2[:, :, :], bc(RK), ALU.mult), "kn")
                if BACK:
                    attention_out(back * PAIR + 1)
                    dve.wait_ge(S("q2s"), PAIR * (back + 1))
                    stage(dve.tensor_scalar(Q2S, Q2S, DIV_EPS, None, ALU.add), "q2s_eps")
                    dve.wait_ge(S("q2s_eps"), back + 1)
                    stage(dve.reciprocal(RQ, Q2S), "rq")
                    dve.wait_ge(S("q_len"), back + 1)
                    dve.wait_ge(S("rq"), back + 1)
                    stage(dve.tensor_tensor(NQ2, NQ, RQ, ALU.mult), "nq")
                    dve.wait_ge(S("nq"), back + 1)
                    stage(dve.tensor_scalar(NQ2, NQ2, NORM_EPS, None, ALU.max), "nq_max")
                    dve.wait_ge(S("nq_max"), back + 1)
                    stage(dve.reciprocal(FQ, NQ2), "nq_rec")
                    dve.wait_ge(S("nq_rec"), back + 1)
                    stage(dve.tensor_tensor(FQ, FQ, RQ, ALU.mult), "fq")
                    dve.wait_ge(S("fq"), back + 1)
                    dve.wait_ge(S("t2"), PAIR * (back + 1))
                    stage(dve.tensor_tensor(TMP[:, :, :], TMP[:, :, :], bc(FQ), ALU.mult), "t2f")
                    dve.wait_ge(S("t2f"), back + 1)
                    dve.wait_ge(S("h_vo"), PAIR * (back + 1))
                    stage(dve.tensor_tensor(pair(back), pair(back), TMP[:, :, :], ALU.add), "h2_done")

            dve.wait_ge(S("cleared"), CLEARS)

            def iteration(it, p, C, M, A, D1, prev_a, first):
                def maximum(b, slot):
                    n, u = divmod(slot, UNITS)
                    i, lo, w, e0, ne = UNITS_M[u]
                    r = query_tile(i)[1]
                    heads = slice(n * EXPERTS + e0, n * EXPERTS + e0 + ne)
                    dst = NM[0:r, i, heads] if lo == 0 else NP[0:r, i - (TILES - 2), heads]
                    dve.wait_ge(S("max_scores"), b * SLOTS + slot + 1)
                    dve.tensor_reduce(dst, PS[0:r, ring_bank(M_BANKS, 1 - p, slot), 0:ne * w].rearrange("p (e w) -> p e w", e=ne), AX.X, ALU.max,
                                      negate=True).then_inc(S("maxed"), 1)

                def split_maxima(b, half, step):
                    h8 = slice(half * 8, half * 8 + 8)
                    count = 2 * b + half + 1
                    if step == 0:
                        dve.wait_ge(S("maxed"), b * SLOTS + (half + 1) * SLOTS // 2)
                        stage(dve.tensor_tensor(NM[:, TILES - 2:TILES, h8], NM[:, TILES - 2:TILES, h8], NP[:, :, h8], ALU.min), "max_whole")
                    if step == 1:
                        done(dve, "max_whole", count)
                        at_least(dve, "max_psum", count - 2)
                        stage(dve.tensor_copy(NB[:, half, :, 0, :], NM[:, :, h8]), "max1")
                    if step == 2:
                        done(dve, "max1", count)
                        stage(dve.tensor_tensor(NR[:, :, :], NM[:, :, h8], NB[:, half, :, 0, :], ALU.subtract), "max_rest")
                    if step == 3:
                        done(dve, "max_rest", count)
                        stage(dve.tensor_copy(NB[:, half, :, 1, :], NR[:, :, :]), "max2")
                    if step == 4:
                        done(dve, "max2", count)
                        stage(dve.tensor_tensor(NB[:, half, :, 2, :], NR[:, :, :], NB[:, half, :, 1, :], ALU.subtract), "max3")

                def sums(b, n, q):
                    dve.wait_ge(S("summed"), (b * HEADS + n + 1) * TILES)
                    dve.wait_ge(S("pads_in"), 16 * EXPERTS * (b + 1))
                    at_least(dve, "raw_psum", b * HEADS + n)
                    stage(dve.tensor_tensor(OT[:, 0:SEQ], PS[:, PV_BANK:PV_BANK + 2, :].rearrange("p a w -> p (a w)")[:, 0:SEQ],
                                            MT[q][:, n, :], ALU.mult), "ot")

                def inner_norm(name, b, slot, at, src, v, gain, bias, dst):
                    k24 = HEADS * TILES
                    s1 = lambda x: S1[:, x, :].rearrange("p (k o) -> p k o", o=1).broadcast_to((P, k24, D))
                    if slot == at:
                        done(dve, f"{name}_in", b + 1)
                        stage(dve.reduce_sum(S1[:, v - 3, :], src, AX.X), f"{name}_sum")
                    if slot == at + 1:
                        done(dve, f"{name}_sum", b + 1)
                        stage(dve.tensor_scalar(S1[:, v - 2, :], S1[:, v - 3, :], 1.0 / D, None, ALU.mult), f"{name}_mean")
                    if slot == at + 2:
                        done(dve, f"{name}_mean", b + 1)
                        stage(dve.tensor_tensor(YC[:, :, :], src, s1(v - 2), ALU.subtract), f"{name}_centred")
                    if slot == at + 4:
                        dve.wait_ge(S(f"{name}_squared"), b + 1)
                        stage(dve.reduce_sum(S1[:, v - 1, :], GL[:, :, :, :].rearrange("p k e g -> p k (e g)"), AX.X), f"{name}_var")
                    if slot == at + 8:
                        dve.wait_ge(S(f"{name}_rstd"), b + 1)
                        stage(dve.tensor_tensor(YC[:, :, :], YC[:, :, :], s1(v + 1), ALU.mult), f"{name}_norm")
                    if slot == at + 9:
                        done(dve, f"{name}_norm", b + 1)
                        stage(dve.tensor_tensor(YC[:, :, :], YC[:, :, :], gain[:, 0:1, :].broadcast_to((P, k24, D)), ALU.mult), f"{name}_gain")
                    if slot == at + 10:
                        done(dve, f"{name}_gain", b + 1)
                        stage(dve.tensor_tensor(dst, YC[:, :, :] if name == "z" else YC[:, :, :].rearrange("p (n t) d -> p n t d", n=HEADS),
                                                bias[:, 0:1, :].broadcast_to((P, k24, D)) if name == "z" else
                                                bias[:, 0:1, :].rearrange("p o (t d) -> p o t d", t=1).broadcast_to((P, HEADS, TILES, D)),
                                                ALU.add), f"{name}_out")

                for slot in range(SLOTS):
                    if M:
                        maximum(it + 1, slot)
                        if SLOTS // 2 <= slot < SLOTS // 2 + 5:
                            split_maxima(it + 1, 0, slot - SLOTS // 2)
                    if C and slot < 5:
                        split_maxima(it, 1, slot)
                    if D1 and slot == OT_AT + 3 * UNITS - SLOTS:
                        sums(it - 1, HEADS - 1, 1 - p)
                    for n in range(HEADS - 1):
                        if C and slot == OT_AT + n * UNITS:
                            sums(it, n, p)
                    if A:
                        b = it + 2
                        h = H[:, bass.ds(b, 1), :, :].rearrange("p o t e -> p (o t) e")
                        s1 = lambda x: S1[:, x, 0:TILES].rearrange("p (t o) -> p t o", o=1).broadcast_to((P, TILES, E))
                        if slot == 1:
                            stage(dve.reduce_sum(S1[:, 0, 0:TILES], h, AX.X), "a_sum")
                        if slot == 2:
                            done(dve, "a_sum", b + 1)
                            stage(dve.tensor_scalar(S1[:, 16, 0:TILES], S1[:, 0, 0:TILES], 1.0 / E, None, ALU.mult), "a_mean")
                        if slot == 3:
                            done(dve, "a_mean", b + 1)
                            stage(dve.tensor_tensor(AC[:, :, :], h, s1(16), ALU.subtract), "a_centred")
                        if slot == 6:
                            dve.wait_ge(S("a_squared"), b + 1)
                            stage(dve.reduce_sum(S1[:, 1, 0:TILES], AS[:, :, :], AX.X), "a_var")
                        if slot == 9:
                            dve.wait_ge(S("a_rstd"), b + 1)
                            stage(dve.tensor_tensor(AN[:, :, :], AC[:, :, :], s1(3), ALU.mult), "a_norm")
                        for idx, at in enumerate(PROJ_AT):
                            if slot == at + 2:
                                half, c = divmod(idx, 2)
                                lo, hi = halves(SEQ)[c]
                                r = P if half < 2 else E
                                top = Q1[:, half, lo:hi] if half < 2 else K1[:, lo:hi]
                                dve.wait_ge(S("q1"), 6 * b + idx + 1)
                                stage(dve.tensor_tensor(QR[0:r, lo:hi], QR[0:r, lo:hi], top, ALU.subtract), "q_rest")
                        for c, at in enumerate(PADS_AT):
                            if slot == at:
                                lo, hi = halves(SEQ)[c]
                                dve.wait_ge(S("pads_psum"), 2 * b + c + 1)
                                at_least(dve, "pads_in", 16 * EXPERTS * b)
                                stage(dve.tensor_scalar(MK[:, lo:hi], PS[0:E, MISC, 0:hi - lo], 0.0, None, ALU.not_equal), "pads")
                    if D1:
                        b = it - 1
                        k24 = HEADS * TILES
                        bc4 = lambda x: S1[:, x, :].rearrange("p (k o) -> p k o", o=1).broadcast_to((P, k24, EXPERTS))
                        if slot == DEN_AT:
                            dve.wait_ge(S("raw"), HEADS * (b + 1))
                            stage(dve.reciprocal(RD, RAW[:, :, :, 0:RAWC].rearrange("p n t (e c) -> p (n t) e c", e=EXPERTS)[:, :, :, D]), "den_rec")
                        if slot == 17:
                            dve.wait_ge(S("gate_parts"), b + 1)
                            stage(dve.reduce_sum(LG, GL[:, :, :, :].rearrange("p k e g -> p k g e"), AX.X), "gate_logits")
                        if slot == 18:
                            done(dve, "gate_logits", b + 1)
                            stage(dve.tensor_tensor(LG.rearrange("p (n t) g -> p n t g", n=HEADS), LG.rearrange("p (n t) g -> p n t g", n=HEADS),
                                                    GB[:, :, :].rearrange("p n (t g) -> p n t g", t=1).broadcast_to((P, HEADS, TILES, EXPERTS)),
                                                    ALU.add), "gate_biased")
                        if slot == 19:
                            done(dve, "gate_biased", b + 1)
                            stage(dve.reduce_max(S1[:, 17, :], LG, AX.X), "gate_max")
                        if slot == 20:
                            done(dve, "gate_max", b + 1)
                            stage(dve.tensor_tensor(LG, LG, bc4(17), ALU.subtract), "gate_sub")
                        if slot == 22:
                            dve.wait_ge(S("gate_exp"), b + 1)
                            stage(dve.reduce_sum(S1[:, 18, :], EG, AX.X), "gate_sum")
                        if slot == 23:
                            stage(dve.tensor_tensor(W4, EG, RD, ALU.mult), "gate_den")
                        if slot == 24:
                            done(dve, "gate_sum", b + 1)
                            stage(dve.reciprocal(S1[:, 19, :], S1[:, 18, :]), "gate_rec")
                        if slot == 25:
                            done(dve, "gate_rec", b + 1)
                            done(dve, "gate_den", b + 1)
                            stage(dve.tensor_tensor(W4, W4, bc4(19), ALU.mult), "mix_w")
                        if slot == 32:
                            dve.wait_ge(S("mixed"), HEADS * (b + 1))
                            stage(dve.reduce_sum(Y[:, :, :], MIXP[:, :, :, :].rearrange("p k e d -> p k d e"), AX.X), "mixture")
                        if slot == 33:
                            done(dve, "mixture", b + 1)
                            dve.wait_ge(S("resid"), HEADS)
                            stage(dve.tensor_tensor(Y[:, :, :], Y[:, :, :], R[:, :, :, :].rearrange("p n t d -> p (n t) d"), ALU.add), "y_in")
                        inner_norm("y", b, slot, Y_AT, Y[:, :, :], 6, LNG, LNB, FX[:, :, :, :].rearrange("p t n d -> p n t d"))
                        if slot == 45:
                            done(dve, "y_out", b + 1)
                            stage(dve.tensor_scalar(FM[:, :, :, :], FX[:, :, :, :], 0.0, None, ALU.not_equal), "fx_mask")
                        for c, at in enumerate(FX_AT):
                            if slot == at:
                                lo, hi = halves(PADDED)[c]
                                dve.wait_ge(S("fxt"), 2 * b + c + 1)
                                stage(dve.tensor_scalar(FMT[:, lo:hi], FXT[0:E, lo:hi], 0.0, None, ALU.not_equal), "fxt_mask")
                        for c, at in enumerate(FC1_AT):
                            if slot == at:
                                lo, hi = halves(PADDED)[c]
                                dve.wait_ge(S("fc1_psum"), 2 * b + c + 1)
                                dve.wait_ge(S("fxt_mask"), 2 * b + c + 1)
                                stage(dve.scalar_tensor_tensor(HXT[0:E, lo:hi], PS[0:E, MISC, 0:hi - lo], 0.0, FMT[:, lo:hi],
                                                               ALU.max, ALU.mult), "hxt")
                        if slot == FC2_AT:
                            dve.wait_ge(S("fc2_psum"), b + 1)
                            done(dve, "fx_mask", b + 1)
                            flat = lambda x: x[:, :, :, :].rearrange("p t n d -> p (t n d)")
                            stage(dve.tensor_tensor(Y[:, :, :].rearrange("p k d -> p (k d)"), PS[:, MISC, 0:TILES * E], flat(FM), ALU.mult), "fc2")
                        if slot == FC2_AT + 2:
                            done(dve, "fc2", b + 1)
                            stage(dve.tensor_tensor(Y[:, :, :], Y[:, :, :], FX[:, :, :, :].rearrange("p t n d -> p (t n) d"), ALU.add), "z_in")
                        inner_norm("z", b, slot, Z_AT, Y[:, :, :], 12, FNG, FNB, FO[:, :, :, :].rearrange("p t n d -> p (t n) d"))
                        bf = lambda x: S1[:, x, 0:TILES].rearrange("p (t o) -> p t o", o=1).broadcast_to((P, TILES, HEADS))
                        if slot == FG_AT:
                            dve.wait_ge(S("fg_psum"), b + 1)
                            stage(dve.tensor_copy(FL, PS[:, MISC, 0:TILES * HEADS].rearrange("p (t n) -> p t n", n=HEADS)), "fg_logits")
                        if slot == FG_AT + 1:
                            done(dve, "fg_logits", b + 1)
                            stage(dve.reduce_max(S1[:, 14, 0:TILES], FL, AX.X), "fg_max")
                        if slot == FG_AT + 2:
                            done(dve, "fg_max", b + 1)
                            stage(dve.tensor_tensor(FL, FL, bf(14), ALU.subtract), "fg_sub")
                        if slot == 85:
                            dve.wait_ge(S("fg_exp"), b + 1)
                            stage(dve.reduce_sum(S1[:, 14, 0:TILES], FE, AX.X), "fg_sum")
                        if slot == 86:
                            done(dve, "fg_sum", b + 1)
                            stage(dve.reciprocal(S1[:, 15, 0:TILES], S1[:, 14, 0:TILES]), "fg_rec")
                        if slot == 87:
                            done(dve, "fg_rec", b + 1)
                            stage(dve.tensor_tensor(FE, FE, bf(15), ALU.mult), "fgate")

            schedule(dve, iteration)

        @block.tensor
        def _(pe):
            pe.wait_ge(S("weights_in"), 16 * WEIGHT_DMAS)
            for k in range(KCHUNKS):
                pe.transpose(PS[:, 0, k * E:(k + 1) * E], TOKW[:, k * P:(k + 1) * P], IDENT[0:E, 0:E])
            turned = ((HL[:, :], 0), (WQN[:, :, :], 64), (WKN[:, :, :], 128), (WVN[:, :, :], 144), (GN[:, :, :], 160),
                      (F1N[:, :, :], 176), (F2N[:, :, :], 192), (FGN[:, :], 208), (WQKV[:, 2 * E:3 * E], 256))
            for w, at in turned:
                k = w.shape[0]
                m = int(np.prod(w.shape[1:]))
                last = pe.transpose(PS[0:m, 1, at:at + k], w, IDENT[0:k, 0:k])
            last.then_inc(S("w_turned"), 1)
            pe.wait_ge(S("w_forms"), 23)
            pe.matmul(PS[0:E + 1, 2, 0:256], HL[:, :], BQ[:, :, :], start=True, stop=True)
            pe.matmul(PS[0:E + 1, 2, 256:384], HL[:, :], BKV[:, :, :, :], start=True, stop=True)
            pe.matmul(PS[0:E + 1, 3, 0:E], WVT[:, :], WOUT[:, :], start=True, stop=True).then_inc(S("w_made"), 1)
            pe.wait_ge(S("w_ready"), 1)
            pe.wait_ge(S("ones_row"), 3)

            PATCH_UNITS = 4 * KCHUNKS

            def turn_patches(g, u):
                chunk, w4 = divmod(u, 4)
                c, half = divmod(chunk, 2)
                if w4 == 0:
                    pe.wait_ge(S("chunk"), g * KCHUNKS + chunk + 1)
                if u < 4 and g > 0 and u >= 2:
                    pe.wait_ge(S("img_in_h"), (g - 1) * 4 + 2 * (u - 1))
                if u >= 4:
                    pe.wait_ge(S("xt_sbuf_act" if u % 2 == 0 else "xt_sbuf_dve"), g * PATCH_UNITS // 2 + (u - 4) // 2 + 1)
                for j in range(4 if w4 < 3 else 2):
                    last = pe.transpose(PS[:, 4 + u % 4, j * ROWS:(j + 1) * ROWS],
                                        XR[:, chunk % 2, 4 * w4 + j, :], IDENT[0:ROWS, 0:ROWS])
                last.then_inc(S("xt_psum"), 1)

            AHEAD = 3
            EARLY = 2
            for g in range(BATCH // GROUP):
                for u in range(0 if g == 0 else EARLY, AHEAD):
                    turn_patches(g, u)
                for u in range(PATCH_UNITS):
                    if u + AHEAD < PATCH_UNITS:
                        turn_patches(g, u + AHEAD)
                    chunk, w4 = divmod(u, 4)
                    n = (4 if w4 < 3 else 2) * ROWS
                    pe.wait_ge(S("xt_sbuf_act" if u % 2 == 0 else "xt_sbuf_dve"), g * PATCH_UNITS // 2 + u // 2 + 1)
                    mm = pe.matmul(PS[0:E, w4, 0:n], WT[:, chunk, :], XT[:, u % 4, 0:n],
                                   start=(chunk == 0), stop=(chunk == KCHUNKS - 1))
                    mm.then_inc(S("xt_read"), 1)
                if g + 1 < BATCH // GROUP:
                    for u in range(EARLY):
                        turn_patches(g + 1, u)
                pe.wait_ge(S("ht"), 4 * (g + 1))
                for q in range(GROUP // QUAD):
                    for b in range(QUAD):
                        pe.transpose(PS[:, 6 + q, b * E:(b + 1) * E], HT[:, q * QUAD + b, 0:P], IDENT[0:E, 0:E])
                        mm = pe.transpose(PS[0:IMG_TAIL, 6 + q, (QUAD + b) * E:(QUAD + b + 1) * E], HT[:, q * QUAD + b, P:PATCHES],
                                          IDENT[0:E, 0:E])
                    mm.then_inc(S("img_tokens"), 1)

            def turn_tokens(n, b, q):
                if b == 0:
                    pe.wait_ge(S("xn"), n // PAIR + 1)
                at_least(pe, "xnt", n)
                for t in range(TILES):
                    mm = pe.transpose(PS[0:E, t // 4, (t % 4) * P:(t % 4 + 1) * P], XN[:, q, b * TILES + t, :], IDENT)
                mm.then_inc(S("xnt_psum"), 1)

            def project_q(n, b):
                pe.wait_ge(S("xnt"), n + 1)
                at_least(pe, "q2t", n)
                pe.matmul(PS[0:E, 2, :], WQC[:, :], XNT[:, b, 0:BANK], start=True, stop=True)
                pe.matmul(PS[0:E, 3, 0:PADDED - BANK], WQC[:, :], XNT[:, b, BANK:PADDED],
                          start=True, stop=True).then_inc(S("q_psum"), 1)

            def project_kv(n, b):
                if n == 0:
                    pe.wait_ge(S("img_in_h"), 4 * (BATCH // GROUP))
                at_least(pe, "h_vo", n)
                for t in range(TILES):
                    mm = pe.matmul(PS[:, 4 + t // 2, (t % 2) * 3 * E:(t % 2 + 1) * 3 * E],
                                   XNT[:, b, t * P:(t + 1) * P], WKV[:, :], start=True, stop=True)
                mm.then_inc(S("kv_psum"), 1)

            def attend(n, b, q):
                pe.wait_ge(S("q4t"), n + 1)
                at_least(pe, "q4s", n)
                for t in range(TILES):
                    at = t * (E + 2)
                    pe.matmul(PS[:, 7, at:at + E + 1], Q2T[:, q, b, t * P:(t + 1) * P], KVW[:, b, :], start=True, stop=True)
                    mm = pe.matmul(PS[:, 7, at + E + 1:at + E + 2], Q4T[:, q, b, t * P:(t + 1) * P],
                                   ONES[0:E, :], start=True, stop=True)
                mm.then_inc(S("t2_psum"), 1)

            for step in range(PAIRS + 1):
                mid, back = step, step - 1
                q = step % 2
                if 0 <= back:
                    at_least(pe, "q4s", PAIR * back)
                    pe.wait_ge(S("v"), PAIR * (back + 1))
                    pe.wait_ge(S("kn"), back + 1)
                    for b in range(PAIR):
                        for t in range(TILES):
                            r = rows(t)
                            pe.matmul(PS[0:E, 7, b * E:(b + 1) * E], V[0:r, 1 - q, b * TILES + t, :],
                                      KN[0:r, 1 - q, b * TILES + t, :], start=(t == 0), stop=(t == TILES - 1))
                if mid < PAIRS:
                    turn_tokens(mid * PAIR, 0, q)
                if 0 <= back:
                    pe.wait_ge(S("kns"), back + 1)
                    for b in range(PAIR):
                        for t in range(TILES):
                            r = rows(t)
                            mm = pe.matmul(PS[0:E, 7, PAIR * E + b:PAIR * E + b + 1], KNS[0:r, 1 - q, b * TILES + t, :], ONES[0:r, :],
                                           start=(t == 0), stop=(t == TILES - 1))
                    mm.then_inc(S("kvt_psum"), 1)
                if mid < PAIRS:
                    project_q(mid * PAIR, 0)
                    project_kv(mid * PAIR, 0)
                if 0 <= back:
                    pe.wait_ge(S("kvt"), back + 1)
                    pe.wait_ge(S("k_len2"), back + 1)
                    for b in range(PAIR):
                        mm = pe.matmul(PS[0:E, 7, 256 + b * E:256 + (b + 1) * E], KVT[:, b, :], WOUT[:, :], start=True, stop=True)
                    mm.then_inc(S("kvw_psum"), 1)
                if mid < PAIRS:
                    turn_tokens(mid * PAIR + 1, 1, q)
                if 0 <= back:
                    pe.wait_ge(S("kvw"), back + 1)
                    attend(back * PAIR, 0, 1 - q)
                if mid < PAIRS:
                    project_q(mid * PAIR + 1, 1)
                    project_kv(mid * PAIR + 1, 1)
                if 0 <= back:
                    attend(back * PAIR + 1, 1, 1 - q)

            pe.wait_ge(S("cleared"), CLEARS)

            def iteration(it, p, C, M, A, D1, prev_a, first):
                last_taken = ["raw", HEADS * (it - 1) + HEADS - 1]

                def side_bank(name, count):
                    at_least(pe, last_taken[0], last_taken[1])
                    last_taken[:] = [name, count]

                def side(width):
                    return PS[:, MISC, 0:width]

                def scores(slot):
                    n, u = divmod(slot, UNITS)
                    j, lo, w, e0, ne = UNITS_S[u]
                    r = rows(j)
                    if slot % (SLOTS // 2) == 0:
                        pe.wait_ge(S(f"max_in{n // 2}"), 16 * (it + 1))
                    at_least(pe, "exped", bank_left(S_BANKS, it, p, slot))
                    h0 = n * EXPERTS + e0
                    pe.matmul(PS[0:r, ring_bank(S_BANKS, p, slot), 0:ne * w], KA[p][0:KDIM + MROWS, n, j * P:j * P + r],
                              QA[p][0:KDIM + MROWS, h0:h0 + ne, lo:lo + w], start=True, stop=True).then_inc(S("scores"), 1)

                def max_scores(b, q, slot):
                    n, u = divmod(slot, UNITS)
                    i, lo, w, e0, ne = UNITS_M[u]
                    s0, r = query_tile(i)
                    if slot % (SLOTS // 2) == 0:
                        pe.wait_ge(S(f"q_in{n // 2}"), 16 * PARTS * (b + 1))
                        pe.wait_ge(S(f"k_in{n // 2}"), 16 * PARTS * (b + 1))
                    at_least(pe, "maxed", bank_left(M_BANKS, b, q, slot))
                    diagonal = lo + w == TAIL + i * P
                    bank = PS[0:r, ring_bank(M_BANKS, q, slot), 0:ne * w]
                    for e in range(ne):
                        mm = pe.matmul(bank[:, e * w:(e + 1) * w], QA[q][0:KDIM, n * EXPERTS + e0 + e, s0:s0 + r],
                                       KA[q][0:KDIM, n, lo:lo + w], start=(e == 0), stop=(not diagonal and e == ne - 1))
                    if diagonal:
                        mm = pe.matmul(bank.rearrange("p (e w) -> p e w", e=ne)[:, :, w - r:w], IDB[:, 0:r],
                                       MASKB[:, 0:r].rearrange("p (e w) -> p e w", e=1).broadcast_to((P, ne, r)),
                                       start=False, stop=True)
                    mm.then_inc(S("max_scores"), 1)

                def weighted_sums(b, n, j, q):
                    r = rows(j)
                    pe.wait_ge(S("masked"), (b * HEADS + n) * TILES + j + 1)
                    if j == 0:
                        at_least(pe, "ot", b * HEADS + n)
                        if n == 0:
                            pe.wait_ge(S("va"), 2 * b + 2)
                    for bank, lo, hi in ((PV_BANK, j * P, BANK), (PV_BANK + 1, max(BANK, j * P), SEQ)):
                        if lo < hi:
                            lo_b = lo % BANK
                            for e in range(EXPERTS):
                                mm = pe.matmul(PS[32 * e:32 * e + 32, bank, lo_b:lo_b + hi - lo], VA[q][0:r, j, n, :],
                                               PT[j][0:r, e, lo - j * P:hi - j * P], start=(j == 0),
                                               stop=(j == (BANK // P - 1 if bank == PV_BANK else TILES - 1)))
                    mm.then_inc(S("summed"), 1)

                def to_tokens(b, n):
                    side_bank("raw", b * HEADS + n + 1)
                    pe.wait_ge(S("ot"), b * HEADS + n + 1)
                    for t in range(TILES):
                        mm = pe.matmul(side(TILES * SELC)[:, t * SELC:(t + 1) * SELC], OT[:, t * P:(t + 1) * P], SEL[:, n, :],
                                       start=True, stop=True)
                    mm.then_inc(S("raw_psum"), 1)

                def turn_maxima(b, half):
                    side_bank("max_sbuf", 2 * b + half + 1)
                    done(pe, "max3", 2 * b + half + 1)
                    bank = PS[0:24, MISC, 0:SEQ // 2].bitcast(BF16)
                    apart(pe)
                    for i in range(TILES):
                        s0, r = query_tile(i)
                        mm = pe.transpose(bank[:, s0:s0 + r], NB[0:r, half, i, :, :], IDB[0:r, 0:r])
                    mm.then_inc(S("max_psum"), 1)

                def turn(src, t0, t1):
                    for t in range(t0, t1):
                        mm = pe.transpose(side(BANK)[0:E, (t - t0) * P:(t - t0 + 1) * P], src(t), IDENT)
                    return mm

                for slot in range(SLOTS):
                    if C:
                        scores(slot)
                    if M:
                        max_scores(it + 1, 1 - p, slot)
                    for n in range(-1, HEADS):
                        for j in range(TILES):
                            if slot == n * UNITS + LAST_UNIT[j] + PV_LAG:
                                if n >= 0 and C:
                                    weighted_sums(it, n, j, p)
                                if n < 0 and D1:
                                    weighted_sums(it - 1, HEADS - 1, j, 1 - p)
                    if C and slot == MAX1_AT:
                        turn_maxima(it, 1)
                    if M and slot == MAX0_AT:
                        turn_maxima(it + 1, 0)
                    if D1 and slot == SEL_AT + 3 * UNITS - SLOTS:
                        to_tokens(it - 1, HEADS - 1)
                    for n in range(HEADS - 1):
                        if C and slot == SEL_AT + n * UNITS:
                            to_tokens(it, n)
                    if A:
                        b = it + 2
                        for c, at in enumerate(TURN_AT):
                            if slot == at:
                                side_bank("xft", 2 * b + c + 1)
                                done(pe, "a_norm", b + 1)
                                apart(pe)
                                turn(lambda t: AN[:, t, :], *((0, 4), (4, TILES))[c]).then_inc(S("xft_psum"), 1)
                        if slot == RESID_AT and known_first_heads(b):
                            side_bank("resid", b + 1)
                            pe.wait_ge(S("xft"), 2 * b + 2)
                            for t in range(TILES):
                                mm = pe.matmul(side(TILES * D)[:, t * D:(t + 1) * D], XFT[p][:, t * P:(t + 1) * P],
                                               HLT[:, b * D:(b + 1) * D], start=True, stop=True)
                            mm.then_inc(S("resid_psum"), 1)
                        for idx, at in enumerate(PROJ_AT):
                            if slot == at:
                                half, c = divmod(idx, 2)
                                lo, hi = halves(SEQ)[c]
                                side_bank("q_out", 6 * b + idx + 1)
                                if idx == 0:
                                    pe.wait_ge(S("xft"), 2 * b + 2)
                                w = WQ[:, half, :] if half < 2 else WK[:, :]
                                pe.matmul(side(hi - lo)[0:w.shape[1]], w, XFT[p][:, lo:hi], start=True, stop=True).then_inc(S("proj"), 1)
                        for c, at in enumerate(PADS_AT):
                            if slot == at:
                                lo, hi = halves(SEQ)[c]
                                side_bank("pads", 2 * b + c + 1)
                                pe.matmul(side(hi - lo)[0:E], HLD[:, :], XFT[p][:, lo:hi], start=True, stop=True).then_inc(S("pads_psum"), 1)
                    if M:
                        for c, at in enumerate(V_AT):
                            if slot == at:
                                b = it + 1
                                t0, t1 = ((0, 4), (4, TILES))[c]
                                side_bank("va", 2 * b + c + 1)
                                for t in range(t0, t1):
                                    mm = pe.matmul(side(BANK)[:, (t - t0) * P:(t - t0 + 1) * P], XFT[1 - p][:, t * P:(t + 1) * P],
                                                   WV[:, :, :], start=True, stop=True)
                                mm.then_inc(S("v_psum"), 1)
                    if D1:
                        b = it - 1
                        for c, at in enumerate(FX_AT):
                            if slot == at:
                                side_bank("fxt", 2 * b + c + 1)
                                done(pe, "y_out", b + 1)
                                apart(pe)
                                turn(lambda t: FX[:, t, :, :], *((0, 4), (4, TILES))[c]).then_inc(S("fxt_psum"), 1)
                        for c, at in enumerate(FC1_AT):
                            if slot == at:
                                lo, hi = halves(PADDED)[c]
                                side_bank("hxt", 2 * b + c + 1)
                                pe.wait_ge(S("fxt"), 2 * b + c + 1)
                                pe.matmul(side(hi - lo)[0:E], F1[:, :, :], FXT[:, lo:hi], start=True, stop=True).then_inc(S("fc1_psum"), 1)
                        if slot == FC2_AT:
                            side_bank("fc2", b + 1)
                            pe.wait_ge(S("hxt"), 2 * b + 2)
                            for t in range(TILES):
                                mm = pe.matmul(side(TILES * E)[:, t * E:(t + 1) * E], HXT[:, t * P:(t + 1) * P], F2[:, :, :],
                                               start=True, stop=True)
                            mm.then_inc(S("fc2_psum"), 1)
                        for c, at in enumerate(FO_AT):
                            if slot == at:
                                side_bank("fot", 2 * b + c + 1)
                                done(pe, "z_out", b + 1)
                                apart(pe)
                                turn(lambda t: FO[:, t, :, :], *((0, 4), (4, TILES))[c]).then_inc(S("fot_psum"), 1)
                        if slot == FG_AT:
                            side_bank("fg_logits", b + 1)
                            pe.wait_ge(S("fot"), 2 * b + 2)
                            for t in range(TILES):
                                mm = pe.matmul(side(TILES * HEADS)[:, t * HEADS:(t + 1) * HEADS], FOT[:, t * P:(t + 1) * P], FGW[:, :],
                                               start=True, stop=True)
                            mm.then_inc(S("fg_psum"), 1)

            schedule(pe, iteration)



def kernel(**inputs):
    import concourse.bacc as _bacc
    from concourse import mybir as _mybir
    from concourse.bass_utils import run_bass_kernel_spmd as _run

    nc = _bacc.Bacc("TRN2", target_bir_lowering=False, num_devices=1)
    nc.disable_value_cache = True
    arrays, aps = {}, {}
    for name, v in list(inputs.items()) + [("const", shape_constants())]:
        v = np.ascontiguousarray(v)
        arrays["in_" + name] = v
        aps[name] = nc.dram_tensor("in_" + name, v.shape, _mybir.dt.from_np(v.dtype), kind="ExternalInput").ap()
    out = nc.dram_tensor("out_0", (BATCH, SEQ, E), _mybir.dt.float32, kind="ExternalOutput").ap()
    build(nc, aps, out)
    result = _run(nc, [arrays], core_ids=[0])
    return result.results[0]["out_0"]
```

```python
import numpy as np
from contextlib import ExitStack

import concourse.bass as bass
from concourse import mybir
from concourse.alu_op_type import AluOpType as ALU

ACT = mybir.ActivationFunctionType
AX = mybir.AxisListType
F32 = mybir.dt.float32
BF16 = mybir.dt.bfloat16
U8 = mybir.dt.uint8

P = 128
BATCH, CHANNELS, IMAGE, PATCH = 16, 3, 224, 16
GRID = IMAGE // PATCH
PATCHES = GRID * GRID
TEXT = 512
E = 64
SEQ = PATCHES + TEXT
TILES = -(-SEQ // P)
TAIL = SEQ - (TILES - 1) * P
PADDED = TILES * P
HEADS, EXPERTS, D = 4, 4, 16
GROUP = BATCH // 2
PAIR = 2
PAIRS = BATCH // PAIR
QUAD = 4
ROWS = GROUP * GRID
KCHUNKS = CHANNELS * PATCH * PATCH // P
IMG_TAIL = PATCHES - P
TXT_HEAD = P - IMG_TAIL
BANK = 512
LN_EPS = 1e-5
DIV_EPS = 1e-7
NORM_EPS = 1e-12
INNER_EPS = 1e-8
MASKED = -1e30

C_IDENT, C_MASK, C_BD, C_BDE, C_SEL = 0, P, 2 * P, 2 * P + 4, 2 * P + 8
RAWC = EXPERTS * (D + 1)
SELC = RAWC + EXPERTS * EXPERTS
C_ALL = C_SEL + RAWC


def shape_constants():
    c = np.zeros((P, C_ALL), np.float32)
    c[:, C_IDENT:C_IDENT + P] = np.eye(P)
    s, t = np.arange(P)[:, None], np.arange(P)[None, :]
    c[:, C_MASK:C_MASK + P] = np.where(t <= s, 0.0, MASKED)
    for r in range(HEADS * D):
        c[r, C_BD + r // D] = 1.0
    for e in range(EXPERTS):
        c[32 * e:32 * e + D, C_BDE + e] = 1.0
        for d in range(D + 1):
            c[32 * e + d, C_SEL + e * (D + 1) + d] = 1.0
    return c


UNITS_S = []
for _j in range(TILES):
    for _lo, _hi in ((_j * P, BANK), (max(BANK, _j * P), SEQ)):
        if _lo < _hi:
            _n = min(EXPERTS, BANK // (_hi - _lo))
            UNITS_S += [(_j, _lo, _hi - _lo, _e, _n) for _e in range(0, EXPERTS, _n)]
UNITS_M = []
for _i in range(TILES):
    _w = TAIL + _i * P
    _cut = _w if _w <= BANK else (_w - P if _w - P <= BANK else BANK)
    for _lo, _hi in ((0, _cut), (_cut, _w)):
        if _lo < _hi:
            _n = min(EXPERTS, BANK // (_hi - _lo))
            UNITS_M += [(_i, _lo, _hi - _lo, _e, _n) for _e in range(0, EXPERTS, _n)]
UNITS = len(UNITS_S)
assert UNITS == len(UNITS_M) == 22
SLOTS = HEADS * UNITS
PIECES = ((10, 0, 0, 256),
          (12, 0, 256, BANK),
          (13, 0, BANK, SEQ),
          (17, 1, P, 320),
          (18, 1, 320, BANK),
          (19, 1, BANK, SEQ),
          (21, 2, 256, BANK),
          (22, 2, BANK, SEQ),
          (23, 3, 3 * P, BANK),
          (24, 3, BANK, SEQ),
          (26, 4, BANK, SEQ),
          (27, 5, 5 * P, SEQ))
LAST_UNIT = [max(u for u, x in enumerate(UNITS_S) if x[0] == j) for j in range(TILES)]
Q_PARTS, K_PARTS = (1, 1, 2, 2, 1, 3), (1, 2, 1, 2, 3, 1)
PARTS = len(Q_PARTS)
KDIM = PARTS * D
MROWS = 3
MASK_LAG, OT_AT, SEL_AT = 1, 27, 35


MAX_STEPS = (
    "max_whole", "max1", "max_rest", "max2", "max3"
)
NORM_STEPS = (
    "a_sum", "a_mean", "a_centred", "a_var", "a_norm"
)
FF_STEPS = (
    "den_rec", "gate_logits", "gate_biased", "gate_max", "gate_sub", "gate_sum", "gate_den", "gate_rec",
    "mix_w", "mixture", "y_in", "y_sum", "y_mean", "y_centred", "y_var", "y_norm", "y_gain", "y_out",
    "fx_mask", "fc2", "z_in", "z_sum", "z_mean", "z_centred", "z_var", "z_norm", "z_gain", "z_out",
    "fg_logits", "fg_max", "fg_sub", "fg_sum", "fg_rec", "fgate"
)
STEPS = {step: (group, steps) for group, steps in (("max_steps", MAX_STEPS), ("norm_steps", NORM_STEPS), ("ff_steps", FF_STEPS))
         for step in steps}


def query_tile(i):
    return (0, TAIL) if i == 0 else (TAIL + (i - 1) * P, P)


def rows(tile):
    return P if tile < TILES - 1 else TAIL


def build(nc, a, out):
    ctx = ExitStack()
    with ctx:
        signals = {}

        def S(name):
            if name not in signals:
                signals[name] = ctx.enter_context(nc.semaphore(name))
            return signals[name]

        def sb(name, shape, dt=F32, stack=ctx):
            return stack.enter_context(nc.sbuf_tensor(name, shape, dt))

        H = sb("H", [P, BATCH, TILES, E])
        CONST = sb("CONST", [P, C_ALL])
        IDENT = CONST[:, C_IDENT:C_IDENT + P]
        BD = CONST[0:HEADS * D, C_BD:C_BD + HEADS]
        BDE = CONST[:, C_BDE:C_BDE + EXPERTS]
        IDB = sb("IDB", [P, P], BF16)
        MASKB = sb("MASKB", [P, P], BF16)
        HLT = sb("HLT", [E + 1, E])
        WQ = sb("WQ", [P, 2, P])
        WK = sb("WK", [P, 2 * E])
        HLD = WK[0:E + 1, E:2 * E]
        WV = sb("WV", [P, HEADS, 32])
        F1 = sb("F1", [P, HEADS, D])
        F2 = sb("F2", [P, HEADS, D])
        FGW = sb("FGW", [E, HEADS])
        SEL = sb("SEL", [P, HEADS, SELC])
        R = sb("R", [P, HEADS, TILES, D])
        GB = sb("GB", [P, HEADS, EXPERTS])
        LNG = sb("LNG", [P, HEADS, D])
        LNB = sb("LNB", [P, HEADS, D])
        FNG = sb("FNG", [P, HEADS, D])
        FNB = sb("FNB", [P, HEADS, D])
        HALF = sb("HALF", [P, 2 * HEADS * TILES])
        NEG_HALF, POS_HALF = HALF[:, 0:HEADS * TILES], HALF[:, HEADS * TILES:]
        PS = ctx.enter_context(nc.psum_tensor("PS", [P, 8, BANK], F32))

        first = ExitStack()
        WT = sb("WT", [P, KCHUNKS, E], stack=first)
        TOKB = sb("TOKB", [E, 1], stack=first)
        WQKV = sb("WQKV", [E + 1, 3 * E], stack=first)
        WKV = sb("WKV", [P, 4 * E], stack=first)
        WOUT = sb("WOUT", [2 * E, E], stack=first)
        BOUT = sb("BOUT", [E + 1, E], stack=first)
        X = sb("X", [ROWS, CHANNELS, PATCH * IMAGE], stack=first)
        XR = sb("XR", [ROWS, 2, GRID, P], stack=first)
        XT = sb("XT", [P, 4, 4 * ROWS], stack=first)
        HT = sb("HT", [E, GROUP, PATCHES], stack=first)
        XC = sb("XC", [P, PAIR * TILES, E], stack=first)
        SQ = sb("SQ", [P, PAIR * TILES, E], stack=first)
        XN = sb("XN", [P, 2, PAIR * TILES, E], stack=first)
        K2 = sb("K2", [P, PAIR * TILES, E], stack=first)
        KV = sb("KV", [P, 2, PAIR * TILES, 2 * E], stack=first)
        TMP = sb("TMP", [P, PAIR * TILES, E], stack=first)
        XNT = sb("XNT", [P, PAIR, PADDED], stack=first)
        QS = sb("QS", [P, PAIR * TILES, E], stack=first)
        QF = sb("QF", [P, PAIR * TILES, E], stack=first)
        Q2T = sb("Q2T", [E, 2, PAIR, PADDED], stack=first)
        KVT = sb("KVT", [2 * E, PAIR, E], stack=first)
        KK = sb("KK", [E, PAIR, E], stack=first)
        KVW = sb("KVW", [E, PAIR, E], stack=first)
        ST = sb("ST", [P, 13, PAIR * TILES], stack=first)
        (MEAN, VAR, VARE, RSTD, K2S, RK, Q2S, Q4S, RQ, NQ, NQ2) = (ST[:, n, :] for n in range(11))
        FQ = [ST[:, 11 + n, :] for n in range(2)]
        SN = sb("SN", [E, 4, PAIR], stack=first)
        TOKW = sb("TOKW", [E, KCHUNKS * P], stack=first)
        HL = sb("HL", [HEADS * D, E + 1], stack=first)
        WQN = sb("WQN", [EXPERTS * D, HEADS, D], stack=first)
        WKN = sb("WKN", [D, HEADS, D], stack=first)
        WVN = sb("WVN", [D, HEADS, D], stack=first)
        GN = sb("GN", [HEADS * EXPERTS, EXPERTS, 32], stack=first)
        F1N = sb("F1N", [D, HEADS, D], stack=first)
        F2N = sb("F2N", [D, HEADS, D], stack=first)
        FGN = sb("FGN", [HEADS, E], stack=first)
        BQ = sb("BQ", [HEADS * D, HEADS, EXPERTS * D], stack=first)
        BKV = sb("BKV", [HEADS * D, 2, HEADS, D], stack=first)
        WVT = sb("WVT", [E, E + 1], stack=first)
        CM = sb("CM", [E + 1, 2, 1], stack=first)
        first.close()

        QA = [sb(f"QA{p}", [P, HEADS * EXPERTS, SEQ], BF16) for p in range(2)]
        KA = [sb(f"KA{p}", [P, HEADS, SEQ], BF16) for p in range(2)]
        PT = [sb(f"PT{j}", [P, EXPERTS, SEQ - j * P]) for j in range(TILES)]
        MT = [sb(f"MT{p}", [P, HEADS, SEQ], U8) for p in range(2)]
        VA = [sb(f"VA{p}", [P, TILES, HEADS, 32]) for p in range(2)]
        XFT = [sb(f"XFT{p}", [P, PADDED]) for p in range(2)]
        Q1 = sb("Q1", [P, 2, SEQ], BF16)
        Q2 = sb("Q2", [P, 2, SEQ], BF16)
        Q3 = sb("Q3", [P, 2, SEQ], BF16)
        QR = sb("QR", [P, SEQ])
        K1 = sb("K1", [E, SEQ], BF16)
        K2B = sb("K2B", [E, SEQ], BF16)
        K3 = sb("K3", [E, SEQ], BF16)
        MK = sb("MK", [P, SEQ], U8)
        OT = sb("OT", [P, PADDED])
        RAW = sb("RAW", [P, HEADS, TILES, SELC])
        NM = sb("NM", [P, TILES, HEADS * EXPERTS])
        NP = sb("NP", [P, 2, HEADS * EXPERTS])
        NR = sb("NR", [P, TILES, 8])
        NB = sb("NB", [P, 2, TILES, 3, 8], BF16)
        NT = [sb(f"NT{h}", [24, SEQ], BF16) for h in range(2)]
        AC = sb("AC", [P, TILES, E])
        AS = sb("AS", [P, TILES, E])
        AN = sb("AN", [P, TILES, E])
        GL = sb("GL", [P, HEADS * TILES, EXPERTS, EXPERTS])
        MIXP = sb("MIXP", [P, HEADS * TILES, EXPERTS, D])
        Y = sb("Y", [P, HEADS * TILES, D])
        YC = sb("YC", [P, HEADS * TILES, D])
        FX = sb("FX", [P, TILES, HEADS, D])
        FM = sb("FM", [P, TILES, HEADS, D], BF16)
        FO = sb("FO", [P, TILES, HEADS, D])
        OUT = sb("OUT", [P, TILES, E])
        FXT = sb("FXT", [P, PADDED])
        FMT = sb("FMT", [E, PADDED], BF16)
        HXT = sb("HXT", [P, PADDED])
        FOT = FXT[0:E, :]
        S4 = sb("S4", [P, 6, HEADS * TILES, EXPERTS])
        RD, LG, EG, W4 = (S4[:, n, :, :] for n in range(4))
        FL, FE = (S4[:, n, 0:TILES, :] for n in (4, 5))
        S1 = sb("S1", [P, 20, HEADS * TILES])

        def it_static(it):
            return it if isinstance(it, int) else None

        def schedule(eng, iteration):
            def run(it, p):
                t = it_static(it)
                known = t is not None
                iteration(it, p,
                          C=not known or 0 <= t < BATCH,
                          M=not known or 0 <= t + 1 < BATCH,
                          A=not known or 0 <= t + 2 < BATCH,
                          D1=not known or 0 <= t - 1 < BATCH,
                          prev_a=not known or 0 <= t + 1 < BATCH,
                          first=known and t < 1)
            for it in (-2, -1, 0, 1):
                run(it, it % 2)
            with eng.Fori(1, BATCH // 2 - 1) as k:
                run(k * 2, 0)
                run(k * 2 + 1, 1)
            for it in (BATCH - 2, BATCH - 1, BATCH):
                run(it, it % 2)

        WEIGHT_DMAS = 27

        def apart(eng):
            eng.sem_inc(S("apart"), 1)

        def done(eng, step, times):
            group, steps = STEPS[step]
            eng.wait_ge(S(group), (times - 1) * len(steps) + steps.index(step) + 1)

        def at_least(eng, name, value):
            if isinstance(value, int) and value <= 0:
                return
            if name in STEPS:
                done(eng, name, value)
            else:
                eng.wait_ge(S(name), value)

        def halves(width):
            return ((0, width // 2), (width // 2, width))

        T2_BANKS = (1, 7)
        S_BANKS, M_BANKS, PV_BANK, MISC = (0, 1), (2, 3, 4), 5, 7

        def ring_bank(banks, p, slot):
            return banks[(slot + (p if SLOTS % len(banks) else 0)) % len(banks)]

        def bank_left(banks, it, p, slot):
            ring = len(banks)
            if slot >= ring:
                return it * SLOTS + slot - ring + 1
            last = max(x for x in range(SLOTS) if ring_bank(banks, 1 - p, x) == ring_bank(banks, p, slot))
            return (it - 1) * SLOTS + last + 1

        def first_out(it):
            return isinstance(it, int) and it == 1

        PROJ_HALF = (2, 0, 1)
        OUT_LAG, NORM_LAG = 0, 8
        PROJ_AT = (22, 27, 39, 42, 65, 73)
        V_AT, TURN_AT, RESID_AT = (3, 5), (18, 20), 21
        DEN_AT, MIX_AT, Y_AT = 16, 31, 33
        FX_AT, FC1_AT, FC2_AT, Z_AT = (49, 50), (51, 54), 60, 63
        FO_AT, FG_AT = (76, 78), 82
        MAX0_AT, MAX1_AT = 56, 11
        CLEARS, WIDE_CLEARS = 13, 3

        def known_first_heads(b):
            return isinstance(b, int) and b < HEADS

        def txt_parts(g):
            yield 1, IMG_TAIL, 0, TXT_HEAD
            for t in range(2, TILES):
                yield t, 0, TXT_HEAD + (t - 2) * P, rows(t)

        block = ctx.enter_context(nc.Block())

        @block.sync
        def _(sp):
            n = 0

            def weight(dst, src):
                sp.dma_start(dst, src).then_inc(S("weights_in"), 16)
                return 1

            sp.wait_ge(S("weights_cleared"), 10)
            n += weight(CONST[:, :], a["const"])
            n += weight(TOKW[:, :], a["L0_tok_W"])
            n += weight(TOKB[:, :], a["L0_tok_b"].rearrange("(e o) -> e o", o=1))
            n += weight(WQKV[0:E, :], a["L0_attn_W_qkv"])
            n += weight(WQKV[E:E + 1, :], a["L0_attn_b_qkv"].rearrange("(o n) -> o n", o=1))
            for half in range(2):
                n += weight(WOUT[half * E:(half + 1) * E, :], a["L0_attn_W_out"])
            n += weight(BOUT[E:E + 1, :], a["L0_attn_b_out"].rearrange("(o n) -> o n", o=1))
            n += weight(HL[:, 0:E], a["L0_ffn_hl_w"].rearrange("n d h -> (n d) h"))
            n += weight(HL[:, E:E + 1], a["L0_ffn_hl_b"].rearrange("n (d o) -> (n d) o", o=1))
            n += weight(WQN[:, :, :], a["L0_ffn_wq"].rearrange("n e o d -> (e o) n d"))
            n += weight(WKN[:, :, :], a["L0_ffn_wk"].rearrange("n o d -> o n d"))
            n += weight(WVN[:, :, :], a["L0_ffn_wv"].rearrange("n o d -> o n d"))
            for e in range(EXPERTS):
                n += weight(GN[:, e, 0:D], a["L0_ffn_gate_w"].rearrange("n g (e d) -> (n g) e d", d=D)[:, e, :])
            for dst, name in ((F1, "fc1"), (F2, "fc2")):
                n += weight((F1N if dst is F1 else F2N)[:, :, :],
                            a[f"L0_ffn_{name}_w"].rearrange("o (n d) -> o n d", n=1).broadcast_to((D, HEADS, D)))
                n += weight(dst[E:E + 1, :, :],
                            a[f"L0_ffn_{name}_b"].rearrange("(a n d) -> a n d", a=1, n=1).broadcast_to((1, HEADS, D)))
            n += weight(FGN[:, :], a["L0_ffn_fgate_w"])
            n += weight(GB[:, :, :], a["L0_ffn_gate_b"].rearrange("(a n) e -> a n e", a=1).broadcast_to((P, HEADS, EXPERTS)))
            for dst, name in ((LNG, "ln_g"), (LNB, "ln_b"), (FNG, "fnorm_g"), (FNB, "fnorm_b")):
                n += weight(dst[:, :, :],
                            a[f"L0_ffn_{name}"].rearrange("(a n d) -> a n d", a=1, n=1).broadcast_to((P, HEADS, D)))
            assert n == WEIGHT_DMAS, n
            for g in range(BATCH // GROUP):
                for c in range(CHANNELS):
                    if g > 0:
                        sp.wait_ge(S("chunk"), (g - 1) * KCHUNKS + 2 * c + 2)
                    for b in range(GROUP):
                        sp.dma_start(X[b * GRID:(b + 1) * GRID, c, :],
                                     a["x"][g * GROUP + b, c, :, :].rearrange("(h p) w -> h (p w)", p=PATCH)
                                     ).then_inc(S(f"x_in{c}"), 16)
            def parts_in(b, p, half, first):
                h8, n2 = half * 8, half * 2
                sp.wait_ge(S("q3"), 6 * b + 2 * half + 4)
                if not first:
                    sp.wait_ge(S("scores"), (b - 2) * SLOTS + (half + 1) * SLOTS // 2)
                for r, (x, y) in enumerate(zip(Q_PARTS, K_PARTS)):
                    sp.dma_start(QA[p][r * D:(r + 1) * D, h8:h8 + 8, :], (Q1, Q2, Q3)[x - 1][:, half, :]
                                 ).then_inc(S(f"q_in{half}"), 16)
                for r, (x, y) in enumerate(zip(Q_PARTS, K_PARTS)):
                    sp.dma_start(KA[p][r * D:(r + 1) * D, n2:n2 + 2, :], (K1, K2B, K3)[y - 1][half * 32:half * 32 + 32, :]
                                 ).then_inc(S(f"k_in{half}"), 16)

            def max_in(b, p, half):
                sp.wait_ge(S("max_sbuf"), 2 * b + half + 1)
                sp.dma_start(QA[p][P - MROWS:P, half * 8:half * 8 + 8, :], NT[half][:, :]).then_inc(S(f"max_in{half}"), 16)

            def iteration(it, p, C, M, A, D1, prev_a, first):
                if prev_a:
                    parts_in(it + 1, 1 - p, 1, first)
                if C:
                    max_in(it, p, 1)
                if prev_a:
                    sp.wait_ge(S("cleared"), 7)
                    sp.wait_ge(S("pads"), 2 * (it + 1) + 2)
                    if not first:
                        sp.wait_ge(S("ot"), HEADS * it)
                    for e in range(EXPERTS):
                        sp.dma_start(MT[1 - p][32 * e:32 * e + D, :, :], MK[E:2 * E, :]).then_inc(S("pads_in"), 16)
                if A:
                    parts_in(it + 2, p, 0, it_static(it) in (-2, -1))
                if M:
                    max_in(it + 1, 1 - p, 0)
                if D1:
                    sp.wait_ge(S("out_made"), it)
                    b = it - 1
                    o = out[bass.ds(b, 1), :, :] if not isinstance(b, int) else out[b:b + 1, :, :]
                    sp.dma_start(o[:, 0:SEQ - TAIL, :].rearrange("o (t p) e -> p (o t) e", p=P), OUT[:, 0:TILES - 1, :]
                                 ).then_inc(S("out_dma"), 16)
                    sp.dma_start(o[:, SEQ - TAIL:SEQ, :].rearrange("o p e -> (o p) e"), OUT[0:TAIL, TILES - 1, :]
                                 ).then_inc(S("out_dma"), 16)

            schedule(sp, iteration)
            sp.wait_ge(S("out_dma"), 32 * BATCH)

        @block.gpsimd
        def _(pool):
            for n, (dst, value, name) in enumerate((
                    (GN[:, :, :], 0.0, "weights_cleared"), (BOUT[:, :], 0.0, "weights_cleared"), (WV[:, :, :], 0.0, "weights_cleared"),
                    (WQ[E:P, :, :], 0.0, "weights_cleared"), (WK[E:P, :], 0.0, "weights_cleared"), (WKV[E:P, :], 0.0, "weights_cleared"),
                    (F1[E:P, :, :], 0.0, "weights_cleared"), (F2[E:P, :, :], 0.0, "weights_cleared"),
                    (NEG_HALF, -0.5, "weights_cleared"), (POS_HALF, 0.5, "weights_cleared"))):
                pool.memset(dst, value).then_inc(S(name), 1)
                pool.wait_ge(S(name), n + 1)
            pool.memset(H[:, :, TILES - 1, :], 0.0).then_inc(S("tail_cleared"), 1)
            pool.wait_ge(S("tail_cleared"), 1)
            for n, (dst, value) in enumerate(((XNT[E:P, :, :], 0.0), (XNT[E:E + 1, :, :], 1.0), (ST[:, :, :], 0.0))):
                pool.memset(dst, value).then_inc(S("ones_row"), 1)
                pool.wait_ge(S("ones_row"), n + 1)

            for step in range(-1, PAIRS + 1):
                norm, mid, back = step + 1, step, step - 1
                if norm < PAIRS:
                    pool.wait_ge(S("var"), norm + 1)
                    pool.tensor_scalar(VARE, VAR, 1.0 / E, LN_EPS, ALU.mult, ALU.add).then_inc(S("var_eps"), 1)
                    pool.wait_ge(S("var_eps"), norm + 1)
                    pool.tensor_tensor(RSTD, VARE, NEG_HALF[:, 0:PAIR * TILES], ALU.pow).then_inc(S("rstd"), 1)
                    pool.wait_ge(S("rstd"), norm + 1)
                if 0 <= back:
                    pool.wait_ge(S("k_len2"), back + 1)
                    pool.tensor_tensor(SN[:, 1, :], SN[:, 0, :], POS_HALF[0:E, 0:PAIR], ALU.pow).then_inc(S("k_len"), 1)
                    pool.wait_ge(S("k_len"), back + 1)
                if 0 <= mid < PAIRS:
                    pool.wait_ge(S("q4s"), mid + 1)
                    pool.tensor_tensor(NQ, Q4S, POS_HALF[:, 0:PAIR * TILES], ALU.pow).then_inc(S("q_len"), 1)
                    pool.wait_ge(S("q_len"), mid + 1)

            pool.wait_ge(S("h2_done"), PAIRS)
            clears = [(XFT[0][E:P, :], 0.0), (XFT[0][E:E + 1, :], 1.0), (XFT[1][E:P, :], 0.0), (XFT[1][E:E + 1, :], 1.0), (NM[:, :, :], 0.0),
                      (MT[0][:, :, :], 1), (MT[1][:, :, :], 1), (OT[:, :], 1.0), (FXT[E:P, :], 0.0), (FXT[E:E + 1, :], 1.0),
                      (HXT[E:P, :], 0.0), (HXT[E:E + 1, :], 1.0), (QA[1][KDIM:P, :, :], 0.0)]
            assert len(clears) == CLEARS

            def clear(first, end):
                for n in range(first, end):
                    pool.memset(*clears[n]).then_inc(S("cleared"), 1)
                    pool.wait_ge(S("cleared"), n + 1)

            clear(0, 4)

            def iteration(it, p, C, M, A, D1, prev_a, first):
                def mask(b, n, j):
                    r = rows(j)
                    units = [u for u, x in enumerate(UNITS_S) if x[0] == j and x[1] == j * P]
                    pool.wait_ge(S("exped"), b * SLOTS + n * UNITS + max(units) + 1)
                    apart(pool)
                    pool.affine_select(out=PT[j][0:r, :, 0:r], in_=PT[j][0:r, :, 0:r], pattern=[[0, EXPERTS], [1, r]],
                                       compare_op=ALU.is_ge, fill=0.0, base=0, channel_multiplier=-1
                                       ).then_inc(S("masked"), 1)

                for slot in range(SLOTS):
                    if A:
                        b = it + 2
                        if slot == 8:
                            done(pool, "a_var", b + 1)
                            apart(pool)
                            pool.tensor_scalar(S1[:, 2, 0:TILES], S1[:, 1, 0:TILES], 1.0 / E, LN_EPS, ALU.mult, ALU.add
                                               ).then_inc(S("a_eps"), 1)
                            pool.wait_ge(S("a_eps"), b + 1)
                            pool.tensor_tensor(S1[:, 3, 0:TILES], S1[:, 2, 0:TILES], NEG_HALF[:, 0:TILES], ALU.pow
                                               ).then_inc(S("a_rstd"), 1)
                        if slot == 9 and it_static(it) == -2:
                            pool.wait_ge(S("a_rstd"), 1)
                            clear(4, CLEARS - 1)
                        if slot == 9 and it_static(it) == -1:
                            pool.wait_ge(S("a_rstd"), 2)
                            clear(CLEARS - 1, CLEARS)
                        for idx, at in enumerate(PROJ_AT):
                            if slot == at + OUT_LAG + 3:
                                half, c = PROJ_HALF[idx // 2], idx % 2
                                lo, hi = halves(SEQ)[c]
                                if half < 2:
                                    src, mid, low = QR[:, lo:hi], Q2[:, half, lo:hi], Q3[:, half, lo:hi]
                                else:
                                    src, mid, low = QR[0:E, lo:hi], K2B[:, lo:hi], K3[:, lo:hi]
                                pool.wait_ge(S("q_rest"), 6 * b + idx + 1)
                                apart(pool)
                                pool.tensor_scalar(mid, src, 1.0, 0.0, ALU.mult, ALU.add).then_inc(S("q2"), 1)
                                pool.wait_ge(S("q2"), 6 * b + idx + 1)
                                pool.tensor_tensor(low, src, mid, ALU.subtract).then_inc(S("q3"), 1)
                                if half == 2:
                                    pool.wait_ge(S("q3"), 6 * b + idx + 1)
                    if D1:
                        b = it - 1
                        if slot == DEN_AT + 1:
                            pool.wait_ge(S("raw"), HEADS * (b + 1))
                            done(pool, "den_rec", b + 1)
                            pool.tensor_tensor(GL[:, :, :, :], RAW[:, :, :, RAWC:SELC].rearrange("p n t (e g) -> p (n t) e g", e=EXPERTS),
                                               RD.rearrange("p k (e o) -> p k e o", o=1).broadcast_to((P, HEADS * TILES, EXPERTS, EXPERTS)),
                                               ALU.mult).then_inc(S("gate_parts"), 1)
                        for n in range(HEADS):
                            if slot == DEN_AT + 9 + n:
                                done(pool, "mix_w", b + 1)
                                k6 = slice(n * TILES, (n + 1) * TILES)
                                pool.tensor_tensor(MIXP[:, k6, :, :],
                                                   RAW[:, n, :, 0:RAWC].rearrange("p t (e c) -> p t e c", e=EXPERTS)[:, :, :, 0:D],
                                                   W4[:, k6, :].rearrange("p k (e o) -> p k e o", o=1).broadcast_to((P, TILES, EXPERTS, D)),
                                                   ALU.mult).then_inc(S("mixed"), 1)
                        for name, at, v in (("y", Y_AT + 4, 6), ("z", Z_AT + 4, 12)):
                            if slot == at:
                                done(pool, f"{name}_var", b + 1)
                                apart(pool)
                                pool.tensor_scalar(S1[:, v, :], S1[:, v - 1, :], 1.0 / D, INNER_EPS, ALU.mult, ALU.add
                                                   ).then_inc(S(f"{name}_eps"), 1)
                                pool.wait_ge(S(f"{name}_eps"), b + 1)
                                pool.tensor_tensor(S1[:, v + 1, :], S1[:, v, :], NEG_HALF, ALU.pow).then_inc(S(f"{name}_rstd"), 1)
                        if slot == SLOTS - 1:
                            done(pool, "fgate", b + 1)
                            if not first_out(it):
                                pool.wait_ge(S("out_dma"), 32 * b)
                            pool.tensor_tensor(OUT[:, :, :].rearrange("p t (n d) -> p (t n) d", n=HEADS),
                                               FO[:, :, :, :].rearrange("p t n d -> p (t n) d"),
                                               FE.rearrange("p t (n o) -> p (t n) o", o=1).broadcast_to((P, HEADS * TILES, D)),
                                               ALU.mult).then_inc(S("out_gated"), 1)
                            pool.wait_ge(S("out_gated"), b + 1)
                            pool.tensor_tensor(OUT[:, :, :], OUT[:, :, :], H[:, bass.ds(b, 1), :, :].rearrange("p o t e -> p (o t) e"),
                                               ALU.add).then_inc(S("out_made"), 1)
                    for n in range(-1, HEADS):
                        for j in range(TILES):
                            if slot == n * UNITS + LAST_UNIT[j] + MASK_LAG:
                                if n >= 0 and C:
                                    mask(it, n, j)
                                if n < 0 and D1:
                                    mask(it - 1, HEADS - 1, j)

            schedule(pool, iteration)

        @block.scalar
        def _(act):
            act.wait_ge(S("tail_cleared"), 1)
            for g in range(BATCH // GROUP):
                for t, p0, tok, n in txt_parts(g):
                    act.dma_start(H[p0:p0 + n, g * GROUP:(g + 1) * GROUP, t, :],
                                  a["txt"][g * GROUP:(g + 1) * GROUP, tok:tok + n, :].rearrange("b p e -> p b e")
                                  ).then_inc(S(f"txt_in{g}"), 16)

            for g in range(BATCH // GROUP):
                for u in range(0, 4 * KCHUNKS, 2):
                    act.wait_ge(S("xt_psum"), g * 4 * KCHUNKS + u + 1)
                    if u >= 4:
                        act.wait_ge(S("xt_read"), g * 4 * KCHUNKS + u - 4 + 1)
                    act.copy(XT[:, u % 4, :], PS[:, 4 + u % 4, 0:4 * ROWS]).then_inc(S("xt_sbuf_act"), 1)
                act.wait_ge(S("xt_read"), (g + 1) * 4 * KCHUNKS)
                for w in range(2):
                    act.activation(HT[:, :, :].rearrange("e b (h w) -> e w (b h)", w=GRID)[:, 4 * w:4 * w + 4, :],
                                   PS[0:E, w, 0:4 * ROWS].rearrange("e (w r) -> e w r", w=4),
                                   ACT.Identity, bias=TOKB[:, 0:1]).then_inc(S("ht"), 1)
                for q in range(GROUP // QUAD):
                    b0 = g * GROUP + q * QUAD
                    act.wait_ge(S("img_tokens"), g * (GROUP // QUAD) + q + 1)
                    act.copy(H[:, b0:b0 + QUAD, 0, :], PS[:, 6 + q, 0:QUAD * E].rearrange("p (b e) -> p b e", b=QUAD)
                             ).then_inc(S("img_in_h"), 1)
                    act.copy(H[0:IMG_TAIL, b0:b0 + QUAD, 1, :],
                             PS[0:IMG_TAIL, 6 + q, QUAD * E:2 * QUAD * E].rearrange("p (b e) -> p b e", b=QUAD)
                             ).then_inc(S("img_in_h"), 1)

            def two_banks(bank):
                return PS[0:E, bank:bank + 2, :].rearrange("e a n -> e (a n)")[:, 0:PADDED]

            def kv_part(part):
                return PS[:, 4:7, :].rearrange("p a (t n) -> p a t n", t=2)[:, :, :, part * E:(part + 1) * E]

            def of_batch(x, b):
                return x[:, b * TILES:(b + 1) * TILES, :].rearrange("p (a t) e -> p a t e", a=3)

            for step in range(-1, PAIRS + 1):
                norm, mid, back = step + 1, step, step - 1
                q = step % 2
                for b in range(PAIR):
                    if 0 <= mid < PAIRS:
                        n = mid * PAIR + b
                        act.wait_ge(S("xnt_psum"), n + 1)
                        at_least(act, "kv_psum", n - PAIR + 1)
                        act.copy(XNT[0:E, b, :], two_banks(0)).then_inc(S("xnt"), 1)
                    if b == 0 and norm < PAIRS:
                        act.wait_ge(S("centred"), norm + 1)
                        act.activation(SQ[:, :, :], XC[:, :, :], ACT.Square).then_inc(S("squared"), 1)
                    if b == 1 and 0 <= back:
                        act.wait_ge(S("kvt_psum"), back + 1)
                        at_least(act, "kvw_psum", back)
                        act.copy(KVT[E:2 * E, :, :], PS[E:2 * E, 7, 0:PAIR * E].rearrange("p (b e) -> p b e", b=PAIR)).then_inc(S("kvt"), 1)
                    if 0 <= mid < PAIRS:
                        at_least(act, "kn", mid)
                        at_least(act, "kvt_psum", mid - 1)
                        act.wait_ge(S("kv_psum"), n + 1)
                        act.activation(of_batch(K2, b), kv_part(0), ACT.Square).then_inc(S("k2"), 1)
                        act.copy(of_batch(KV[:, q, :, E:2 * E], b), kv_part(1)).then_inc(S("v"), 1)
                        at_least(act, "q2s", mid)
                        at_least(act, "q2t_psum", n - PAIR + 1)
                        act.activation(of_batch(QS, b), kv_part(3), ACT.Square).then_inc(S("q_squared"), 1)
                if 0 <= mid < PAIRS:
                    for b in range(PAIR):
                        n = mid * PAIR + b
                        act.wait_ge(S("q2t_psum"), n + 1)
                        at_least(act, "t2_psum", n - 2 * PAIR + 1)
                        act.copy(Q2T[:, q, b, :], two_banks(2)).then_inc(S("q2t"), 1)
                        if b == 0:
                            act.wait_ge(S("q_squared"), PAIR * (mid + 1))
                            at_least(act, "q4s", mid)
                            act.activation(QF[:, :, :], QS[:, :, :], ACT.Square).then_inc(S("q4"), 1)

            act.wait_ge(S("h2_done"), PAIRS)

            def iteration(it, p, C, M, A, D1, prev_a, first):
                def exponentials(slot):
                    n, u = divmod(slot, UNITS)
                    j, lo, w, e0, ne = UNITS_S[u]
                    count = it * SLOTS + slot
                    r = rows(j)
                    act.wait_ge(S("scores"), count + 1)
                    if UNITS_S[u - 1][0] != j or u == 0:
                        at_least(act, "summed", (it * HEADS + n - 1) * TILES + j + 1)
                    act.activation(PT[j][0:r, e0:e0 + ne, lo - j * P:lo - j * P + w],
                                   PS[0:r, ring_bank(S_BANKS, p, slot), 0:ne * w].rearrange("p (e w) -> p e w", e=ne),
                                   ACT.Exp).then_inc(S("exped"), 1)

                def raw(b, n):
                    act.wait_ge(S("raw_psum"), b * HEADS + n + 1)
                    if n == 0:
                        at_least(act, "mixed", HEADS * b)
                    act.copy(RAW[:, n, :, :], PS[:, 7, 0:TILES * SELC].rearrange("p (t c) -> p t c", t=TILES)).then_inc(S("raw"), 1)

                def maxima(b, half):
                    act.wait_ge(S("max_psum"), 2 * b + half + 1)
                    at_least(act, f"max_in{half}", 16 * b)
                    act.copy(NT[half][:, :], PS[0:24, 7, 0:SEQ // 2].bitcast(BF16)).then_inc(S("max_sbuf"), 1)

                for slot in range(SLOTS):
                    if C:
                        exponentials(slot)
                    if slot == MAX1_AT + OUT_LAG and C:
                        maxima(it, 1)
                    if slot == MAX0_AT + OUT_LAG and M:
                        maxima(it + 1, 0)
                    if D1 and slot == SEL_AT + 1 + OUT_LAG + 3 * UNITS - SLOTS:
                        raw(it - 1, HEADS - 1)
                    for n in range(HEADS - 1):
                        if C and slot == SEL_AT + 1 + OUT_LAG + n * UNITS:
                            raw(it, n)
                    if A:
                        b = it + 2
                        if slot == 4:
                            done(act, "a_centred", b + 1)
                            act.activation(AS[:, :, :], AC[:, :, :], ACT.Square).then_inc(S("a_squared"), 1)
                        for c, at in enumerate(TURN_AT):
                            if slot == at + OUT_LAG:
                                lo, hi = halves(PADDED)[c]
                                act.wait_ge(S("xft_psum"), 2 * b + c + 1)
                                act.copy(XFT[p][0:E, lo:hi], PS[0:E, 7, 0:hi - lo]).then_inc(S("xft"), 1)
                        if slot == RESID_AT + OUT_LAG and known_first_heads(b):
                            act.wait_ge(S("resid_psum"), b + 1)
                            act.copy(R[:, b, :, :], PS[:, MISC, 0:TILES * D].rearrange("p (t d) -> p t d", t=TILES)).then_inc(S("resid"), 1)
                        for idx, at in enumerate(PROJ_AT):
                            if slot == at + OUT_LAG:
                                half, c = PROJ_HALF[idx // 2], idx % 2
                                lo, hi = halves(SEQ)[c]
                                act.wait_ge(S("proj"), 6 * b + idx + 1)
                                at_least(act, "q3", 6 * b + idx - 1)
                                if half == 0:
                                    act.wait_ge(S("pads"), 2 * b + c + 1)
                                act.copy(QR[:, lo:hi], PS[:, MISC, 0:hi - lo]).then_inc(S("q_out"), 1)
                            if slot == at + OUT_LAG + 1:
                                half, c = PROJ_HALF[idx // 2], idx % 2
                                lo, hi = halves(SEQ)[c]
                                if c == 0 and half < 2:
                                    at_least(act, f"q_in{half}", 16 * PARTS * b)
                                if c == 0 and half == 2:
                                    at_least(act, "k_in0", 16 * PARTS * b)
                                    at_least(act, "k_in1", 16 * PARTS * b)
                                dst, src = (Q1[:, half, lo:hi], QR[:, lo:hi]) if half < 2 else (K1[:, lo:hi], QR[0:E, lo:hi])
                                act.wait_ge(S("q_out"), 6 * b + idx + 1)
                                act.copy(dst, src).then_inc(S("q1"), 1)
                    if M:
                        for c, at in enumerate(V_AT):
                            if slot == at + OUT_LAG:
                                b = it + 1
                                t0, t1 = ((0, TILES // 2), (TILES // 2, TILES))[c]
                                act.wait_ge(S("v_psum"), 2 * b + c + 1)
                                act.copy(VA[1 - p][:, t0:t1, :, :],
                                         PS[:, 7, 0:(t1 - t0) * P].rearrange("p (t n c) -> p t n c", t=t1 - t0, n=HEADS)
                                         ).then_inc(S("va"), 1)
                    if D1:
                        b = it - 1
                        if slot == DEN_AT + 5:
                            done(act, "gate_sub", b + 1)
                            act.activation(EG, LG, ACT.Exp).then_inc(S("gate_exp"), 1)
                        for name, at in (("y", Y_AT + 2), ("z", Z_AT + 2)):
                            if slot == at:
                                done(act, f"{name}_centred", b + 1)
                                act.activation(GL[:, :, :, :].rearrange("p k e g -> p k (e g)"), YC[:, :, :], ACT.Square
                                               ).then_inc(S(f"{name}_squared"), 1)
                        for c, at in enumerate(FX_AT):
                            if slot == at + OUT_LAG:
                                lo, hi = halves(PADDED)[c]
                                act.wait_ge(S("fxt_psum"), 2 * b + c + 1)
                                act.copy(FXT[0:E, lo:hi], PS[0:E, 7, 0:hi - lo]).then_inc(S("fxt"), 1)
                        for c, at in enumerate(FO_AT):
                            if slot == at + OUT_LAG:
                                lo, hi = halves(PADDED)[c]
                                act.wait_ge(S("fot_psum"), 2 * b + c + 1)
                                act.copy(FOT[:, lo:hi], PS[0:E, 7, 0:hi - lo]).then_inc(S("fot"), 1)
                        if slot == FG_AT + 2:
                            done(act, "fg_sub", b + 1)
                            act.activation(FE, FL, ACT.Exp).then_inc(S("fg_exp"), 1)

            schedule(act, iteration)

        @block.vector
        def _(dve):
            def stage(ins, name):
                ins.then_inc(S(STEPS[name][0] if name in STEPS else name), 1)

            dve.wait_ge(S("weights_in"), 16 * WEIGHT_DMAS)
            dve.tensor_copy(IDB[:, :], IDENT).then_inc(S("w_forms"), 1)
            dve.tensor_copy(MASKB[:, :], CONST[:, C_MASK:C_MASK + P]).then_inc(S("w_forms"), 1)
            dve.reduce_sum(CM[:, :, 0], WQKV[:, 0:2 * E].rearrange("p (a e) -> p a e", a=2), AX.X).then_inc(S("w_mean"), 1)
            dve.wait_ge(S("w_mean"), 1)
            dve.tensor_scalar(CM[:, :, 0], CM[:, :, 0], 1.0 / E, None, ALU.mult).then_inc(S("w_mean"), 1)
            dve.wait_ge(S("w_mean"), 2)
            dve.tensor_tensor(WKV[0:E + 1, 3 * E:4 * E], WQKV[:, 0:E], CM[:, 0, :].broadcast_to((E + 1, E)), ALU.subtract).then_inc(S("w_forms"), 1)
            dve.tensor_tensor(WKV[0:E + 1, 0:E], WQKV[:, E:2 * E], CM[:, 1, :].broadcast_to((E + 1, E)), ALU.subtract).then_inc(S("w_forms"), 1)
            dve.tensor_copy(WKV[0:E + 1, E:2 * E], WQKV[:, 2 * E:3 * E]).then_inc(S("w_forms"), 1)
            dve.wait_ge(S("w_turned"), 1)
            dve.tensor_copy(WT[:, :, :], PS[:, 0, 0:KCHUNKS * E].rearrange("p (k e) -> p k e", k=KCHUNKS)).then_inc(S("w_forms"), 1)
            dve.tensor_copy(HLT[:, :], PS[0:E + 1, 1, 0:E]).then_inc(S("w_forms"), 1)
            dve.tensor_copy(HLD.rearrange("p (d n) -> p n d", n=HEADS),
                            PS[0:E + 1, 1, 0:E].rearrange("p (n d) -> p n d", n=HEADS)).then_inc(S("w_forms"), 1)
            bd = BD.rearrange("p (n o) -> p n o", o=1)
            dve.tensor_tensor(BQ[:, :, :], PS[0:E, 1, 64:128].rearrange("p (n c) -> p n c", n=1).broadcast_to((E, HEADS, E)),
                              bd.broadcast_to((E, HEADS, E)), ALU.mult).then_inc(S("w_forms"), 1)
            for dst, at in ((BKV[:, 0, :, :], 128), (BKV[:, 1, :, :], 144), (F1[0:E, :, :], 176), (F2[0:E, :, :], 192)):
                dve.tensor_tensor(dst, PS[0:E, 1, at:at + D].rearrange("p (n c) -> p n c", n=1).broadcast_to((E, HEADS, D)),
                                  bd.broadcast_to((E, HEADS, D)), ALU.mult).then_inc(S("w_forms"), 1)
            dve.tensor_copy(FGW[:, :], PS[0:E, 1, 208:212]).then_inc(S("w_forms"), 1)
            dve.tensor_copy(WVT[:, :], PS[0:E, 1, 256:256 + E + 1]).then_inc(S("w_forms"), 1)
            for n in range(HEADS):
                dve.tensor_copy(SEL[:, n, 0:RAWC], CONST[:, C_SEL:C_SEL + RAWC]).then_inc(S("w_forms"), 1)
                dve.tensor_tensor(SEL[:, n, RAWC:SELC].rearrange("p (e g) -> p e g", e=EXPERTS),
                                  PS[:, 1, 160 + n * EXPERTS:160 + (n + 1) * EXPERTS].rearrange("p (e g) -> p e g", e=1)
                                  .broadcast_to((P, EXPERTS, EXPERTS)),
                                  BDE.rearrange("p (e g) -> p e g", g=1).broadcast_to((P, EXPERTS, EXPERTS)),
                                  ALU.mult).then_inc(S("w_forms"), 1)
            dve.wait_ge(S("w_made"), 1)
            for half in range(2):
                dve.tensor_scalar(WQ[0:E + 1, half, :].rearrange("p (o h) -> p h o", o=D),
                                  PS[0:E + 1, 2, half * P:(half + 1) * P].rearrange("p (h o) -> p h o", o=D),
                                  float(D) ** 0.5, None, ALU.mult).then_inc(S("w_forms"), 1)
                dve.tensor_copy(WK[0:E + 1, half * 32:half * 32 + 32].rearrange("p (o n) -> p n o", n=2),
                                PS[0:E + 1, 2, 256 + half * 32:256 + half * 32 + 32].rearrange("p (n o) -> p n o", n=2)
                                ).then_inc(S("w_forms"), 1)
            dve.tensor_copy(WV[0:E + 1, :, 0:D], PS[0:E + 1, 2, 320:384].rearrange("p (n d) -> p n d", n=HEADS)).then_inc(S("w_forms"), 1)
            dve.memset(WV[E:E + 1, :, D:D + 1], 1.0).then_inc(S("w_forms"), 1)
            dve.tensor_tensor(WKV[0:E + 1, 2 * E:3 * E], PS[0:E + 1, 3, 0:E], BOUT[:, :], ALU.add).then_inc(S("w_ready"), 1)

            def bc(x):
                return x.rearrange("p (n o) -> p n o", o=1).broadcast_to((P, PAIR * TILES, E))

            for g in range(BATCH // GROUP):
                def cut(g, chunk):
                    c, half = divmod(chunk, 2)
                    if half == 0:
                        dve.wait_ge(S(f"x_in{c}"), 16 * GROUP * (g + 1))
                    at_least(dve, "xt_psum", g * 4 * KCHUNKS + 4 * (chunk - 1))
                    x = X[:, c, :].rearrange("r (p w x) -> r w p x", p=PATCH, w=GRID)
                    dve.tensor_copy(XR[:, chunk % 2, :, :].rearrange("r w (p x) -> r w p x", p=8),
                                         x[:, :, half * 8:half * 8 + 8, :]).then_inc(S("chunk"), 1)

                if g == 0:
                    cut(g, 0)
                for u in range(1, 4 * KCHUNKS, 2):
                    if u % 4 == 1 and u // 4 + 1 < KCHUNKS:
                        cut(g, u // 4 + 1)
                    dve.wait_ge(S("xt_psum"), g * 4 * KCHUNKS + u + 1)
                    if u >= 4:
                        dve.wait_ge(S("xt_read"), g * 4 * KCHUNKS + u - 4 + 1)
                    n = (4 if u % 4 < 3 else 2) * ROWS
                    dve.tensor_copy(XT[:, u % 4, 0:n], PS[:, 4 + u % 4, 0:n]).then_inc(S("xt_sbuf_dve"), 1)
                if g + 1 < BATCH // GROUP:
                    cut(g + 1, 0)
                dve.wait_ge(S("xt_read"), (g + 1) * 4 * KCHUNKS)
                for w, n in ((2, 4), (3, 2)):
                    dve.tensor_scalar(HT[:, :, :].rearrange("e b (h w) -> e w (b h)", w=GRID)[:, 4 * w:4 * w + n, :],
                                      PS[0:E, w, 0:n * ROWS].rearrange("e (w r) -> e w r", w=n),
                                      TOKB[:, 0:1], None, ALU.add).then_inc(S("ht"), 1)

            def pair(i):
                return H[:, i * PAIR:(i + 1) * PAIR, :, :].rearrange("p b t e -> p (b t) e")

            def tokens_and_v(n):
                dve.wait_ge(S("kv_psum"), n + 1)
                dve.wait_ge(S("q_squared"), n + 1)
                h = H[:, n:n + 1, :, :].rearrange("p b (a t) e -> p (b a) t e", a=3)
                stage(dve.tensor_tensor(h, PS[:, 4:7, :].rearrange("p a (t n) -> p a t n", t=2)[:, :, :, 2 * E:3 * E],
                                        h, ALU.add), "h_vo")

            def attention_out(n):
                i, b = divmod(n, PAIR)
                dve.wait_ge(S("fq"), i + 1)
                dve.wait_ge(S("t2_psum"), n + 1)
                t6 = slice(b * TILES, (b + 1) * TILES)
                stage(dve.tensor_tensor(TMP[:, t6, :], PS[:, T2_BANKS[b], 0:TILES * E].rearrange("p (t n) -> p t n", t=TILES),
                                        FQ[i % 2][:, t6].rearrange("p (n o) -> p n o", o=1).broadcast_to((P, TILES, E)),
                                        ALU.mult), "t2")

            for g in range(BATCH // GROUP):
                dve.wait_ge(S(f"txt_in{g}"), 16 * (TILES - 1))
            for step in range(-1, PAIRS + 1):
                norm, mid, back = step + 1, step, step - 1
                NORM, MID, BACK = norm < PAIRS, 0 <= mid < PAIRS, 0 <= back
                q = step % 2
                if NORM:
                    dve.wait_ge(S("img_in_h"), 2 * (norm * PAIR // QUAD + 1))
                    stage(dve.reduce_sum(MEAN, pair(norm), AX.X), "sum")
                    dve.wait_ge(S("sum"), norm + 1)
                    stage(dve.tensor_scalar(MEAN, MEAN, 1.0 / E, None, ALU.mult), "mean")
                    dve.wait_ge(S("mean"), norm + 1)
                    stage(dve.tensor_tensor(XC[:, :, :], pair(norm), bc(MEAN), ALU.subtract), "centred")
                if NORM:
                    dve.wait_ge(S("squared"), norm + 1)
                    stage(dve.reduce_sum(VAR, SQ[:, :, :], AX.X), "var")
                if MID:
                    tokens_and_v(mid * PAIR)
                if BACK:
                    dve.wait_ge(S("kvt_psum"), back + 1)
                    dve.wait_ge(S("kvt"), back + 1)
                    stage(dve.tensor_tensor(KK[:, :, :], PS[0:E, 7, 0:PAIR * E].rearrange("p (b e) -> p b e", b=PAIR),
                                            IDENT[0:E, 0:E].rearrange("p (b e) -> p b e", b=1).broadcast_to((E, PAIR, E)), ALU.mult), "kk")
                    dve.wait_ge(S("kk"), back + 1)
                    stage(dve.reduce_sum(SN[:, 0, :], KK[:, :, :], AX.X), "k_len2")
                if NORM:
                    dve.wait_ge(S("rstd"), norm + 1)
                    at_least(dve, "xnt_psum", PAIR * (norm - 1))
                    stage(dve.tensor_tensor(XN[:, 1 - q, :, :], XC[:, :, :], bc(RSTD), ALU.mult), "xn")
                if BACK:
                    dve.wait_ge(S("k_len"), back + 1)
                    stage(dve.tensor_scalar(SN[:, 2, :], SN[:, 1, :], NORM_EPS, float(SEQ) ** 0.5, ALU.max, ALU.mult), "k_len_max")
                    dve.wait_ge(S("k_len_max"), back + 1)
                    stage(dve.reciprocal(SN[:, 3, :], SN[:, 2, :]), "k_scale")
                if BACK:
                    dve.wait_ge(S("k_scale"), back + 1)
                    dve.wait_ge(S("kvw_psum"), back + 1)
                    at_least(dve, "t2_psum", PAIR * back)
                    stage(dve.tensor_tensor(KVW[:, :, :], PS[0:E, 7, 256:256 + PAIR * E].rearrange("p (b e) -> p b e", b=PAIR),
                                            SN[:, 3, :].rearrange("p (b o) -> p b o", o=1).broadcast_to((E, PAIR, E)),
                                            ALU.mult), "kvw")
                if MID:
                    tokens_and_v(mid * PAIR + 1)
                    dve.wait_ge(S("k2"), PAIR * (mid + 1))
                    stage(dve.reduce_sum(K2S, K2[:, :, :], AX.X), "k2s")
                    dve.wait_ge(S("k2s"), mid + 1)
                    stage(dve.tensor_scalar(K2S, K2S, DIV_EPS, None, ALU.add), "k2s_eps")
                    dve.wait_ge(S("k2s_eps"), mid + 1)
                    stage(dve.reciprocal(RK, K2S), "rk")
                    dve.wait_ge(S("rk"), mid + 1)
                    at_least(dve, "kvt_psum", mid - 1)
                    stage(dve.tensor_tensor(KV[:, q, :, 0:E], K2[:, :, :], bc(RK), ALU.mult), "kn")
                if BACK:
                    attention_out(back * PAIR)
                if MID:
                    dve.wait_ge(S("q4"), mid + 1)
                    stage(dve.reduce_sum(Q4S, QF[:, :, :], AX.X), "q4s")
                if BACK:
                    attention_out(back * PAIR + 1)
                if MID:
                    stage(dve.reduce_sum(Q2S, QS[:, :, :], AX.X), "q2s")
                    dve.wait_ge(S("q2s"), mid + 1)
                    stage(dve.tensor_scalar(Q2S, Q2S, DIV_EPS, None, ALU.add), "q2s_eps")
                    dve.wait_ge(S("q2s_eps"), mid + 1)
                    stage(dve.reciprocal(RQ, Q2S), "rq")
                    dve.wait_ge(S("q_len"), mid + 1)
                    dve.wait_ge(S("rq"), mid + 1)
                    stage(dve.tensor_tensor(NQ2, NQ, RQ, ALU.mult), "nq")
                    dve.wait_ge(S("nq"), mid + 1)
                    stage(dve.tensor_scalar(NQ2, NQ2, NORM_EPS, None, ALU.max), "nq_max")
                    dve.wait_ge(S("nq_max"), mid + 1)
                    stage(dve.reciprocal(FQ[q], NQ2), "nq_rec")
                    dve.wait_ge(S("nq_rec"), mid + 1)
                    stage(dve.tensor_tensor(FQ[q], FQ[q], RQ, ALU.mult), "fq")
                if BACK:
                    dve.wait_ge(S("t2"), PAIR * (back + 1))
                    dve.wait_ge(S("h_vo"), PAIR * (back + 1))
                    stage(dve.tensor_tensor(pair(back), pair(back), TMP[:, :, :], ALU.add), "h2_done")

            dve.wait_ge(S("h2_done"), PAIRS)

            def iteration(it, p, C, M, A, D1, prev_a, first):
                def maximum(b, slot):
                    n, u = divmod(slot, UNITS)
                    i, lo, w, e0, ne = UNITS_M[u]
                    r = query_tile(i)[1]
                    heads = slice(n * EXPERTS + e0, n * EXPERTS + e0 + ne)
                    dst = NM[0:r, i, heads] if lo == 0 else NP[0:r, i - (TILES - 2), heads]
                    dve.wait_ge(S("max_scores"), b * SLOTS + slot + 1)
                    dve.tensor_reduce(dst, PS[0:r, ring_bank(M_BANKS, 1 - p, slot), 0:ne * w].rearrange("p (e w) -> p e w", e=ne), AX.X, ALU.max,
                                      negate=True).then_inc(S("maxed"), 1)

                def split_maxima(b, half, step):
                    h8 = slice(half * 8, half * 8 + 8)
                    count = 2 * b + half + 1
                    if step == 0:
                        dve.wait_ge(S("maxed"), b * SLOTS + (half + 1) * SLOTS // 2)
                        stage(dve.tensor_tensor(NM[:, TILES - 2:TILES, h8], NM[:, TILES - 2:TILES, h8], NP[:, :, h8], ALU.min), "max_whole")
                    if step == 1:
                        done(dve, "max_whole", count)
                        at_least(dve, "max_psum", count - 2)
                        stage(dve.tensor_copy(NB[:, half, :, 0, :], NM[:, :, h8]), "max1")
                    if step == 2:
                        done(dve, "max1", count)
                        stage(dve.tensor_tensor(NR[:, :, :], NM[:, :, h8], NB[:, half, :, 0, :], ALU.subtract), "max_rest")
                    if step == 3:
                        done(dve, "max_rest", count)
                        stage(dve.tensor_copy(NB[:, half, :, 1, :], NR[:, :, :]), "max2")
                    if step == 4:
                        done(dve, "max2", count)
                        stage(dve.tensor_tensor(NB[:, half, :, 2, :], NR[:, :, :], NB[:, half, :, 1, :], ALU.subtract), "max3")

                def sums(b, n, q):
                    dve.wait_ge(S("summed"), (b * HEADS + n + 1) * TILES)
                    dve.wait_ge(S("pads_in"), 16 * EXPERTS * (b + 1))
                    at_least(dve, "raw_psum", b * HEADS + n)
                    stage(dve.tensor_tensor(OT[:, 0:SEQ], PS[:, PV_BANK:PV_BANK + 2, :].rearrange("p a w -> p (a w)")[:, 0:SEQ],
                                            MT[q][:, n, :], ALU.mult), "ot")

                def inner_norm(name, b, slot, at, src, v, gain, bias, dst):
                    k24 = HEADS * TILES
                    s1 = lambda x: S1[:, x, :].rearrange("p (k o) -> p k o", o=1).broadcast_to((P, k24, D))
                    if slot == at:
                        done(dve, f"{name}_in", b + 1)
                        stage(dve.reduce_sum(S1[:, v - 3, :], src, AX.X), f"{name}_sum")
                    if slot == at:
                        done(dve, f"{name}_sum", b + 1)
                        stage(dve.tensor_scalar(S1[:, v - 2, :], S1[:, v - 3, :], 1.0 / D, None, ALU.mult), f"{name}_mean")
                    if slot == at + 1:
                        done(dve, f"{name}_mean", b + 1)
                        stage(dve.tensor_tensor(YC[:, :, :], src, s1(v - 2), ALU.subtract), f"{name}_centred")
                    if slot == at + 3:
                        dve.wait_ge(S(f"{name}_squared"), b + 1)
                        stage(dve.reduce_sum(S1[:, v - 1, :], GL[:, :, :, :].rearrange("p k e g -> p k (e g)"), AX.X), f"{name}_var")
                    if slot == at + NORM_LAG:
                        dve.wait_ge(S(f"{name}_rstd"), b + 1)
                        stage(dve.tensor_tensor(YC[:, :, :], YC[:, :, :], s1(v + 1), ALU.mult), f"{name}_norm")
                    if slot == at + NORM_LAG + 1:
                        done(dve, f"{name}_norm", b + 1)
                        stage(dve.tensor_tensor(YC[:, :, :], YC[:, :, :], gain[:, 0:1, :].broadcast_to((P, k24, D)), ALU.mult), f"{name}_gain")
                    if slot == at + NORM_LAG + 2:
                        done(dve, f"{name}_gain", b + 1)
                        stage(dve.tensor_tensor(dst, YC[:, :, :] if name == "z" else YC[:, :, :].rearrange("p (n t) d -> p n t d", n=HEADS),
                                                bias[:, 0:1, :].broadcast_to((P, k24, D)) if name == "z" else
                                                bias[:, 0:1, :].rearrange("p o (t d) -> p o t d", t=1).broadcast_to((P, HEADS, TILES, D)),
                                                ALU.add), f"{name}_out")

                for slot in range(SLOTS):
                    if it_static(it) == -2:
                        for at, dst, value in ((10, KA[0][KDIM:P, :, :], 1.0), (11, QA[0][KDIM:P, :, :], 0.0), (80, KA[1][KDIM:P, :, :], 1.0)):
                            if slot == at:
                                dve.memset(dst, value).then_inc(S("wide_cleared"), 1)
                    if M:
                        if slot == 0:
                            dve.wait_ge(S("cleared"), 5)
                        maximum(it + 1, slot)
                        if SLOTS // 2 <= slot < SLOTS // 2 + 5:
                            split_maxima(it + 1, 0, slot - SLOTS // 2)
                    if C and slot < 5:
                        split_maxima(it, 1, slot)
                    if D1 and slot == OT_AT + 3 * UNITS - SLOTS:
                        sums(it - 1, HEADS - 1, 1 - p)
                    for n in range(HEADS - 1):
                        if C and slot == OT_AT + n * UNITS:
                            sums(it, n, p)
                    if A:
                        b = it + 2
                        h = H[:, bass.ds(b, 1), :, :].rearrange("p o t e -> p (o t) e")
                        s1 = lambda x: S1[:, x, 0:TILES].rearrange("p (t o) -> p t o", o=1).broadcast_to((P, TILES, E))
                        if slot == 1:
                            stage(dve.reduce_sum(S1[:, 0, 0:TILES], h, AX.X), "a_sum")
                        if slot == 2:
                            done(dve, "a_sum", b + 1)
                            stage(dve.tensor_scalar(S1[:, 16, 0:TILES], S1[:, 0, 0:TILES], 1.0 / E, None, ALU.mult), "a_mean")
                        if slot == 3:
                            done(dve, "a_mean", b + 1)
                            stage(dve.tensor_tensor(AC[:, :, :], h, s1(16), ALU.subtract), "a_centred")
                        if slot == 6:
                            dve.wait_ge(S("a_squared"), b + 1)
                            stage(dve.reduce_sum(S1[:, 1, 0:TILES], AS[:, :, :], AX.X), "a_var")
                        if slot == 9:
                            dve.wait_ge(S("a_rstd"), b + 1)
                            stage(dve.tensor_tensor(AN[:, :, :], AC[:, :, :], s1(3), ALU.mult), "a_norm")
                        for idx, at in enumerate(PROJ_AT):
                            if slot == at + OUT_LAG + 2:
                                half, c = PROJ_HALF[idx // 2], idx % 2
                                lo, hi = halves(SEQ)[c]
                                r = P if half < 2 else E
                                top = Q1[:, half, lo:hi] if half < 2 else K1[:, lo:hi]
                                dve.wait_ge(S("q1"), 6 * b + idx + 1)
                                stage(dve.tensor_tensor(QR[0:r, lo:hi], QR[0:r, lo:hi], top, ALU.subtract), "q_rest")
                        for c, at in enumerate(PROJ_AT[:2]):
                            if slot == at + OUT_LAG + 3:
                                lo, hi = halves(SEQ)[c]
                                at_least(dve, "pads_in", 16 * EXPERTS * b)
                                stage(dve.tensor_scalar(MK[E:2 * E, lo:hi], QR[E:2 * E, lo:hi], 0.0, None, ALU.not_equal), "pads")
                    if D1:
                        b = it - 1
                        k24 = HEADS * TILES
                        bc4 = lambda x: S1[:, x, :].rearrange("p (k o) -> p k o", o=1).broadcast_to((P, k24, EXPERTS))
                        if slot == DEN_AT:
                            dve.wait_ge(S("raw"), HEADS * (b + 1))
                            stage(dve.reciprocal(RD, RAW[:, :, :, 0:RAWC].rearrange("p n t (e c) -> p (n t) e c", e=EXPERTS)[:, :, :, D]), "den_rec")
                        if slot == DEN_AT + 3:
                            dve.wait_ge(S("gate_parts"), b + 1)
                            stage(dve.reduce_sum(LG, GL[:, :, :, :].rearrange("p k e g -> p k g e"), AX.X), "gate_logits")
                        if slot == DEN_AT + 3:
                            done(dve, "gate_logits", b + 1)
                            stage(dve.tensor_tensor(LG.rearrange("p (n t) g -> p n t g", n=HEADS), LG.rearrange("p (n t) g -> p n t g", n=HEADS),
                                                    GB[:, :, :].rearrange("p n (t g) -> p n t g", t=1).broadcast_to((P, HEADS, TILES, EXPERTS)),
                                                    ALU.add), "gate_biased")
                        if slot == DEN_AT + 4:
                            done(dve, "gate_biased", b + 1)
                            stage(dve.reduce_max(S1[:, 17, :], LG, AX.X), "gate_max")
                        if slot == DEN_AT + 4:
                            done(dve, "gate_max", b + 1)
                            stage(dve.tensor_tensor(LG, LG, bc4(17), ALU.subtract), "gate_sub")
                        if slot == DEN_AT + 6:
                            dve.wait_ge(S("gate_exp"), b + 1)
                            stage(dve.reduce_sum(S1[:, 18, :], EG, AX.X), "gate_sum")
                        if slot == DEN_AT + 6:
                            stage(dve.tensor_tensor(W4, EG, RD, ALU.mult), "gate_den")
                        if slot == DEN_AT + 7:
                            done(dve, "gate_sum", b + 1)
                            stage(dve.reciprocal(S1[:, 19, :], S1[:, 18, :]), "gate_rec")
                        if slot == DEN_AT + 8:
                            done(dve, "gate_rec", b + 1)
                            done(dve, "gate_den", b + 1)
                            stage(dve.tensor_tensor(W4, W4, bc4(19), ALU.mult), "mix_w")
                        if slot == MIX_AT:
                            dve.wait_ge(S("mixed"), HEADS * (b + 1))
                            stage(dve.reduce_sum(Y[:, :, :], MIXP[:, :, :, :].rearrange("p k e d -> p k d e"), AX.X), "mixture")
                        if slot == MIX_AT + 1:
                            done(dve, "mixture", b + 1)
                            dve.wait_ge(S("resid"), HEADS)
                            stage(dve.tensor_tensor(Y[:, :, :], Y[:, :, :], R[:, :, :, :].rearrange("p n t d -> p (n t) d"), ALU.add), "y_in")
                        inner_norm("y", b, slot, Y_AT, Y[:, :, :], 6, LNG, LNB, FX[:, :, :, :].rearrange("p t n d -> p n t d"))
                        if slot == Y_AT + NORM_LAG + 3:
                            done(dve, "y_out", b + 1)
                            stage(dve.tensor_scalar(FM[:, :, :, :], FX[:, :, :, :], 0.0, None, ALU.not_equal), "fx_mask")
                        for c, at in enumerate(FX_AT):
                            if slot == at + OUT_LAG:
                                lo, hi = halves(PADDED)[c]
                                dve.wait_ge(S("fxt"), 2 * b + c + 1)
                                stage(dve.tensor_scalar(FMT[:, lo:hi], FXT[0:E, lo:hi], 0.0, None, ALU.not_equal), "fxt_mask")
                        for c, at in enumerate(FC1_AT):
                            if slot == at + 1:
                                lo, hi = halves(PADDED)[c]
                                dve.wait_ge(S("fc1_psum"), 2 * b + c + 1)
                                dve.wait_ge(S("fxt_mask"), 2 * b + c + 1)
                                stage(dve.scalar_tensor_tensor(HXT[0:E, lo:hi], PS[0:E, MISC, 0:hi - lo], 0.0, FMT[:, lo:hi],
                                                               ALU.max, ALU.mult), "hxt")
                        if slot == FC2_AT + 1:
                            dve.wait_ge(S("fc2_psum"), b + 1)
                            done(dve, "fx_mask", b + 1)
                            flat = lambda x: x[:, :, :, :].rearrange("p t n d -> p (t n d)")
                            stage(dve.tensor_tensor(Y[:, :, :].rearrange("p k d -> p (k d)"), PS[:, MISC, 0:TILES * E], flat(FM), ALU.mult), "fc2")
                        if slot == FC2_AT + 2:
                            done(dve, "fc2", b + 1)
                            stage(dve.tensor_tensor(Y[:, :, :], Y[:, :, :], FX[:, :, :, :].rearrange("p t n d -> p (t n) d"), ALU.add), "z_in")
                        inner_norm("z", b, slot, Z_AT, Y[:, :, :], 12, FNG, FNB, FO[:, :, :, :].rearrange("p t n d -> p (t n) d"))
                        bf = lambda x: S1[:, x, 0:TILES].rearrange("p (t o) -> p t o", o=1).broadcast_to((P, TILES, HEADS))
                        if slot == FG_AT + 1:
                            dve.wait_ge(S("fg_psum"), b + 1)
                            stage(dve.tensor_copy(FL, PS[:, MISC, 0:TILES * HEADS].rearrange("p (t n) -> p t n", n=HEADS)), "fg_logits")
                        if slot == FG_AT + 1:
                            done(dve, "fg_logits", b + 1)
                            stage(dve.reduce_max(S1[:, 14, 0:TILES], FL, AX.X), "fg_max")
                        if slot == FG_AT + 1:
                            done(dve, "fg_max", b + 1)
                            stage(dve.tensor_tensor(FL, FL, bf(14), ALU.subtract), "fg_sub")
                        if slot == SLOTS - 1:
                            dve.wait_ge(S("fg_exp"), b + 1)
                            stage(dve.reduce_sum(S1[:, 14, 0:TILES], FE, AX.X), "fg_sum")
                        if slot == SLOTS - 1:
                            done(dve, "fg_sum", b + 1)
                            stage(dve.reciprocal(S1[:, 15, 0:TILES], S1[:, 14, 0:TILES]), "fg_rec")
                        if slot == SLOTS - 1:
                            done(dve, "fg_rec", b + 1)
                            stage(dve.tensor_tensor(FE, FE, bf(15), ALU.mult), "fgate")

            schedule(dve, iteration)

        @block.tensor
        def _(pe):
            pe.wait_ge(S("weights_in"), 16 * WEIGHT_DMAS)
            for k in range(KCHUNKS):
                pe.transpose(PS[:, 0, k * E:(k + 1) * E], TOKW[:, k * P:(k + 1) * P], IDENT[0:E, 0:E])
            turned = ((HL[:, :], 0), (WQN[:, :, :], 64), (WKN[:, :, :], 128), (WVN[:, :, :], 144), (GN[:, :, :], 160),
                      (F1N[:, :, :], 176), (F2N[:, :, :], 192), (FGN[:, :], 208), (WQKV[:, 2 * E:3 * E], 256))
            for w, at in turned:
                k = w.shape[0]
                m = int(np.prod(w.shape[1:]))
                last = pe.transpose(PS[0:m, 1, at:at + k], w, IDENT[0:k, 0:k])
            last.then_inc(S("w_turned"), 1)
            pe.wait_ge(S("w_forms"), 23)
            pe.matmul(PS[0:E + 1, 2, 0:256], HL[:, :], BQ[:, :, :], start=True, stop=True)
            pe.matmul(PS[0:E + 1, 2, 256:384], HL[:, :], BKV[:, :, :, :], start=True, stop=True)
            pe.matmul(PS[0:E + 1, 3, 0:E], WVT[:, :], WOUT[0:E, :], start=True, stop=True).then_inc(S("w_made"), 1)
            pe.wait_ge(S("w_ready"), 1)
            pe.wait_ge(S("ones_row"), 3)

            PATCH_UNITS = 4 * KCHUNKS

            def turn_patches(g, u):
                chunk, w4 = divmod(u, 4)
                c, half = divmod(chunk, 2)
                if w4 == 0:
                    pe.wait_ge(S("chunk"), g * KCHUNKS + chunk + 1)
                if u < 4 and g > 0 and u >= 2:
                    pe.wait_ge(S("img_in_h"), (g - 1) * 4 + 2 * (u - 1))
                if u >= 4:
                    pe.wait_ge(S("xt_sbuf_act" if u % 2 == 0 else "xt_sbuf_dve"), g * PATCH_UNITS // 2 + (u - 4) // 2 + 1)
                for j in range(4 if w4 < 3 else 2):
                    last = pe.transpose(PS[:, 4 + u % 4, j * ROWS:(j + 1) * ROWS],
                                        XR[:, chunk % 2, 4 * w4 + j, :], IDENT[0:ROWS, 0:ROWS])
                last.then_inc(S("xt_psum"), 1)

            AHEAD = 3
            EARLY = 2
            for g in range(BATCH // GROUP):
                for u in range(0 if g == 0 else EARLY, AHEAD):
                    turn_patches(g, u)
                for u in range(PATCH_UNITS):
                    if u + AHEAD < PATCH_UNITS:
                        turn_patches(g, u + AHEAD)
                    chunk, w4 = divmod(u, 4)
                    n = (4 if w4 < 3 else 2) * ROWS
                    pe.wait_ge(S("xt_sbuf_act" if u % 2 == 0 else "xt_sbuf_dve"), g * PATCH_UNITS // 2 + u // 2 + 1)
                    mm = pe.matmul(PS[0:E, w4, 0:n], WT[:, chunk, :], XT[:, u % 4, 0:n],
                                   start=(chunk == 0), stop=(chunk == KCHUNKS - 1))
                    mm.then_inc(S("xt_read"), 1)
                if g + 1 < BATCH // GROUP:
                    for u in range(EARLY):
                        turn_patches(g + 1, u)
                pe.wait_ge(S("ht"), 4 * (g + 1))
                for q in range(GROUP // QUAD):
                    for b in range(QUAD):
                        pe.transpose(PS[:, 6 + q, b * E:(b + 1) * E], HT[:, q * QUAD + b, 0:P], IDENT[0:E, 0:E])
                        mm = pe.transpose(PS[0:IMG_TAIL, 6 + q, (QUAD + b) * E:(QUAD + b + 1) * E], HT[:, q * QUAD + b, P:PATCHES],
                                          IDENT[0:E, 0:E])
                    mm.then_inc(S("img_tokens"), 1)

            def turn_tokens(n, b, q):
                if b == 0:
                    pe.wait_ge(S("xn"), n // PAIR + 1)
                    at_least(pe, "t2", n - PAIR - 1)
                at_least(pe, "xnt", n)
                for t in range(TILES):
                    mm = pe.transpose(PS[0:E, t // 4, (t % 4) * P:(t % 4 + 1) * P], XN[:, q, b * TILES + t, :], IDENT)
                mm.then_inc(S("xnt_psum"), 1)

            def project(n, b):
                pe.wait_ge(S("xnt"), n + 1)
                if n == 0:
                    pe.wait_ge(S("img_in_h"), 4 * (BATCH // GROUP))
                at_least(pe, "h_vo", n)
                for t in range(TILES):
                    mm = pe.matmul(PS[:, 4 + t // 2, (t % 2) * 4 * E:(t % 2 + 1) * 4 * E],
                                   XNT[:, b, t * P:(t + 1) * P], WKV[:, :], start=True, stop=True)
                mm.then_inc(S("kv_psum"), 1)

            def turn_q(n, b):
                pe.wait_ge(S("q_squared"), n + 1)
                at_least(pe, "q2t", n)
                for t in range(TILES):
                    mm = pe.transpose(PS[0:E, 2 + t // 4, (t % 4) * P:(t % 4 + 1) * P], QS[:, b * TILES + t, :], IDENT)
                mm.then_inc(S("q2t_psum"), 1)

            def attend(n, b, q):
                pe.wait_ge(S("q2t"), n + 1)
                if b == 0:
                    pe.wait_ge(S("xnt"), min(n + 2 + PAIR, BATCH))
                for t in range(TILES):
                    mm = pe.matmul(PS[:, T2_BANKS[b], t * E:(t + 1) * E], Q2T[:, q, b, t * P:(t + 1) * P], KVW[:, b, :],
                                   start=True, stop=True)
                mm.then_inc(S("t2_psum"), 1)

            for step in range(PAIRS + 1):
                mid, back = step, step - 1
                q = step % 2
                for b in range(PAIR):
                    if mid < PAIRS:
                        turn_tokens(mid * PAIR + b, b, q)
                    if 0 <= back:
                        if b == 0:
                            at_least(pe, "t2", PAIR * back)
                            pe.wait_ge(S("v"), PAIR * (back + 1))
                            pe.wait_ge(S("kn"), back + 1)
                        for t in range(TILES):
                            kv = KV[0:rows(t), 1 - q, b * TILES + t, :]
                            mm = pe.matmul(PS[:, 7, b * E:(b + 1) * E], kv, kv[:, 0:E], start=(t == 0), stop=(t == TILES - 1))
                        if b == 1:
                            mm.then_inc(S("kvt_psum"), 1)
                    if mid < PAIRS:
                        project(mid * PAIR + b, b)
                if 0 <= back:
                    pe.wait_ge(S("kvt"), back + 1)
                    pe.wait_ge(S("kk"), back + 1)
                    for b in range(PAIR):
                        mm = pe.matmul(PS[0:E, 7, 256 + b * E:256 + (b + 1) * E], KVT[E:2 * E, b, :], WOUT[E:2 * E, :],
                                       start=True, stop=True)
                    mm.then_inc(S("kvw_psum"), 1)
                if mid < PAIRS:
                    turn_q(mid * PAIR, 0)
                if 0 <= back:
                    pe.wait_ge(S("kvw"), back + 1)
                    attend(back * PAIR, 0, 1 - q)
                if mid < PAIRS:
                    turn_q(mid * PAIR + 1, 1)
                if 0 <= back:
                    attend(back * PAIR + 1, 1, 1 - q)

            pe.wait_ge(S("h2_done"), PAIRS)

            def iteration(it, p, C, M, A, D1, prev_a, first):
                last_taken = ["raw", HEADS * (it - 1) + HEADS - 1]

                def side_bank(name, count):
                    at_least(pe, last_taken[0], last_taken[1])
                    last_taken[:] = [name, count]

                def side(width):
                    return PS[:, MISC, 0:width]

                def scores(slot):
                    n, u = divmod(slot, UNITS)
                    j, lo, w, e0, ne = UNITS_S[u]
                    r = rows(j)
                    if slot % (SLOTS // 2) == 0:
                        pe.wait_ge(S(f"max_in{n // 2}"), 16 * (it + 1))
                    at_least(pe, "exped", bank_left(S_BANKS, it, p, slot))
                    h0 = n * EXPERTS + e0
                    pe.matmul(PS[0:r, ring_bank(S_BANKS, p, slot), 0:ne * w], KA[p][:, n, j * P:j * P + r],
                              QA[p][:, h0:h0 + ne, lo:lo + w], start=True, stop=True).then_inc(S("scores"), 1)

                def max_scores(b, q, slot):
                    n, u = divmod(slot, UNITS)
                    i, lo, w, e0, ne = UNITS_M[u]
                    s0, r = query_tile(i)
                    if slot % (SLOTS // 2) == 0:
                        pe.wait_ge(S(f"q_in{n // 2}"), 16 * PARTS * (b + 1))
                        pe.wait_ge(S(f"k_in{n // 2}"), 16 * PARTS * (b + 1))
                    at_least(pe, "maxed", bank_left(M_BANKS, b, q, slot))
                    diagonal = lo + w == TAIL + i * P
                    bank = PS[0:r, ring_bank(M_BANKS, q, slot), 0:ne * w]
                    for e in range(ne):
                        mm = pe.matmul(bank[:, e * w:(e + 1) * w], QA[q][0:P - MROWS, n * EXPERTS + e0 + e, s0:s0 + r],
                                       KA[q][0:P - MROWS, n, lo:lo + w], start=(e == 0), stop=(not diagonal and e == ne - 1))
                    if diagonal:
                        mm = pe.matmul(bank.rearrange("p (e w) -> p e w", e=ne)[:, :, w - r:w], IDB[:, 0:r],
                                       MASKB[:, 0:r].rearrange("p (e w) -> p e w", e=1).broadcast_to((P, ne, r)),
                                       start=False, stop=True)
                    mm.then_inc(S("max_scores"), 1)

                def weighted_sums(b, n, q, piece):
                    _, j, lo, hi = PIECES[piece]
                    r = rows(j)
                    first_of_tile = piece == 0 or PIECES[piece - 1][1] != j
                    last_of_tile = piece == len(PIECES) - 1 or PIECES[piece + 1][1] != j
                    if first_of_tile:
                        pe.wait_ge(S("masked"), (b * HEADS + n) * TILES + j + 1)
                    if piece == 0:
                        at_least(pe, "ot", b * HEADS + n)
                        if n == 0:
                            pe.wait_ge(S("va"), 2 * b + 2)
                    bank, at = divmod(lo, BANK)
                    of_bank = [x for x, (_, _, lo_x, _) in enumerate(PIECES) if lo_x // BANK == bank]
                    for e in range(EXPERTS):
                        mm = pe.matmul(PS[32 * e:32 * e + 32, PV_BANK + bank, at:at + hi - lo], VA[q][0:r, j, n, :],
                                       PT[j][0:r, e, lo - j * P:hi - j * P], start=(piece == of_bank[0]),
                                       stop=(piece == of_bank[-1]))
                    if last_of_tile:
                        mm.then_inc(S("summed"), 1)

                def to_tokens(b, n, part):
                    if part == 0:
                        side_bank("raw", b * HEADS + n + 1)
                        pe.wait_ge(S("ot"), b * HEADS + n + 1)
                    for t in range(part * TILES // 2, (part + 1) * TILES // 2):
                        mm = pe.matmul(side(TILES * SELC)[:, t * SELC:(t + 1) * SELC], OT[:, t * P:(t + 1) * P], SEL[:, n, :],
                                       start=True, stop=True)
                    if part == 1:
                        mm.then_inc(S("raw_psum"), 1)

                def turn_maxima(b, half):
                    side_bank("max_sbuf", 2 * b + half + 1)
                    done(pe, "max3", 2 * b + half + 1)
                    bank = PS[0:24, MISC, 0:SEQ // 2].bitcast(BF16)
                    apart(pe)
                    for i in range(TILES):
                        s0, r = query_tile(i)
                        mm = pe.transpose(bank[:, s0:s0 + r], NB[0:r, half, i, :, :], IDB[0:r, 0:r])
                    mm.then_inc(S("max_psum"), 1)

                def turn(src, t0, t1):
                    for t in range(t0, t1):
                        mm = pe.transpose(side(BANK)[0:E, (t - t0) * P:(t - t0 + 1) * P], src(t), IDENT)
                    return mm

                for slot in range(SLOTS):
                    if C:
                        if slot == 0:
                            pe.wait_ge(S("cleared"), CLEARS)
                        scores(slot)
                    if M:
                        if slot == 0:
                            pe.wait_ge(S("wide_cleared"), WIDE_CLEARS)
                        max_scores(it + 1, 1 - p, slot)
                    for n in range(-1, HEADS):
                        for piece, (at, *_) in enumerate(PIECES):
                            if slot == n * UNITS + at:
                                if n >= 0 and C:
                                    weighted_sums(it, n, p, piece)
                                if n < 0 and D1:
                                    weighted_sums(it - 1, HEADS - 1, 1 - p, piece)
                    if C and slot == MAX1_AT:
                        turn_maxima(it, 1)
                    if M and slot == MAX0_AT:
                        turn_maxima(it + 1, 0)
                    for part in range(2):
                        if D1 and slot == SEL_AT + part + 3 * UNITS - SLOTS:
                            to_tokens(it - 1, HEADS - 1, part)
                        for n in range(HEADS - 1):
                            if C and slot == SEL_AT + part + n * UNITS:
                                to_tokens(it, n, part)
                    if A:
                        b = it + 2
                        for c, at in enumerate(TURN_AT):
                            if slot == at:
                                side_bank("xft", 2 * b + c + 1)
                                done(pe, "a_norm", b + 1)
                                apart(pe)
                                turn(lambda t: AN[:, t, :], *((0, TILES // 2), (TILES // 2, TILES))[c]).then_inc(S("xft_psum"), 1)
                        if slot == RESID_AT and known_first_heads(b):
                            side_bank("resid", b + 1)
                            pe.wait_ge(S("xft"), 2 * b + 2)
                            for t in range(TILES):
                                mm = pe.matmul(side(TILES * D)[:, t * D:(t + 1) * D], XFT[p][0:E + 1, t * P:(t + 1) * P],
                                               HLT[:, b * D:(b + 1) * D], start=True, stop=True)
                            mm.then_inc(S("resid_psum"), 1)
                        for idx, at in enumerate(PROJ_AT):
                            if slot == at:
                                half, c = PROJ_HALF[idx // 2], idx % 2
                                lo, hi = halves(SEQ)[c]
                                side_bank("q_out", 6 * b + idx + 1)
                                if idx == 0:
                                    pe.wait_ge(S("xft"), 2 * b + 2)
                                    pe.wait_ge(S("cleared"), 4)
                                w = WQ[:, half, :] if half < 2 else WK[:, :]
                                pe.matmul(side(hi - lo), w, XFT[p][:, lo:hi], start=True, stop=True).then_inc(S("proj"), 1)
                    if M:
                        for c, at in enumerate(V_AT):
                            if slot == at:
                                b = it + 1
                                t0, t1 = ((0, TILES // 2), (TILES // 2, TILES))[c]
                                side_bank("va", 2 * b + c + 1)
                                for t in range(t0, t1):
                                    mm = pe.matmul(side(BANK)[:, (t - t0) * P:(t - t0 + 1) * P], XFT[1 - p][:, t * P:(t + 1) * P],
                                                   WV[:, :, :], start=True, stop=True)
                                mm.then_inc(S("v_psum"), 1)
                    if D1:
                        b = it - 1
                        for c, at in enumerate(FX_AT):
                            if slot == at:
                                side_bank("fxt", 2 * b + c + 1)
                                done(pe, "y_out", b + 1)
                                apart(pe)
                                turn(lambda t: FX[:, t, :, :], *((0, TILES // 2), (TILES // 2, TILES))[c]).then_inc(S("fxt_psum"), 1)
                        for c, at in enumerate(FC1_AT):
                            if slot == at:
                                lo, hi = halves(PADDED)[c]
                                side_bank("hxt", 2 * b + c + 1)
                                pe.wait_ge(S("fxt"), 2 * b + c + 1)
                                pe.matmul(side(hi - lo)[0:E], F1[:, :, :], FXT[:, lo:hi], start=True, stop=True).then_inc(S("fc1_psum"), 1)
                        if slot == FC2_AT:
                            side_bank("fc2", b + 1)
                            pe.wait_ge(S("hxt"), 2 * b + 2)
                            for t in range(TILES):
                                mm = pe.matmul(side(TILES * E)[:, t * E:(t + 1) * E], HXT[:, t * P:(t + 1) * P], F2[:, :, :],
                                               start=True, stop=True)
                            mm.then_inc(S("fc2_psum"), 1)
                        for c, at in enumerate(FO_AT):
                            if slot == at:
                                side_bank("fot", 2 * b + c + 1)
                                done(pe, "z_out", b + 1)
                                apart(pe)
                                turn(lambda t: FO[:, t, :, :], *((0, TILES // 2), (TILES // 2, TILES))[c]).then_inc(S("fot_psum"), 1)
                        if slot == FG_AT:
                            side_bank("fg_logits", b + 1)
                            pe.wait_ge(S("fot"), 2 * b + 2)
                            for t in range(TILES):
                                mm = pe.matmul(side(TILES * HEADS)[:, t * HEADS:(t + 1) * HEADS], FOT[:, t * P:(t + 1) * P], FGW[:, :],
                                               start=True, stop=True)
                            mm.then_inc(S("fg_psum"), 1)

            schedule(pe, iteration)



def kernel(**inputs):
    import concourse.bacc as _bacc
    from concourse import mybir as _mybir
    from concourse.bass_utils import run_bass_kernel_spmd as _run

    nc = _bacc.Bacc("TRN2", target_bir_lowering=False, num_devices=1)
    nc.disable_value_cache = True
    arrays, aps = {}, {}
    for name, v in list(inputs.items()) + [("const", shape_constants())]:
        v = np.ascontiguousarray(v)
        arrays["in_" + name] = v
        aps[name] = nc.dram_tensor("in_" + name, v.shape, _mybir.dt.from_np(v.dtype), kind="ExternalInput").ap()
    out = nc.dram_tensor("out_0", (BATCH, SEQ, E), _mybir.dt.float32, kind="ExternalOutput").ap()
    build(nc, aps, out)
    result = _run(nc, [arrays], core_ids=[0])
    return result.results[0]["out_0"]
```
